# Optimizing a Trainium2 kernel written in Bass

```python
import numpy as np
import jax
import jax.numpy as jnp

def _softmax(x, axis=-1):
    return jax.nn.softmax(x, axis=axis)

def _gelu(x):
    return jax.nn.gelu(x, approximate=True)

def _silu(x):
    return jax.nn.silu(x)

def _sigmoid(x):
    return jax.nn.sigmoid(x)

def _layernorm(x, axis=-1, eps=1e-05):
    m = jnp.mean(x, axis=axis, keepdims=True)
    v = jnp.var(x, axis=axis, keepdims=True)
    return (x - m) / jnp.sqrt(v + eps)

def _scatter_add(tgt, idx, src, axis=0):
    return tgt.at[idx].add(src)

def _segment_sum(src, seg, n):
    return jax.ops.segment_sum(src, seg, n)
kernel_name = 'mk_adaln_d1_jaxref_r8_393ffe'

def setup_inputs(seed: int=0):
    np.random.seed(seed)
    _w = jnp.asarray

    def _L0_attn_setup():
        import jax, jax.numpy as jnp
        import numpy as np
        L, H, D_MODEL, D_FF = (4, 16, 128, 512)
        HD = D_MODEL // H
        LN_EPS = 1e-05
        ATT_EPS = 1e-06
        CHUNK = 128

        def _ln(x, g, b):
            m = jnp.mean(x, axis=-1, keepdims=True)
            v = jnp.var(x, axis=-1, keepdims=True)
            return (x - m) * jax.lax.rsqrt(v + LN_EPS) * g + b

        def _feature_map(x):
            return jax.nn.elu(x) + 1.0

        def _causal_linear_attention(q, k, v):
            B, S, Hn, D = q.shape
            nC = S // CHUNK
            q = q.reshape(B, nC, CHUNK, Hn, D)
            k = k.reshape(B, nC, CHUNK, Hn, D)
            v = v.reshape(B, nC, CHUNK, Hn, D)
            KV = jnp.einsum('bnchd,bnche->bnhde', k, v)
            Ks = jnp.sum(k, axis=2)
            KVcum = jnp.cumsum(KV, axis=1) - KV
            Kcum = jnp.cumsum(Ks, axis=1) - Ks
            inter = jnp.einsum('bnchd,bnhde->bnche', q, KVcum)
            den_inter = jnp.einsum('bnchd,bnhd->bnch', q, Kcum)
            scores = jnp.einsum('bnchd,bnkhd->bnhck', q, k)
            mask = jnp.tril(jnp.ones((CHUNK, CHUNK), dtype=bool))
            scores = jnp.where(mask, scores, 0.0)
            intra = jnp.einsum('bnhck,bnkhe->bnche', scores, v)
            den_intra = jnp.transpose(jnp.sum(scores, axis=-1), (0, 1, 3, 2))
            out = (inter + intra) / (den_inter + den_intra + ATT_EPS)[..., None]
            return out.reshape(B, S, Hn, D)

        def _forward(x, Wq, bq, Wk, bk, Wv, bv, Wo, bo, W1, b1, W2, b2, g1, be1, g2, be2, gf, bef):
            B, S, Dm = x.shape
            for l in range(L):
                q = (x @ Wq[l] + bq[l]).reshape(B, S, H, HD)
                k = (x @ Wk[l] + bk[l]).reshape(B, S, H, HD)
                v = (x @ Wv[l] + bv[l]).reshape(B, S, H, HD)
                att = _causal_linear_attention(_feature_map(q), _feature_map(k), v)
                x = x + att.reshape(B, S, Dm) @ Wo[l] + bo[l]
                y = x = _ln(x, g1[l], be1[l])
                y = jax.nn.gelu(y @ W1[l] + b1[l], approximate=False)
                y = y @ W2[l] + b2[l]
                x = _ln(x + y, g2[l], be2[l])
            return _ln(x, gf, bef)
        key = jax.random.key(seed)
        ks = jax.random.split(key, 8)
        B, S = (2, 512)
        sc = 0.02

        def w(k, shape):
            return jax.random.normal(k, shape, jnp.float32) * sc
        return {'x': jax.random.normal(ks[0], (B, S, D_MODEL), jnp.float32), 'Wq': w(ks[1], (L, D_MODEL, D_MODEL)), 'bq': jnp.zeros((L, D_MODEL), jnp.float32), 'Wk': w(ks[2], (L, D_MODEL, D_MODEL)), 'bk': jnp.zeros((L, D_MODEL), jnp.float32), 'Wv': w(ks[3], (L, D_MODEL, D_MODEL)), 'bv': jnp.zeros((L, D_MODEL), jnp.float32), 'Wo': w(ks[4], (L, D_MODEL, D_MODEL)), 'bo': jnp.zeros((L, D_MODEL), jnp.float32), 'W1': w(ks[5], (L, D_MODEL, D_FF)), 'b1': jnp.zeros((L, D_FF), jnp.float32), 'W2': w(ks[6], (L, D_FF, D_MODEL)), 'b2': jnp.zeros((L, D_MODEL), jnp.float32), 'g1': jnp.ones((L, D_MODEL), jnp.float32), 'be1': jnp.zeros((L, D_MODEL), jnp.float32), 'g2': jnp.ones((L, D_MODEL), jnp.float32), 'be2': jnp.zeros((L, D_MODEL), jnp.float32), 'gf': jnp.ones((D_MODEL,), jnp.float32), 'bef': jnp.zeros((D_MODEL,), jnp.float32)}
    _L0_attn_in = _L0_attn_setup()

    def _L0_ffn_setup():
        import jax, jax.numpy as jnp
        import numpy as np
        B, S, D = (1, 256, 128)
        F = 176
        E = 16
        K = 2
        CAP_FACTOR = 1.25

        def _mlp(h, wg, wu, wd):
            return jax.nn.silu(h @ wg) * (h @ wu) @ wd
        key = jax.random.key(seed)
        ks = jax.random.split(key, 10)
        sd = 0.02
        return {'x': jax.random.normal(ks[0], (B, S, D), jnp.float32), 'router_w': jax.random.normal(ks[1], (D, E), jnp.float32) * sd, 'router_b': jnp.zeros((E,), jnp.float32), 'w_gate': jax.random.normal(ks[2], (E, D, F), jnp.float32) * sd, 'w_up': jax.random.normal(ks[3], (E, D, F), jnp.float32) * sd, 'w_down': jax.random.normal(ks[4], (E, F, D), jnp.float32) * sd, 'sw_gate': jax.random.normal(ks[5], (D, F), jnp.float32) * sd, 'sw_up': jax.random.normal(ks[6], (D, F), jnp.float32) * sd, 'sw_down': jax.random.normal(ks[7], (F, D), jnp.float32) * sd}
    _L0_ffn_in = _L0_ffn_setup()
    _L0_c = _w((lambda *s: np.random.randn(*s).astype(np.float32) * 0.05)(8, 128))
    _L0_wmod = _w((lambda *s: np.random.randn(*s).astype(np.float32) * 0.05)(128, 6 * 128) * 128 ** (-0.5))
    _d = {'L0_attn_x': _L0_attn_in['x'], 'L0_attn_Wq': _L0_attn_in['Wq'], 'L0_attn_bq': _L0_attn_in['bq'], 'L0_attn_Wk': _L0_attn_in['Wk'], 'L0_attn_bk': _L0_attn_in['bk'], 'L0_attn_Wv': _L0_attn_in['Wv'], 'L0_attn_bv': _L0_attn_in['bv'], 'L0_attn_Wo': _L0_attn_in['Wo'], 'L0_attn_bo': _L0_attn_in['bo'], 'L0_attn_W1': _L0_attn_in['W1'], 'L0_attn_b1': _L0_attn_in['b1'], 'L0_attn_W2': _L0_attn_in['W2'], 'L0_attn_b2': _L0_attn_in['b2'], 'L0_attn_g1': _L0_attn_in['g1'], 'L0_attn_be1': _L0_attn_in['be1'], 'L0_attn_g2': _L0_attn_in['g2'], 'L0_attn_be2': _L0_attn_in['be2'], 'L0_attn_gf': _L0_attn_in['gf'], 'L0_attn_bef': _L0_attn_in['bef'], 'L0_ffn_router_w': _L0_ffn_in['router_w'], 'L0_ffn_router_b': _L0_ffn_in['router_b'], 'L0_ffn_w_gate': _L0_ffn_in['w_gate'], 'L0_ffn_w_up': _L0_ffn_in['w_up'], 'L0_ffn_w_down': _L0_ffn_in['w_down'], 'L0_ffn_sw_gate': _L0_ffn_in['sw_gate'], 'L0_ffn_sw_up': _L0_ffn_in['sw_up'], 'L0_ffn_sw_down': _L0_ffn_in['sw_down'], 'L0_c': _L0_c, 'L0_wmod': _L0_wmod}
    _x0 = _d['L0_attn_x']
    _d['L0_attn_x'] = jax.random.normal(jax.random.fold_in(jax.random.key(seed), 1), (8, 512, 128), dtype=_x0.dtype)
    del _x0
    return _d

def reference(L0_attn_x, L0_attn_Wq, L0_attn_bq, L0_attn_Wk, L0_attn_bk, L0_attn_Wv, L0_attn_bv, L0_attn_Wo, L0_attn_bo, L0_attn_W1, L0_attn_b1, L0_attn_W2, L0_attn_b2, L0_attn_g1, L0_attn_be1, L0_attn_g2, L0_attn_be2, L0_attn_gf, L0_attn_bef, L0_ffn_router_w, L0_ffn_router_b, L0_ffn_w_gate, L0_ffn_w_up, L0_ffn_w_down, L0_ffn_sw_gate, L0_ffn_sw_up, L0_ffn_sw_down, L0_c, L0_wmod):

    def _L0_attn_ref(x, Wq, bq, Wk, bk, Wv, bv, Wo, bo, W1, b1, W2, b2, g1, be1, g2, be2, gf, bef):
        import jax, jax.numpy as jnp
        import numpy as np
        L, H, D_MODEL, D_FF = (4, 16, 128, 512)
        HD = D_MODEL // H
        LN_EPS = 1e-05
        ATT_EPS = 1e-06
        CHUNK = 128

        def _ln(x, g, b):
            m = jnp.mean(x, axis=-1, keepdims=True)
            v = jnp.var(x, axis=-1, keepdims=True)
            return (x - m) * jax.lax.rsqrt(v + LN_EPS) * g + b

        def _feature_map(x):
            return jax.nn.elu(x) + 1.0

        def _causal_linear_attention(q, k, v):
            B, S, Hn, D = q.shape
            nC = S // CHUNK
            q = q.reshape(B, nC, CHUNK, Hn, D)
            k = k.reshape(B, nC, CHUNK, Hn, D)
            v = v.reshape(B, nC, CHUNK, Hn, D)
            KV = jnp.einsum('bnchd,bnche->bnhde', k, v)
            Ks = jnp.sum(k, axis=2)
            KVcum = jnp.cumsum(KV, axis=1) - KV
            Kcum = jnp.cumsum(Ks, axis=1) - Ks
            inter = jnp.einsum('bnchd,bnhde->bnche', q, KVcum)
            den_inter = jnp.einsum('bnchd,bnhd->bnch', q, Kcum)
            scores = jnp.einsum('bnchd,bnkhd->bnhck', q, k)
            mask = jnp.tril(jnp.ones((CHUNK, CHUNK), dtype=bool))
            scores = jnp.where(mask, scores, 0.0)
            intra = jnp.einsum('bnhck,bnkhe->bnche', scores, v)
            den_intra = jnp.transpose(jnp.sum(scores, axis=-1), (0, 1, 3, 2))
            out = (inter + intra) / (den_inter + den_intra + ATT_EPS)[..., None]
            return out.reshape(B, S, Hn, D)

        def _forward(x, Wq, bq, Wk, bk, Wv, bv, Wo, bo, W1, b1, W2, b2, g1, be1, g2, be2, gf, bef):
            B, S, Dm = x.shape
            for l in range(L):
                q = (x @ Wq[l] + bq[l]).reshape(B, S, H, HD)
                k = (x @ Wk[l] + bk[l]).reshape(B, S, H, HD)
                v = (x @ Wv[l] + bv[l]).reshape(B, S, H, HD)
                att = _causal_linear_attention(_feature_map(q), _feature_map(k), v)
                x = x + att.reshape(B, S, Dm) @ Wo[l] + bo[l]
                y = x = _ln(x, g1[l], be1[l])
                y = jax.nn.gelu(y @ W1[l] + b1[l], approximate=False)
                y = y @ W2[l] + b2[l]
                x = _ln(x + y, g2[l], be2[l])
            return _ln(x, gf, bef)
        return _forward(x, Wq, bq, Wk, bk, Wv, bv, Wo, bo, W1, b1, W2, b2, g1, be1, g2, be2, gf, bef)

    def _L0_ffn_ref(x, router_w, router_b, w_gate, w_up, w_down, sw_gate, sw_up, sw_down):
        import jax, jax.numpy as jnp
        import numpy as np
        B, S, D = (1, 256, 128)
        F = 176
        E = 16
        K = 2
        CAP_FACTOR = 1.25

        def _mlp(h, wg, wu, wd):
            return jax.nn.silu(h @ wg) * (h @ wu) @ wd
        b, s, d = x.shape
        N = b * s
        NK = N * K
        C = int(np.ceil(CAP_FACTOR * NK / E))
        x_tokens = x.reshape(N, d)
        logits = x_tokens @ router_w + router_b
        probs = jax.nn.softmax(logits, axis=-1)
        vals, idx = jax.lax.top_k(probs, K)
        vals = vals / (jnp.sum(vals, axis=-1, keepdims=True) + 1e-09)
        idx_flat = idx.reshape(NK)
        vals_flat = vals.reshape(NK)
        oh_e = jax.nn.one_hot(idx_flat, E, dtype=x.dtype)
        pos = (jnp.cumsum(oh_e, axis=0) * oh_e).sum(axis=1) - 1
        within = (pos < C).astype(x.dtype)
        pos_c = jnp.clip(pos, 0, C - 1).astype(jnp.int32)
        token_ids = jnp.arange(NK) // K
        x_pair = x_tokens[token_ids] * within[:, None]
        expert_inputs = jnp.zeros((E, C, d), x.dtype).at[idx_flat, pos_c].add(x_pair)
        expert_outputs = jax.vmap(_mlp)(expert_inputs, w_gate, w_up, w_down)
        gathered = expert_outputs[idx_flat, pos_c] * (vals_flat * within)[:, None]
        output_tokens = gathered.reshape(N, K, d).sum(axis=1)
        return x + _mlp(x, sw_gate, sw_up, sw_down) + output_tokens.reshape(b, s, d)
    x = L0_attn_x
    mod = (_silu(L0_c) @ L0_wmod).reshape(L0_c.shape[0], 6, 1, -1)
    sa, ca, ga, sb, cb, gb = (mod[:, 0], mod[:, 1], mod[:, 2], mod[:, 3], mod[:, 4], mod[:, 5])
    ga = (2 * (ga >= 0) - 1) * jnp.maximum(jnp.abs(ga), 0.25)
    gb = (2 * (gb >= 0) - 1) * jnp.maximum(jnp.abs(gb), 0.25)
    h = _layernorm(x, axis=-1) * (1 + ca) + sa
    x = x + ga * _L0_attn_ref(h, L0_attn_Wq, L0_attn_bq, L0_attn_Wk, L0_attn_bk, L0_attn_Wv, L0_attn_bv, L0_attn_Wo, L0_attn_bo, L0_attn_W1, L0_attn_b1, L0_attn_W2, L0_attn_b2, L0_attn_g1, L0_attn_be1, L0_attn_g2, L0_attn_be2, L0_attn_gf, L0_attn_bef)
    h = _layernorm(x, axis=-1) * (1 + cb) + sb
    x = x + gb * _L0_ffn_ref(h, L0_ffn_router_w, L0_ffn_router_b, L0_ffn_w_gate, L0_ffn_w_up, L0_ffn_w_down, L0_ffn_sw_gate, L0_ffn_sw_up, L0_ffn_sw_down)
    return x

_drawn_inputs = setup_inputs


def setup_inputs(seed=0):
    import zlib

    import numpy as np

    out = dict(_drawn_inputs(seed))
    spreads = {'L0_attn_bq': (0.0, 0.8),
     'L0_attn_bk': (0.0, 0.8),
     'L0_attn_bv': (0.0, 0.745),
     'L0_attn_bo': (0.0, 0.1),
     'L0_attn_b1': (0.0, 0.661),
     'L0_attn_b2': (0.0, 0.1),
     'L0_attn_g1': (1.0, 0.2),
     'L0_attn_be1': (0.0, 0.1),
     'L0_attn_g2': (1.0, 0.2),
     'L0_attn_be2': (0.0, 0.1),
     'L0_attn_gf': (1.0, 0.2),
     'L0_attn_bef': (0.0, 0.349),
     'L0_ffn_router_b': (0.0, 0.8)}
    factors = {'L0_attn_Wq': 8.0,
     'L0_attn_Wk': 8.0,
     'L0_attn_Wv': 8.0,
     'L0_attn_Wo': 5.439,
     'L0_ffn_router_w': 8.0,
     'L0_ffn_w_gate': 8.0,
     'L0_ffn_w_up': 8.0,
     'L0_ffn_w_down': 8.0,
     'L0_ffn_sw_gate': 8.0,
     'L0_ffn_sw_up': 8.0,
     'L0_ffn_sw_down': 8.0}
    for name, (base, spread) in spreads.items():
        noise = np.random.default_rng([zlib.crc32(name.encode()), seed]).standard_normal(out[name].shape)
        drawn = base * np.exp(spread * noise) if base else spread * noise
        out[name] = jnp.asarray(drawn.astype(out[name].dtype))
    for name, factor in factors.items():
        out[name] = (out[name] * factor).astype(out[name].dtype)
    return out
```

```python
import concourse.bass as bass
from concourse import mybir
from contextlib import ExitStack

F32 = mybir.dt.float32
BF16 = mybir.dt.bfloat16
U32 = mybir.dt.uint32
ALU = mybir.AluOpType
ACT = mybir.ActivationFunctionType
AXX = mybir.AxisListType.X
ds = bass.ds

P = 128
B, S, D = 8, 512, 128
L, H, HD, FF = 4, 16, 8, 512
NT = S // P
TILES = B * NT
EV = HD + 1
CW = EV * D
CB = CW // 3
SW = EV * H
FC = FF // P
STEPS = L * B
LN_EPS, ATT_EPS = 1e-5, 1e-6
NB = 3 * D
BIAS = NB + 2 * D


def wait(engine, sem, value):
    if isinstance(value, int) and value <= 0:
        return
    engine.wait_ge(sem, value)


def wait_apart(engine, sem, value, ready, *more):
    waits = ((sem, value),) + more
    for _, value in waits:
        if not isinstance(value, int):
            engine.compute_val(value)
    engine.wait_ge(ready, 1)
    for sem, value in waits:
        wait(engine, sem, value)


def adaln_block_kernel(nc, x, Wq, bq, Wk, bk, Wv, bv, Wo, bo, W1, b1, W2, b2, g1, be1, g2, be2, gf, bef,
                       router_w, router_b, w_gate, w_up, w_down, sw_gate, sw_up, sw_down, c, wmod, out):
    E = router_w.shape[1]
    F = w_gate.shape[2]
    FA, FB = P, F - P
    TOK = B * S
    CAP = -(-5 * 2 * TOK // (4 * E))
    CT = CAP // P
    HC = CAP // 2
    assert CAP % (2 * P) in (0, P) and HC <= 512 and CAP % P == 0
    ROWS = E * CAP
    MODS = 6 * D

    x_v = x.rearrange("b (n p) d -> b p n d", p=P)
    out_v = out.rearrange("b (n p) d -> b p n d", p=P)
    mod_dram = nc.dram_tensor("mod_scratch", [B, MODS], F32, kind="Internal").ap()
    xe_dram = nc.dram_tensor("expert_in_scratch", [ROWS + 2 * TOK, D], F32, kind="Internal").ap()
    ye_dram = nc.dram_tensor("expert_out_scratch", [ROWS, D], F32, kind="Internal").ap()
    xe_tiles = xe_dram[0:ROWS, :].rearrange("(e p j) d -> e p (j d)", e=E, p=P)
    ye_tiles = ye_dram.rearrange("(e p j) d -> e p (j d)", e=E, p=P)

    with ExitStack() as ctx:
        def sb(name, shape, dt=F32):
            return ctx.enter_context(nc.sbuf_tensor(name, shape, dt))

        def sem(name):
            return ctx.enter_context(nc.semaphore(name))

        ident = sb("ident", [P, P])
        tri = sb("tri", [P, P])
        tri_before = sb("tri_before", [P, P], BF16)
        ones_bf = sb("ones_bf", [P, P], BF16)
        ones3 = sb("ones3", [3, P], BF16)
        headmask = sb("headmask", [P, EV, H])
        halfneg = sb("halfneg", [P, 4 * B])
        rank16 = sb("rank16", [P, E])
        expert_base = sb("expert_base", [P, E])
        trash = sb("trash", [P, TILES])
        iota_i = sb("iota_i", [P, 64], mybir.dt.int32)
        wqkv = sb("wqkv", [P, L, NB])
        wo = sb("wo", [P, L, D])
        w1 = sb("w1", [P, L, FF])
        w2 = sb("w2", [P, L, FC, D])
        b1c = sb("b1c", [P, L, FC])
        gains = sb("gains", [P, 4, L, D])
        gfb = sb("gfb", [P, 2, D])
        bias3 = sb("bias3", [3, L * BIAS + E + SW], BF16)
        bias3_l = bias3[:, 0:L * BIAS].rearrange("r (l c) -> r l c", l=L)
        rb3 = bias3[:, L * BIAS:L * BIAS + E]
        eps3 = bias3[:, L * BIAS + E:]
        cT = sb("cT", [P, B])
        csT = sb("csT", [P, B])
        wmod_s = sb("wmod_s", [P, MODS])
        mod8 = sb("mod8", [B, MODS])
        gsign = sb("gsign", [B, 2, D])
        mod = sb("mod", [P, B, 6, D])
        x0 = sb("x0", [P, TILES, D])
        X = sb("X", [P, TILES, D])
        stats = sb("stats", [P, TILES, 6])
        mv = sb("mv", [P, TILES, 2])
        var = sb("var", [P, TILES])
        rstd = sb("rstd", [P, TILES])
        xs = sb("xs", [P, NT, D])
        x1s = sb("x1s", [P, NT, D])
        w1s = sb("w1s", [P, FF])
        xT = sb("xT", [P, NT, P])
        x1T = sb("x1T", [P, S])
        ex = sb("ex", [P, 2, 2 * D])
        rl = sb("rl", [P, 2, 2 * D])
        qk = sb("qk", [P, NT, 2, D])
        v1 = sb("v1", [P, NT, EV, H])
        kv = sb("kv", [P, NT, CW])
        qT = sb("qT", [P, P])
        kvm = sb("kvm", [P, SW])
        kvt = sb("kvt", [P, SW])
        BR = L * BIAS + E + SW
        brow = kv[:, :, :].rearrange("p n c -> p (n c)")[0:3, 0:BR]
        brow_r = X[:, :, :].rearrange("p t d -> p (t d)")[0:3, 0:BR]
        brow_all = sb("brow_all", [P, BR])
        brow_s = brow_all[0:3, :]
        bpart = sb("bpart", [3, BR], BF16)
        prod = sb("prod", [P, CW])
        red = sb("red", [P, SW])
        tot = sb("tot", [P, EV, H])
        rden = sb("rden", [P, H])
        att = sb("att", [P, D])
        attT = sb("attT", [P, P])
        y1 = sb("y1", [P, 2, D])
        st1 = sb("st1", [P, 2, 6])
        mv1 = sb("mv1", [P, 2, 2])
        var1 = sb("var1", [P, 2])
        rstd1 = sb("rstd1", [P, 2])
        xn1 = sb("xn1", [P, 2, D])
        xg1 = sb("xg1", [P, D])
        hT = sb("hT", [P, FC, S])
        y2 = sb("y2", [P, NT, D])
        st2 = sb("st2", [P, NT, 6])
        mv2 = sb("mv2", [P, NT, 2])
        var2 = sb("var2", [P, NT])
        rstd2 = sb("rstd2", [P, NT])
        xn2 = sb("xn2", [P, NT, D])
        xg2 = sb("xg2", [P, NT, D])

        ps = ctx.enter_context(nc.psum_tensor("ps", [P, 8, 512], F32))
        ps_cum = ps[:, 0:3, 0:CB]
        ps_qkv = ps[:, 3, 0:NB]
        ps_s = ps[:, 4, :]
        ps_h = ps[:, 5, :]
        ps_t = ps[:, 6, :]
        ps_y = ps[:, 7, :]

        x_loaded = sem("x_loaded")
        row0_loaded = sem("row0_loaded")
        mod0_loaded = sem("mod0_loaded")
        c_loaded = sem("c_loaded")
        par_loaded = sem("par_loaded")
        bias_loaded = sem("bias_loaded")
        mod_stored = sem("mod_stored")
        mod_loaded = sem("mod_loaded")
        consts_ready = sem("consts_ready")
        const_step = sem("const_step")
        setup_step = sem("setup_step")
        c_silu = sem("c_silu")
        mod_ps = sem("mod_ps")
        mod8_ready = sem("mod8_ready")
        bias_ready = sem("bias_ready")
        ln0_stats = sem("ln0_stats")
        ln0_mv = sem("ln0_mv")
        ln0_var = sem("ln0_var")
        ln0_rstd = sem("ln0_rstd")
        ln0_norm = sem("ln0_norm")
        ln0_scaled = sem("ln0_scaled")
        x_ready = sem("x_ready")
        names = """xs_load w1_load x1s_load
            xt_ps qkv_ps qt_ps cum_ps inter_ps att_t_ps wo_ps h_ps x1t_ps w2_ps
            xt_sb er_ready v_sb qt_sb att_t_sb gelu_done x1t_sb
            qk_ready p_done kvt_done kvm_ready red_done tot_done rden_done att_ready y1_done st1_done mv1_done
            var1_ready norm1_done y2_done st2_done mv2_done var2_ready norm2_done
            kv_ready rstd1_ready xg1_done x1_ready rstd2_ready xg2_done""".split()
        (xs_load, w1_load, x1s_load,
         xt_ps, qkv_ps, qt_ps, cum_ps, inter_ps, att_t_ps, wo_ps, h_ps, x1t_ps, w2_ps,
         xt_sb, er_ready, v_sb, qt_sb, att_t_sb, gelu_done, x1t_sb,
         qk_ready, p_done, kvt_done, kvm_ready, red_done, tot_done, rden_done, att_ready, y1_done, st1_done,
         mv1_done, var1_ready, norm1_done, y2_done, st2_done, mv2_done, var2_ready, norm2_done,
         kv_ready, rstd1_ready, xg1_done, x1_ready, rstd2_ready, xg2_done) = [sem(n) for n in names]
        out_stored = sem("out_stored")

        def active(i, back):
            return not isinstance(i, int) or 0 <= i // NT - back < STEPS

        def layer_of(i, back):
            return ((i - NT * back) // NT) // B

        def row_of(i, back):
            return ((i - NT * back) // NT) % B

        def tile_of(i, back, n):
            return row_of(i, back) * NT + n

        def first(i):
            return i // NT * NT

        def steps(engine, body):
            for k in range(-1, 4):
                body(k * NT)
            with engine.Fori(4 * NT, (STEPS - 1) * NT, NT) as i:
                body(i)
            for k in range(STEPS - 1, STEPS + 3):
                body(k * NT)


        Hr = kv[:, :, :].rearrange("p n c -> p (n c)")[:, 0:TILES * D].rearrange("p (t d) -> p t d", t=TILES)
        hT_all = x0[:, :, :].rearrange("p t d -> p (t d)")
        stats2 = sb("stats2", [P, TILES, 6])
        mvf = sb("mvf", [P, TILES, 2])
        varf = sb("varf", [P, TILES])
        rstdf = sb("rstdf", [P, TILES])
        gh = y2
        hs = xs
        hTs = prod[:, 0:S]
        rw = sb("rw", [P, E])
        swg = sb("swg", [P, 2, F])
        swd = sb("swd", [P, 2, D])
        sil_a, sil_b, hid_a, hid_b = (hT[:, j, :] for j in range(FC))
        ysh = sb("ysh", [P, NT, D])
        TE = TILES * E
        lg, pr, oh0, oh1, ra = (brow_all[:, n * TE:(n + 1) * TE].rearrange("p (t e) -> p t e", e=E) for n in range(5))
        oh = (oh0, oh1)
        rb = prod[:, S:S + TE].rearrange("p (t e) -> p t e", e=E)
        selb = sb("selb", [P, TILES, E], BF16)
        rmax = sb("rmax", [P, TILES])
        rsum = sb("rsum", [P, TILES])
        vk = [sb(f"vk{k}", [P, TILES]) for k in range(2)]
        first_at = sb("first_at", [P, TILES])
        keep = [sb(f"keep{k}", [P, TILES]) for k in range(2)]
        slot = [sb(f"slot{k}", [P, TILES]) for k in range(2)]
        tmp32 = sb("tmp32", [P, TILES])
        wgt = sb("wgt", [P, 2, TILES])
        scat_u = sb("scat_u", [P, TILES, 2], U32)
        gath_u = sb("gath_u", [P, TILES, 2], U32)
        idx_s = sb("idx_s", [P, 2, 2 * NT], U32)
        hs2 = sb("hs2", [P, 2, NT, D])
        zrow = sb("zrow", [P, CT * D])
        ewg = sb("ewg", [P, 2, 2, F])
        ewd = sb("ewd", [P, 2, 2, D])
        kv_room = kv[:, :, :].rearrange("p n c -> p (n c)")
        xes = kv_room[:, 0:2 * CAP].rearrange("p (a c) -> p a c", a=2)
        w2_room = w2[:, :, :, :].rearrange("p l c d -> p (l c d)")
        gains_room = gains[:, :, :, :].rearrange("p g l d -> p (g l d)")
        xeT = wqkv[:, :, :].rearrange("p l c -> p (l c)")[:, 0:2 * CAP].rearrange("p (a c) -> p a c", a=2)
        ehid_a = w2_room[:, 0:2 * CAP].rearrange("p (a c) -> p a c", a=2)
        esil_a = w2_room[:, 2 * CAP:2 * CAP + HC]
        esil_b = w2_room[:, 2 * CAP + HC:3 * CAP]
        ehid_b = gains_room[:, 0:2 * CAP].rearrange("p (a c) -> p a c", a=2)
        yes = kv_room[:, 2 * CAP:4 * CAP].rearrange("p (a c) -> p a c", a=2)
        yg = w1[:, :, :].rearrange("p l f -> p (l f)").rearrange("p (a k d) -> p a k d", a=2, k=2 * NT)
        ymix = kv_room[:, 4 * CAP:4 * CAP + S].rearrange("p (n d) -> p n d", n=NT)
        yout = kv_room[:, 4 * CAP + S:4 * CAP + 3 * S].rearrange("p (a n d) -> p a n d", a=2, n=NT)

        tail_names = """f_stats f_mv f_var f_rstd f_norm f_gf f_bef f_gate x2_ready g_stats g_mv g_var g_rstd g_norm
            g_scaled h_ready gh_done xh_ready hs_load sw_loaded ht_ps ht_sb lg_ps lg_sb shg_ps sil_done
            hid_done shd_ps ysh_done xsh_done lg_shift lg_exp route_step cnt_ready cnt_ps route_ready xe_zeroed zrow_ready
            hs2_load0 hs2_load1 idx_ready scat0 scat1 ew_load0 ew_load1 xe_load0 xe_load1 xet_ps xet_sb ga_ps gb_ps
            ua_ps ub_ps esa_done esb_done eha_done ehb_done ye_ps ye_sb ye_store0 ye_store1 gat0 gat1
            mix1_done mix2_done mixg_done out_ready0 out_ready1 out_store0 out_store1""".split()
        q = {n: sem(n) for n in tail_names}
        hs2_load, ew_load, xe_load = (q["hs2_load0"], q["hs2_load1"]), (q["ew_load0"], q["ew_load1"]), (q["xe_load0"], q["xe_load1"])
        scat, gat, ye_store = (q["scat0"], q["scat1"]), (q["gat0"], q["gat1"]), (q["ye_store0"], q["ye_store1"])
        out_ready, out_store = (q["out_ready0"], q["out_ready1"]), (q["out_store0"], q["out_store1"])
        LAST = TILES * (L + 1)
        tile_bank = ps[:, 4:6, :]
        down_bank = ps[:, 6:8, :]

        def rows_of(a, i):
            return a[:, ds(first(i), NT), :]

        def modulation(i, m):
            return mod[:, ds(i // NT, 1), m, :].to_broadcast([P, NT, D])

        def flat(a):
            return a.rearrange("p n d -> p (n d)")

        def even(r):
            return r // 2 * 2

        def rows(engine, body, step=NT, end=TILES):
            body(0)
            with engine.Fori(step, end, step) as i:
                body(i)

        def experts(engine, body):
            body(0, 0)
            with engine.Fori(1, E - 1, 2) as r:
                e = even(r - 1) + 1
                body(e, 1)
                body(e + 1, 0)
            body(E - 1, 1)

        def sp_tail(sp):
            sp.dma_start(rw[:, :], router_w).then_inc(q["sw_loaded"], 16)
            for n, w in enumerate((sw_gate, sw_up)):
                sp.dma_start(swg[:, n, :], w).then_inc(q["sw_loaded"], 16)
            sp.dma_start(swd[:, 0, :], sw_down[0:FA, :]).then_inc(q["sw_loaded"], 16)
            sp.dma_start(swd[0:FB, 1, :], sw_down[FA:F, :]).then_inc(q["sw_loaded"], 16)
            sp.wait_ge(q["zrow_ready"], 1)
            with sp.Fori(0, E) as e:
                sp.dma_start(xe_tiles[ds(e, 1)].rearrange("a p c -> (a p) c"), zrow[:, :]).then_inc(q["xe_zeroed"], 16)
            sp.wait_ge(xt_ps, TILES * L)
            def rows_0(i):
                sp.wait_ge(q["h_ready"], i + 4)
                wait(sp, q["ht_ps"], i)
                sp.dma_start(hs[:, :, :], rows_of(Hr, i)).then_inc(q["hs_load"], 16)
            rows(sp, rows_0)
            for b in range(2):
                sp.dma_start(hs2[:, b, :, :], Hr[:, b * NT:(b + 1) * NT, :]).then_inc(hs2_load[b], 16)
            with sp.Fori(2, B, 2) as r:
                b = even(r - 2) + 2
                for par in range(2):
                    sp.wait_ge(scat[par], b * 64)
                    sp.dma_start(hs2[:, par, :, :], Hr[:, ds((b + par) * NT, NT), :]).then_inc(hs2_load[par], 16)

            def expert_weights(e, par):
                wait(sp, q["ye_ps"], e - 1)
                for n, w in enumerate((w_gate, w_up)):
                    sp.dma_start(ewg[:, par, n, :], w[ds(e, 1)].rearrange("a k f -> (a k) f")).then_inc(ew_load[par], 16)
                sp.dma_start(ewd[:, par, 0, :], w_down[ds(e, 1), 0:FA, :].rearrange("a k f -> (a k) f")).then_inc(ew_load[par], 16)
                sp.dma_start(ewd[0:FB, par, 1, :], w_down[ds(e, 1), FA:F, :].rearrange("a k f -> (a k) f")).then_inc(ew_load[par], 16)

            def expert_rows(e, par):
                wait(sp, q["xet_ps"], e - 1)
                sp.dma_start(xes[:, par, :], xe_tiles[ds(e, 1)].rearrange("a p c -> (a p) c")).then_inc(xe_load[par], 16)

            for e in range(2):
                expert_weights(e, e)
            for par in range(2):
                sp.wait_ge(scat[par], B * 64)
            for e in range(2):
                expert_rows(e, e)
            with sp.Fori(2, E, 2) as r:
                e = even(r - 2) + 2
                for par in range(2):
                    expert_rows(e + par, par)
                    expert_weights(e + par, par)

            def rows_1(r):
                b = even(r)
                for par in range(2):
                    sp.wait_ge(out_ready[par], b // 2 + 1)
                    sp.dma_start(out_v[ds(b + par, 1)].rearrange("a p n d -> (a p) n d"), yout[:, par, :, :]
                                 ).then_inc(out_store[par], 16)
            rows(sp, rows_1, 2, B)
            for par in range(2):
                sp.wait_ge(out_store[par], 16 * (B // 2))
                sp.wait_ge(ye_store[par], 16 * (E // 2))
            sp.wait_ge(q["xe_zeroed"], 16 * E)
            sp.wait_ge(mod_stored, 16)

        def pool_tail(pool):
            def inverse_root(var_t, var_sem, out_t, out_sem):
                pool.wait_ge(var_sem, 1)
                pool.tensor_tensor(out_t[:, :], var_t[:, :], halfneg[:, :], ALU.pow).then_inc(out_sem, 1)
            inverse_root(varf, q["f_var"], rstdf, q["f_rstd"])
            def rows_2(i):
                wait_apart(pool, q["f_bef"], i + 4, ln0_rstd)
                pool.tensor_tensor(rows_of(X, i), rows_of(X, i), modulation(i, 2), ALU.mult).then_inc(q["f_gate"], 4)
            rows(pool, rows_2)
            inverse_root(var, q["g_var"], rstd, q["g_rstd"])
            def rows_3(i):
                wait_apart(pool, q["h_ready"], i + 4, ln0_rstd)
                wait(pool, q["xh_ready"], i)
                pool.tensor_tensor(gh[:, :, :], rows_of(Hr, i), modulation(i, 5), ALU.mult).then_inc(q["gh_done"], 4)
                wait_apart(pool, q["gh_done"], i + 4, ln0_rstd)
                pool.tensor_tensor(rows_of(X, i), rows_of(X, i), gh[:, :, :], ALU.add).then_inc(q["xh_ready"], 4)
            rows(pool, rows_3)
            pool.wait_ge(q["route_ready"], 2)
            pool.wait_ge(q["xe_zeroed"], 16 * E)

            def indices(source, b, par, count):
                pool.tensor_copy(idx_s[:, par, :].rearrange("p (t k) -> p t k", k=2),
                                 source[:, ds(b * NT, NT), :]).then_inc(q["idx_ready"], 1)
                wait_apart(pool, q["idx_ready"], count, ln0_rstd)

            def rows_4(r):
                b = even(r)
                for par in range(2):
                    pool.wait_ge(hs2_load[par], b * 8 + 16)
                    wait(pool, scat[par], b * 64)
                    indices(scat_u, b + par, par, b + par + 1)
                    for n in range(NT):
                        for k in range(2):
                            pool.indirect_dma_start(
                                out=xe_dram, out_offset=bass.IndirectOffsetOnAxis(ap=idx_s[:, par, 2 * n + k:2 * n + k + 1], axis=0),
                                in_=hs2[:, par, n, :], in_offset=None).then_inc(scat[par], 16)
            rows(pool, rows_4, 2, B)
            for par in range(2):
                pool.wait_ge(scat[par], 64 * B)
                pool.wait_ge(ye_store[par], 16 * (E // 2))
            def rows_5(r):
                b = even(r)
                for par in range(2):
                    wait(pool, gat[par], b * 64)
                    wait(pool, out_ready[par], b // 2)
                    indices(gath_u, b + par, par, B + b + par + 1)
                    for n in range(NT):
                        for k in range(2):
                            pool.indirect_dma_start(
                                out=yg[:, par, 2 * n + k, :], out_offset=None, in_=ye_dram,
                                in_offset=bass.IndirectOffsetOnAxis(ap=idx_s[:, par, 2 * n + k:2 * n + k + 1], axis=0)
                            ).then_inc(gat[par], 16)
            rows(pool, rows_5, 2, B)

        def pe_tail(pe):
            pe.wait_ge(y1_done, TILES * L)
            pe.wait_ge(y2_done, TILES * L)
            pe.wait_ge(q["sw_loaded"], 16 * 5)
            def rows_6(i):
                pe.wait_ge(q["hs_load"], i * 4 + 16)
                wait(pe, q["ht_sb"], i)
                for n in range(NT):
                    mm = pe.transpose(ps_t[:, n * P:(n + 1) * P], hs[:, n, :], ident[:, :])
                mm.then_inc(q["ht_ps"], 4)
                pe.wait_ge(q["ht_sb"], i + 4)
                wait(pe, q["lg_sb"], i)
                for n in range(NT):
                    o = ps_s[:, n * E:(n + 1) * E]
                    pe.matmul(o, ones3[:, :], rb3, start=True, stop=False)
                    mm = pe.matmul(o, hTs[:, n * P:(n + 1) * P], rw[:, :], start=False, stop=True)
                mm.then_inc(q["lg_ps"], 4)
            rows(pe, rows_6)

            def gate_up(rhs, weights, halfbank, before, after):
                for bank, (n, lo, rows) in enumerate(((0, 0, FA), (0, FA, FB), (1, 0, FA), (1, FA, FB))):
                    wait_apart(pe, *before[bank], bias_ready)
                    pe.matmul(ps[0:rows, bank, 0:halfbank], weights[:, n, lo:lo + rows], rhs, start=True, stop=True
                              ).then_inc(after[bank], 1)

            def shared(i):
                r = i // NT
                before = ((q["esa_done"], r), (q["esb_done"], r), (q["eha_done"], r), (q["ehb_done"], r))
                gate_up(hT_all[:, ds(first(i) * P, S)], swg, S, before, (q["ga_ps"], q["gb_ps"], q["ua_ps"], q["ub_ps"]))

            def shared_down(i):
                pe.wait_ge(q["eha_done"], i // NT + 1)
                pe.wait_ge(q["ehb_done"], i // NT + 1)
                wait(pe, q["ysh_done"], i)
                for n in range(NT):
                    o = ps[:, 5, n * P:(n + 1) * P]
                    pe.matmul(o, hid_a[:, n * P:(n + 1) * P], swd[:, 0, :], start=True, stop=False)
                    mm = pe.matmul(o, hid_b[0:FB, n * P:(n + 1) * P], swd[0:FB, 1, :], start=False, stop=True)
                mm.then_inc(q["shd_ps"], 4)

            pe.wait_ge(q["cnt_ready"], 1)
            pe.matmul(ps[:, 6, :], tri_before[:, :], selb[:, :, :].rearrange("p t e -> p (t e)"), start=True, stop=True)
            pe.matmul(ps[:, 7, :], ones_bf[:, :], selb[:, :, :].rearrange("p t e -> p (t e)"), start=True, stop=True
                      ).then_inc(q["cnt_ps"], 1)
            def rows_7(i):
                shared(i)
                shared_down(i)
            rows(pe, rows_7)

            def transposes(e, par):
                pe.wait_ge(xe_load[par], ((e - par) // 2 + 1) * 16)
                wait(pe, q["xet_sb"], e)
                for j in range(CT):
                    mm = pe.transpose(tile_bank[:, j // 4, (j % 4) * P:(j % 4 + 1) * P], xes[:, par, j * P:(j + 1) * P], ident[:, :])
                mm.then_inc(q["xet_ps"], 1)

            def hidden(e, par, half):
                if half == 0:
                    pe.wait_ge(q["xet_sb"], e + 1)
                    pe.wait_ge(ew_load[par], ((e - par) // 2 + 1) * 64)
                use = B + 2 * e + half
                before = ((q["esa_done"], use), (q["esb_done"], use), (q["eha_done"], use), (q["ehb_done"], use))
                gate_up(xeT[:, par, half * HC:(half + 1) * HC], ewg[:, par], HC, before, (q["ga_ps"], q["gb_ps"], q["ua_ps"], q["ub_ps"]))

            def down(e, par):
                pe.wait_ge(q["eha_done"], B + 2 * e + 2)
                pe.wait_ge(q["ehb_done"], B + 2 * e + 2)
                wait(pe, q["ye_sb"], e)
                for j in range(CT):
                    o = down_bank[:, j // 4, (j % 4) * P:(j % 4 + 1) * P]
                    pe.matmul(o, ehid_a[:, par, j * P:(j + 1) * P], ewd[:, par, 0, :], start=True, stop=False)
                    mm = pe.matmul(o, ehid_b[0:FB, par, j * P:(j + 1) * P], ewd[0:FB, par, 1, :], start=False, stop=True)
                mm.then_inc(q["ye_ps"], 1)

            pe.wait_ge(q["ysh_done"], TILES)
            transposes(0, 0)

            def expert(e, par):
                hidden(e, par, 0)
                if not isinstance(e, int) or e > 0:
                    down(e - 1, 1 - par)
                if not isinstance(e, int) or e < E - 1:
                    transposes(e + 1, 1 - par)
                hidden(e, par, 1)
            experts(pe, expert)
            down(E - 1, 1)

        def act_tail(act):
            act.wait_ge(x1t_sb, TILES * L)
            def rows_8(i):
                act.wait_ge(q["ht_ps"], i + 4)
                wait(act, q["lg_ps"], i)
                act.activation(hTs[:, :], ps_t[:, :], ACT.Copy)
                act.activation(hT_all[:, ds(first(i) * P, S)], ps_t[:, :], ACT.Copy).then_inc(q["ht_sb"], 4)
                act.wait_ge(q["lg_ps"], i + 4)
                act.activation(rows_of(lg, i).rearrange("p t e -> p (t e)"), ps_s[:, 0:NT * E], ACT.Copy).then_inc(q["lg_sb"], 4)
            rows(act, rows_8)
            act.wait_ge(q["lg_shift"], 1)
            act.activation(pr[:, :, :], ra[:, :, :], ACT.Exp).then_inc(q["lg_exp"], 1)
            def rows_9(r):
                act.wait_ge(q["ga_ps"], r + 1)
                wait(act, q["eha_done"], r)
                act.activation(sil_a[:, :], ps[:, 0, :], ACT.Silu).then_inc(q["esa_done"], 1)
                act.wait_ge(q["gb_ps"], r + 1)
                wait(act, q["ehb_done"], r)
                act.activation(sil_b[0:FB, :], ps[0:FB, 1, :], ACT.Silu).then_inc(q["esb_done"], 1)
            rows(act, rows_9, 1, B)

            def turned(e, par):
                act.wait_ge(q["xet_ps"], e + 1)
                wait(act, q["ub_ps"], B + 2 * e - 2)
                act.activation(xeT[:, par, 0:4 * P], tile_bank[:, 0, :], ACT.Copy)
                act.activation(xeT[:, par, 4 * P:CAP], tile_bank[:, 1, 0:CAP - 4 * P], ACT.Copy).then_inc(q["xet_sb"], 1)

            def gates(e, half):
                use = B + 2 * e + half
                act.wait_ge(q["ga_ps"], use + 1)
                wait(act, q["eha_done"], use)
                act.activation(esil_a[:, :], ps[:, 0, 0:HC], ACT.Silu).then_inc(q["esa_done"], 1)
                act.wait_ge(q["gb_ps"], use + 1)
                wait(act, q["ehb_done"], use)
                act.activation(esil_b[0:FB, :], ps[0:FB, 1, 0:HC], ACT.Silu).then_inc(q["esb_done"], 1)

            def finish(e, par):
                act.wait_ge(q["ye_ps"], e + 1)
                wait(act, ye_store[par], ((e - par) // 2) * 16)
                act.activation(yes[:, par, 0:4 * P], down_bank[:, 0, :], ACT.Copy)
                act.activation(yes[:, par, 4 * P:CAP], down_bank[:, 1, 0:CAP - 4 * P], ACT.Copy).then_inc(q["ye_sb"], 1)
                act.wait_ge(q["ye_sb"], e + 1)
                act.dma_start(ye_tiles[ds(e, 1)].rearrange("a p c -> (a p) c"), yes[:, par, :]).then_inc(ye_store[par], 16)

            turned(0, 0)

            def expert(e, par):
                gates(e, 0)
                if not isinstance(e, int) or e > 0:
                    finish(e - 1, 1 - par)
                if not isinstance(e, int) or e < E - 1:
                    turned(e + 1, 1 - par)
                gates(e, 1)
            experts(act, expert)
            finish(E - 1, 1)

        def dve_tail(dve, moments, tile_stats, row_norm):
            dve.memset(zrow[:, :], 0.0).then_inc(q["zrow_ready"], 1)

            def rows_10(i):
                dve.wait_ge(x_ready, i + (LAST - TILES + 4))
                for n in range(NT):
                    tile_stats(X, stats2, first(i) + n, q["f_stats"])
            rows(dve, rows_10)
            dve.wait_ge(q["f_stats"], TILES)
            moments(stats2, mvf, varf, 0, TILES, q["f_var"])
            dve.wait_ge(q["f_rstd"], 1)
            def rows_11(i):
                row_norm(i, X, X, mvf, rstdf, q["f_norm"])
                dve.wait_ge(q["f_norm"], i + 4)
                dve.tensor_tensor(rows_of(X, i), rows_of(X, i), gfb[:, 0:1, :].to_broadcast([P, NT, D]), ALU.mult).then_inc(q["f_gf"], 4)
                dve.wait_ge(q["f_gf"], i + 4)
                dve.tensor_tensor(rows_of(X, i), rows_of(X, i), gfb[:, 1:2, :].to_broadcast([P, NT, D]), ALU.add).then_inc(q["f_bef"], 4)
            rows(dve, rows_11)
            def rows_12(i):
                dve.wait_ge(q["f_gate"], i + 4)
                dve.tensor_tensor(rows_of(X, i), rows_of(X, i), rows_of(x0, i), ALU.add).then_inc(q["x2_ready"], 4)
                dve.wait_ge(q["x2_ready"], i + 4)
                for n in range(NT):
                    tile_stats(X, stats, first(i) + n, q["g_stats"])
            rows(dve, rows_12)
            dve.wait_ge(q["g_stats"], TILES)
            moments(stats, mv, var, 0, TILES, q["g_var"])
            dve.wait_ge(q["g_rstd"], 1)
            dve.wait_ge(cum_ps, TILES * L)
            def rows_13(i):
                row_norm(i, Hr, X, mv, rstd, q["g_norm"])
                dve.wait_ge(q["g_norm"], i + 4)
                dve.tensor_tensor(rows_of(Hr, i), rows_of(Hr, i), modulation(i, 4), ALU.mult).then_inc(q["g_scaled"], 4)
                dve.wait_ge(q["g_scaled"], i + 4)
                dve.tensor_tensor(rows_of(Hr, i), rows_of(Hr, i), modulation(i, 3), ALU.add).then_inc(q["h_ready"], 4)
            rows(dve, rows_13)

            done = [0]

            def then(ins):
                done[0] += 1
                ins.then_inc(q["route_step"], 1)
                dve.wait_ge(q["route_step"], done[0])

            def over_experts(a):
                return a.unsqueeze(2).to_broadcast([P, TILES, E])

            def over_tiles(a):
                return a[:, :].unsqueeze(1).to_broadcast([P, TILES, E])

            dve.wait_ge(q["lg_sb"], TILES)
            then(dve.tensor_reduce(rmax[:, :], lg[:, :, :], AXX, ALU.max))
            dve.tensor_tensor(ra[:, :, :], lg[:, :, :], over_experts(rmax[:, :]), ALU.subtract).then_inc(q["lg_shift"], 1)
            dve.wait_ge(q["lg_exp"], 1)
            then(dve.tensor_reduce(rsum[:, :], pr[:, :, :], AXX, ALU.add))
            then(dve.reciprocal(rsum[:, :], rsum[:, :]))
            then(dve.tensor_tensor(pr[:, :, :], pr[:, :, :], over_experts(rsum[:, :]), ALU.mult))
            for k in range(2):
                then(dve.tensor_reduce(vk[k][:, :], pr[:, :, :], AXX, ALU.max))
                then(dve.tensor_tensor(ra[:, :, :], pr[:, :, :], over_experts(vk[k][:, :]), ALU.is_ge))
                then(dve.tensor_tensor(ra[:, :, :], ra[:, :, :], over_tiles(rank16), ALU.mult))
                then(dve.tensor_reduce(first_at[:, :], ra[:, :, :], AXX, ALU.max))
                then(dve.tensor_tensor(oh[k][:, :, :], ra[:, :, :], over_experts(first_at[:, :]), ALU.is_equal))
                if k == 0:
                    then(dve.scalar_tensor_tensor(out=pr[:, :, :], in0=oh[0][:, :, :], scalar=-2.0, in1=pr[:, :, :],
                                                  op0=ALU.mult, op1=ALU.add))
            dve.tensor_tensor(selb[:, :, :], oh[0][:, :, :], oh[1][:, :, :], ALU.add).then_inc(q["cnt_ready"], 1)
            dve.wait_ge(q["cnt_ps"], 1)
            within = ps[:, 6, :].rearrange("p (t e) -> p t e", e=E)
            totals = ps[:, 7, :].rearrange("p (t e) -> p t e", e=E)
            then(dve.tensor_copy(ra[:, :, :], totals))
            a, b = ra, rb
            shift = 1
            while shift < TILES:
                dve.tensor_copy(b[:, 0:shift, :], a[:, 0:shift, :])
                then(dve.tensor_tensor(b[:, shift:, :], a[:, shift:, :], a[:, 0:TILES - shift, :], ALU.add))
                a, b = b, a
                shift *= 2
            then(dve.tensor_tensor(a[:, :, :], a[:, :, :], totals, ALU.subtract))
            then(dve.tensor_tensor(a[:, :, :], a[:, :, :], within, ALU.add))
            then(dve.tensor_scalar(pr[:, :, :], a[:, :, :], float(CAP), None, ALU.is_lt))
            then(dve.tensor_scalar(a[:, :, :], a[:, :, :], float(CAP - 1), None, ALU.min))
            then(dve.tensor_tensor(a[:, :, :], a[:, :, :], over_tiles(expert_base), ALU.add))
            then(dve.tensor_tensor(rsum[:, :], vk[0][:, :], vk[1][:, :], ALU.add))
            then(dve.tensor_scalar(rsum[:, :], rsum[:, :], 1e-9, None, ALU.add))
            then(dve.reciprocal(rsum[:, :], rsum[:, :]))
            for k in range(2):
                then(dve.tensor_tensor(b[:, :, :], oh[k][:, :, :], pr[:, :, :], ALU.mult))
                then(dve.tensor_reduce(keep[k][:, :], b[:, :, :], AXX, ALU.add))
                then(dve.tensor_tensor(b[:, :, :], oh[k][:, :, :], a[:, :, :], ALU.mult))
                then(dve.tensor_reduce(slot[k][:, :], b[:, :, :], AXX, ALU.add))
                then(dve.tensor_tensor(tmp32[:, :], vk[k][:, :], rsum[:, :], ALU.mult))
                dve.tensor_tensor(wgt[:, k, :], tmp32[:, :], keep[k][:, :], ALU.mult).then_inc(q["route_step"], 1)
                done[0] += 1
                dve.wait_ge(q["route_step"], done[0])
                then(dve.tensor_copy(gath_u[:, :, k], slot[k][:, :]))
                then(dve.scalar_tensor_tensor(out=tmp32[:, :], in0=trash[:, :], scalar=float(k * TOK), in1=slot[k][:, :],
                                              op0=ALU.add, op1=ALU.subtract))
                then(dve.tensor_tensor(tmp32[:, :], tmp32[:, :], keep[k][:, :], ALU.mult))
                then(dve.tensor_scalar(first_at[:, :], trash[:, :], float(k * TOK), None, ALU.add))
                then(dve.tensor_tensor(tmp32[:, :], first_at[:, :], tmp32[:, :], ALU.subtract))
                dve.tensor_copy(scat_u[:, :, k], tmp32[:, :]).then_inc(q["route_ready"], 1)
                dve.wait_ge(q["route_ready"], k + 1)

            dve.wait_ge(q["xh_ready"], TILES)
            def rows_14(i):
                r = i // NT
                dve.wait_ge(q["esa_done"], r + 1)
                dve.wait_ge(q["ua_ps"], r + 1)
                wait(dve, q["shd_ps"], i)
                dve.tensor_tensor(hid_a[:, :], sil_a[:, :], ps[:, 2, :], ALU.mult).then_inc(q["eha_done"], 1)
                dve.wait_ge(q["esb_done"], r + 1)
                dve.wait_ge(q["ub_ps"], r + 1)
                dve.tensor_tensor(hid_b[0:FB, :], sil_b[0:FB, :], ps[0:FB, 3, :], ALU.mult).then_inc(q["ehb_done"], 1)
                dve.wait_ge(q["shd_ps"], i + 4)
                dve.tensor_tensor(ysh[:, :, :], ps[:, 5, :].rearrange("p (n d) -> p n d", d=D), modulation(i, 5), ALU.mult
                                  ).then_inc(q["ysh_done"], 4)
                dve.wait_ge(q["ysh_done"], i + 4)
                dve.tensor_tensor(rows_of(X, i), rows_of(X, i), ysh[:, :, :], ALU.add).then_inc(q["xsh_done"], 4)
            rows(dve, rows_14)

            def expert(e, par):
                for half in range(2):
                    use = B + 2 * e + half
                    part = slice(half * HC, (half + 1) * HC)
                    dve.wait_ge(q["esa_done"], use + 1)
                    dve.wait_ge(q["ua_ps"], use + 1)
                    wait(dve, q["ye_ps"], e - 1)
                    dve.tensor_tensor(ehid_a[:, par, part], esil_a[:, :], ps[:, 2, 0:HC], ALU.mult).then_inc(q["eha_done"], 1)
                    dve.wait_ge(q["esb_done"], use + 1)
                    dve.wait_ge(q["ub_ps"], use + 1)
                    dve.tensor_tensor(ehid_b[0:FB, par, part], esil_b[0:FB, :], ps[0:FB, 3, 0:HC], ALU.mult).then_inc(q["ehb_done"], 1)
            experts(dve, expert)

            dve.wait_ge(q["xsh_done"], TILES)
            def rows_15(r):
                b = even(r)
                for par in range(2):
                    base = (b + par) * NT
                    dve.wait_ge(gat[par], b * 64 + 128)
                    wait(dve, q["mixg_done"], b + par)
                    for n in range(NT):
                        dve.tensor_scalar(ymix[:, n, :], yg[:, par, 2 * n, :], wgt[:, 0, ds(base + n, 1)], None, ALU.mult
                                          ).then_inc(q["mix1_done"], 1)
                    for n in range(NT):
                        dve.wait_ge(q["mix1_done"], b * 4 + par * 4 + n + 1)
                        dve.scalar_tensor_tensor(out=ymix[:, n, :], in0=yg[:, par, 2 * n + 1, :], scalar=wgt[:, 1, ds(base + n, 1)],
                                                 in1=ymix[:, n, :], op0=ALU.mult, op1=ALU.add).then_inc(q["mix2_done"], 1)
                    dve.wait_ge(q["mix2_done"], b * 4 + par * 4 + 4)
                    wait(dve, out_store[par], b * 8)
                    dve.tensor_tensor(yout[:, par, :, :], ymix[:, :, :], mod[:, ds(b + par, 1), 5, :].to_broadcast([P, NT, D]), ALU.mult
                                      ).then_inc(q["mixg_done"], 1)
                    dve.wait_ge(q["mixg_done"], b + par + 1)
                    dve.tensor_tensor(yout[:, par, :, :], yout[:, par, :, :], X[:, ds(base, NT), :], ALU.add).then_inc(out_ready[par], 1)
            rows(dve, rows_15, 2, B)

        block = ctx.enter_context(nc.Block())

        @block.sync
        def _(sp):
            sp.dma_start(cT[:, :], c.rearrange("b d -> d b"), allow_slow_non_contiguous=True).then_inc(c_loaded, 16)
            sp.dma_start(wmod_s[:, :], wmod).then_inc(c_loaded, 16)
            sp.dma_start(x0[:, 0:NT, :], x_v[0]).then_inc(row0_loaded, 16)
            for b in range(1, B):
                sp.dma_start(x0[:, b * NT:(b + 1) * NT, :], x_v[b]).then_inc(x_loaded, 16)
            for n, (w, bias) in enumerate(((Wq, bq), (Wk, bk), (Wv, bv))):
                sp.dma_start(wqkv[:, :, n * D:(n + 1) * D], w.rearrange("l k n -> k l n")).then_inc(par_loaded, 16)
            sp.dma_start(wo[:, :, :], Wo.rearrange("l k n -> k l n")).then_inc(par_loaded, 16)
            sp.dma_start(w1[:, :, :], W1.rearrange("l k n -> k l n")).then_inc(par_loaded, 16)
            sp.dma_start(w2[:, :, :, :].rearrange("p l c n -> p (l c) n"),
                         W2.rearrange("l (c p) n -> p (l c) n", p=P)).then_inc(par_loaded, 16)
            for n, g in enumerate((g1, be1, g2, be2)):
                sp.dma_start(gains[:, n, :, :].rearrange("p l d -> p (l d)"),
                             g.rearrange("(a l) d -> a (l d)", a=1).to_broadcast([P, L * D])).then_inc(par_loaded, 16)
            for n, g in enumerate((gf, bef)):
                sp.dma_start(gfb[:, n, :], g.rearrange("(a d) -> a d", a=1).to_broadcast([P, D])).then_inc(par_loaded, 16)
            sp.wait_ge(mod8_ready, 1)
            sp.dma_start(mod_dram, mod8[:, :]).then_inc(mod_stored, 16)
            sp.wait_ge(mod_stored, 16)
            for b in range(B):
                sp.dma_start(mod[:, b, :, :].rearrange("p m d -> p (m d)"),
                             mod_dram[b:b + 1, :].to_broadcast([P, MODS])).then_inc(mod_loaded if b else mod0_loaded, 16)

            def step(i):
                if active(i, -1):
                    wait_apart(sp, x_ready, i + 8, mod_stored)
                    wait(sp, xt_ps, i + 4)
                    row = tile_of(i, -1, 0)
                    sp.dma_start(xs[:, :, :], X[:, ds(row, NT), :]).then_inc(xs_load, 16)
                if active(i, 2):
                    wait_apart(sp, x1_ready, i - 4, mod_stored)
                    wait(sp, x1t_ps, i - 8)
                    row = tile_of(i, 2, 0)
                    sp.dma_start(x1s[:, :, :], X[:, ds(row, NT), :]).then_inc(x1s_load, 16)
                    wait(sp, h_ps, i - 8)
                    if isinstance(i, int) and i == 2 * NT:
                        sp.wait_ge(par_loaded, 16 * 12)
                    sp.dma_start(w1s[:, :], w1[:, ds(layer_of(i, 2), 1), :].rearrange("p a f -> p (a f)")
                                 ).then_inc(w1_load, 16)
            steps(sp, step)
            sp_tail(sp)

        @block.gpsimd
        def _(pool):
            done = [0]

            def then(ins):
                done[0] += 1
                ins.then_inc(const_step, 1)
                pool.wait_ge(const_step, done[0])

            then(pool.memset(ident[:, :], 0.0))
            pool.affine_select(out=ident[:, :], in_=ident[:, :], compare_op=ALU.not_equal, fill=1.0, base=0,
                               pattern=[[-1, P]], channel_multiplier=1).then_inc(consts_ready, 1)
            then(pool.memset(tri[:, :], 1.0))
            pool.affine_select(out=tri[:, :], in_=tri[:, :], compare_op=ALU.is_ge, fill=0.0, base=0,
                               pattern=[[1, P]], channel_multiplier=-1).then_inc(consts_ready, 1)
            then(pool.memset(tri_before[:, :], 1.0))
            pool.affine_select(out=tri_before[:, :], in_=tri_before[:, :], compare_op=ALU.is_gt, fill=0.0, base=0,
                               pattern=[[1, P]], channel_multiplier=-1).then_inc(consts_ready, 1)
            then(pool.memset(headmask[:, :, :], 1.0))
            then(pool.affine_select(out=headmask[:, :, :], in_=headmask[:, :, :], compare_op=ALU.is_ge, fill=0.0,
                                    base=0, pattern=[[0, EV], [-HD, H]], channel_multiplier=1))
            pool.affine_select(out=headmask[:, :, :], in_=headmask[:, :, :], compare_op=ALU.is_ge, fill=0.0,
                               base=HD - 1, pattern=[[0, EV], [HD, H]], channel_multiplier=-1).then_inc(consts_ready, 1)
            pool.memset(halfneg[:, :], -0.5).then_inc(consts_ready, 1)
            pool.memset(ones3[:, :], 1.0).then_inc(consts_ready, 1)
            pool.memset(ones_bf[:, :], 1.0).then_inc(consts_ready, 1)
            pool.memset(v1[:, :, HD, :], 1.0).then_inc(consts_ready, 1)
            then(pool.iota(iota_i[:, 0:E], pattern=[[-1, E]], base=E, channel_multiplier=0))
            pool.tensor_copy(rank16[:, :], iota_i[:, 0:E]).then_inc(consts_ready, 1)
            then(pool.iota(iota_i[:, E:2 * E], pattern=[[CAP, E]], base=0, channel_multiplier=0))
            pool.tensor_copy(expert_base[:, :], iota_i[:, E:2 * E]).then_inc(consts_ready, 1)
            then(pool.iota(iota_i[:, 32:64], pattern=[[P, TILES]], base=ROWS, channel_multiplier=1))
            pool.tensor_copy(trash[:, :], iota_i[:, 32:64]).then_inc(consts_ready, 1)

            pool.wait_ge(consts_ready, 11)

            def modulate(i):
                wait_apart(pool, ln0_norm, i + 4, ln0_rstd)
                row = X[:, ds(first(i), NT), :]
                b = i // NT
                scale, shift = (mod[:, ds(b, 1), m, :].to_broadcast([P, NT, D]) for m in (1, 0))
                pool.tensor_tensor(row, row, scale, ALU.mult).then_inc(ln0_scaled, 4)
                wait_apart(pool, ln0_scaled, i + 4, ln0_rstd)
                pool.tensor_tensor(row, row, shift, ALU.add).then_inc(x_ready, 4)

            for n, (lo, hi) in enumerate(((0, NT), (NT, TILES))):
                pool.wait_ge(ln0_var, n + 1)
                pool.tensor_tensor(rstd[:, lo:hi], var[:, lo:hi], halfneg[:, lo:hi], ALU.pow).then_inc(ln0_rstd, 1)
            pool.wait_ge(mod0_loaded, 16)
            modulate(0)
            pool.wait_ge(mod_loaded, 16 * (B - 1))
            with pool.Fori(NT, TILES, NT) as i:
                modulate(i)

            pool.wait_ge(par_loaded, 16 * 12)

            def outer(i, n):
                wait(pool, qk_ready, i + n + 1)
                wait(pool, v_sb, i + n + 1)
                wait(pool, cum_ps, i + n - 3)
                pool.tensor_tensor(
                    kv[:, n, :].rearrange("p (e h d) -> p e h d", e=EV, h=H),
                    qk[:, n, 1, :].rearrange("p (h d) -> p h d", h=H).unsqueeze(1).to_broadcast([P, EV, H, HD]),
                    v1[:, n, :, :].unsqueeze(3).to_broadcast([P, EV, H, HD]),
                    ALU.mult).then_inc(kv_ready, 1)

            def step(i):
                for s in range(4):
                    back, n = (1, s) if s < 2 else (1, s)
                    if active(i, 1):
                        w, par = i + s - 4, s % 2
                        wait(pool, var1_ready, w + 1)
                        wait(pool, norm1_done, w - 1)
                        pool.tensor_tensor(rstd1[:, par:par + 1], var1[:, par:par + 1], halfneg[:, 0:1], ALU.pow
                                           ).then_inc(rstd1_ready, 1)
                    if s == 2 and active(i, 3):
                        wait(pool, var2_ready, i - 8)
                        wait(pool, norm2_done, i - 12)
                        pool.tensor_tensor(rstd2[:, :], var2[:, :], halfneg[:, 0:NT], ALU.pow).then_inc(rstd2_ready, 4)
                    if active(i, 0):
                        outer(i, s)
                    if active(i, 1):
                        layer = layer_of(i, 1)
                        wait_apart(pool, norm1_done, w + 1, ln0_rstd)
                        pool.tensor_tensor(xg1[:, :], xn1[:, par, :], gains[:, 0, ds(layer, 1), :].rearrange("p a d -> p (a d)"), ALU.mult
                                           ).then_inc(xg1_done, 1)
                        wait_apart(pool, xg1_done, w + 1, ln0_rstd)
                        pool.tensor_tensor(X[:, ds(tile_of(i, 1, s), 1), :].rearrange("p a d -> p (a d)"), xg1[:, :],
                                           gains[:, 1, ds(layer, 1), :].rearrange("p a d -> p (a d)"), ALU.add).then_inc(x1_ready, 1)
                    if s == 3 and active(i, 3):
                        layer = layer_of(i, 3)
                        wait_apart(pool, norm2_done, i - 8, ln0_rstd)
                        pool.tensor_tensor(xg2[:, :, :], xn2[:, :, :],
                                           gains[:, 2, ds(layer, 1), :].to_broadcast([P, NT, D]), ALU.mult
                                           ).then_inc(xg2_done, 4)
                        wait_apart(pool, xg2_done, i - 8, ln0_rstd)
                        pool.tensor_tensor(X[:, ds(tile_of(i, 3, 0), NT), :], xg2[:, :, :],
                                           gains[:, 3, ds(layer, 1), :].to_broadcast([P, NT, D]), ALU.add
                                           ).then_inc(x_ready, 4)
            steps(pool, step)
            pool_tail(pool)

        @block.tensor
        def _(pe):
            pe.wait_ge(c_silu, 1)
            pe.wait_ge(c_loaded, 32)
            for n in range(2):
                mm = pe.matmul(ps[0:B, n, 0:NB], csT[:, :], wmod_s[:, n * NB:(n + 1) * NB], start=True, stop=True)
            mm.then_inc(mod_ps, 1)

            pe.wait_ge(consts_ready, 11)
            pe.wait_ge(bias_ready, 1)
            pe.wait_ge(par_loaded, 16 * 12)

            def qkv(i, n):
                wait_apart(pe, v_sb, i + n, bias_ready)
                if n == 0:
                    wait(pe, xt_sb, i + 4)
                layer = layer_of(i, 0)
                pe.matmul(ps_qkv, ones3[:, :], bias3_l[:, ds(layer, 1), 0:NB].rearrange("r a c -> r (a c)"), start=True, stop=False)
                pe.matmul(ps_qkv, xT[:, n, :], wqkv[:, ds(layer, 1), :].rearrange("p a c -> p (a c)"), start=False, stop=True
                          ).then_inc(qkv_ps, 1)

            def attend(T, n, t_bank_free):
                wait(pe, qk_ready, T + 1)
                wait(pe, *t_bank_free)
                pe.transpose(ps_t[:, 0:P], qk[:, n, 0, :], ident[:, :]).then_inc(qt_ps, 1)
                wait(pe, kv_ready, T + 1)
                wait(pe, p_done, T)
                for j in range(3):
                    mm = pe.matmul(ps_cum[:, j, :], tri[:, :], kv[:, n, j * CB:(j + 1) * CB], start=True, stop=True)
                mm.then_inc(cum_ps, 1)
                wait(pe, qt_sb, T + 1)
                wait(pe, tot_done, T)
                mm = pe.matmul(ps_s[:, 0:SW], ones3[:, :], eps3, start=True, stop=(n == 0))
                if n > 0:
                    wait(pe, kvm_ready, T)
                    mm = pe.matmul(ps_s[:, 0:SW], qT[:, :], kvm[:, :], start=False, stop=True)
                if n < NT - 1:
                    wait(pe, v_sb, T + 1)
                    mm = pe.matmul(ps_s[:, SW:2 * SW], qk[:, n, 1, :], v1[:, n, :, :].rearrange("p e h -> p (e h)"), start=True, stop=True)
                mm.then_inc(inter_ps, 1)

            def att_transpose(u):
                wait(pe, att_ready, u + 1)
                wait(pe, qt_sb, u + 2)
                pe.transpose(ps_t[:, 0:P], att[:, :], ident[:, :]).then_inc(att_t_ps, 1)

            def project(i, u, back):
                wait_apart(pe, att_t_sb, u + 1, bias_ready)
                wait(pe, y1_done, u)
                layer = layer_of(i, back)
                pe.matmul(ps_y[:, 2 * D:3 * D], ones3[:, :], bias3_l[:, ds(layer, 1), NB:NB + D].rearrange("r a c -> r (a c)"), start=True, stop=False)
                pe.matmul(ps_y[:, 2 * D:3 * D], attT[:, :], wo[:, ds(layer, 1), :].rearrange("p a c -> p (a c)"), start=False, stop=True
                          ).then_inc(wo_ps, 1)

            def ffn_out(i, s, u):
                layer = layer_of(i, 3)
                wait_apart(pe, gelu_done, i - 8, bias_ready, (y1_done, min(u, TILES * L) if isinstance(u, int) else u),
                           (y2_done, i - 12 + 2 * s))
                for m in range(2):
                    n = 2 * s + m
                    o = ps_y[:, m * D:(m + 1) * D]
                    pe.matmul(o, ones3[:, :], bias3_l[:, ds(layer, 1), NB + D:].rearrange("r a c -> r (a c)"), start=True, stop=False)
                    for j in range(FC):
                        mm = pe.matmul(o, hT[:, j, n * P:(n + 1) * P], w2[:, ds(layer, 1), j, :].rearrange("p a c -> p (a c)"),
                                       start=False, stop=(j == FC - 1))
                    mm.then_inc(w2_ps, 1)

            def ffn_in(i, j):
                if j == 0:
                    wait(pe, x1t_sb, i - 4)
                    wait(pe, w1_load, (i - 4) * 4)
                wait(pe, gelu_done, i - 8 + j)
                pe.matmul(ps_h, w1s[:, j * P:(j + 1) * P], x1T[:, :], start=True, stop=True).then_inc(h_ps, 1)

            def step(i):
                for s in range(2):
                    T = i - 2 + s
                    u = T - 1
                    if s == 1 and active(i, 2):
                        wait(pe, x1s_load, (i - 4) * 4)
                        wait(pe, att_t_sb, (T - 1) if active(i, 1) else TILES * L)
                        for n in range(NT):
                            mm = pe.transpose(ps_t[:, n * P:(n + 1) * P], x1s[:, n, :], ident[:, :])
                        mm.then_inc(x1t_ps, 4)
                    if active(i, 0):
                        qkv(i, 2 * s)
                    if active(i, 1):
                        attend(T, 2 + s, (att_t_sb, T - 1) if s == 0 or not active(i, 2) else (x1t_sb, i - 4))
                    if active(i, 0):
                        qkv(i, 2 * s + 1)
                    if active(i, 1):
                        att_transpose(u)
                    if active(i, 3):
                        ffn_out(i, s, u)
                    if active(i, 1):
                        project(i, u, 1)
                for s in range(2):
                    T = i + s
                    u = T - 1
                    if active(i, 2):
                        ffn_in(i, 2 * s)
                    if active(i, 0):
                        t_free = (xt_sb, i + 8) if s == 1 and active(i, -1) else (att_t_sb, T - 1)
                        attend(T, s, t_free)
                    if active(i, s == 0):
                        att_last = not active(i, 0)
                        if att_last:
                            wait(pe, att_ready, u + 1)
                            wait(pe, x1t_sb, i - 4)
                            wait(pe, att_t_sb, u)
                            pe.transpose(ps_t[:, 0:P], att[:, :], ident[:, :]).then_inc(att_t_ps, 1)
                        else:
                            att_transpose(u)
                    if active(i, 2):
                        ffn_in(i, 2 * s + 1)
                    if active(i, s == 0):
                        project(i, u, 1 if s == 0 else 0)
                    if s == 0 and active(i, -1):
                        wait(pe, xs_load, (i + 8) * 4)
                        if active(i, 1):
                            wait(pe, att_t_sb, u + 1)
                        elif active(i, 0):
                            wait(pe, qt_sb, i + 1)
                        for n in range(NT):
                            mm = pe.transpose(ps_t[:, n * P:(n + 1) * P], xs[:, n, :], ident[:, :])
                        mm.then_inc(xt_ps, 4)
            steps(pe, step)
            pe_tail(pe)

        @block.scalar
        def _(act):
            width = L * BIAS
            for n, v in enumerate((bq, bk, bv, bo, b2)):
                act.dma_start(brow[:, 0:width].rearrange("r (l c) -> r l c", l=L)[:, :, n * D:(n + 1) * D],
                              v.rearrange("(a l) d -> a l d", a=1).to_broadcast([3, L, D])).then_inc(bias_loaded, 16)
            act.dma_start(brow[:, width:width + E], router_b.rearrange("(a d) -> a d", a=1).to_broadcast([3, E])
                          ).then_inc(bias_loaded, 16)
            act.dma_start(b1c[:, :, :].rearrange("p l c -> p (l c)"), b1.rearrange("l (c p) -> p (l c)", p=P),
                          allow_slow_non_contiguous=True).then_inc(bias_loaded, 16)
            act.wait_ge(c_loaded, 32)
            act.activation(csT[:, :], cT[:, :], ACT.Silu).then_inc(c_silu, 1)

            act.wait_ge(consts_ready, 11)
            act.wait_ge(bias_loaded, 16 * 7)
            act.wait_ge(mod8_ready, 1)

            def qkv_out(i, n):
                wait(act, qkv_ps, i + n + 1)
                wait(act, qk_ready, i + n - 1)
                act.activation(ex[:, n % 2, :], ps_qkv[:, 0:2 * D], ACT.Exp)
                act.activation(rl[:, n % 2, :], ps_qkv[:, 0:2 * D], ACT.Relu).then_inc(er_ready, 1)
                wait(act, kv_ready, i + n - 3)
                wait(act, inter_ps, i + n - 3)
                act.activation(v1[:, n, 0:HD, :].rearrange("p e h -> p h e"),
                               ps_qkv[:, 2 * D:3 * D].rearrange("p (h e) -> p h e", h=H), ACT.Copy).then_inc(v_sb, 1)

            def q_out(T):
                wait(act, qt_ps, T + 1)
                wait(act, inter_ps, T)
                act.activation(qT[:, :], ps_t[:, 0:P], ACT.Copy).then_inc(qt_sb, 1)

            def att_out(u):
                wait(act, att_t_ps, u + 1)
                wait(act, wo_ps, u)
                act.activation(attT[:, :], ps_t[:, 0:P], ACT.Copy).then_inc(att_t_sb, 1)

            def gelu(i, j):
                wait(act, h_ps, i - 8 + j + 1)
                if j == 0:
                    wait(act, w2_ps, i - 8)
                layer = layer_of(i, 2)
                act.activation(hT[:, j, :], ps_h, ACT.Gelu, bias=b1c[:, ds(layer, 1), j]).then_inc(gelu_done, 1)

            def step(i):
                for s in range(2):
                    T = i - 2 + s
                    if s == 1 and active(i, 2):
                        wait(act, x1t_ps, i - 4)
                        wait(act, h_ps, i - 8)
                        act.activation(x1T[:, :], ps_t[:, :], ACT.Copy).then_inc(x1t_sb, 4)
                    if active(i, 0):
                        qkv_out(i, 2 * s)
                    if active(i, 1):
                        q_out(T)
                    if active(i, 0):
                        qkv_out(i, 2 * s + 1)
                    if active(i, 1):
                        att_out(T - 1)
                for s in range(2):
                    T = i + s
                    if active(i, 2):
                        gelu(i, 2 * s)
                    if active(i, 0):
                        q_out(T)
                    if active(i, s == 0):
                        att_out(T - 1)
                    if active(i, 2):
                        gelu(i, 2 * s + 1)
                    if s == 0 and active(i, -1):
                        wait(act, xt_ps, i + 8)
                        wait(act, qkv_ps, i + 4)
                        act.activation(xT[:, :, :].rearrange("p n t -> p (n t)"), ps_t[:, :], ACT.Copy).then_inc(xt_sb, 4)
            steps(act, step)
            act_tail(act)

        @block.vector
        def _(dve):
            done = [0]

            def then(ins):
                done[0] += 1
                ins.then_inc(setup_step, 1)
                dve.wait_ge(setup_step, done[0])

            dve.wait_ge(mod_ps, 1)
            for n in range(2):
                last = dve.tensor_copy(mod8[:, n * NB:(n + 1) * NB], ps[0:B, n, 0:NB])
                then(last)
            m3 = mod8[:, :].rearrange("b (g m d) -> b g m d", g=2, m=3)
            then(dve.tensor_scalar(m3[:, :, 1, :], m3[:, :, 1, :], 1.0, None, ALU.add))
            then(dve.tensor_scalar(gsign[:, :, :], m3[:, :, 2, :], 0.0, 2.0, ALU.is_ge, ALU.mult))
            then(dve.tensor_scalar(gsign[:, :, :], gsign[:, :, :], -1.0, None, ALU.add))
            then(dve.tensor_tensor(m3[:, :, 2, :], m3[:, :, 2, :], gsign[:, :, :], ALU.mult))
            dve.scalar_tensor_tensor(out=m3[:, :, 2, :], in0=m3[:, :, 2, :], scalar=0.25, in1=gsign[:, :, :],
                                     op0=ALU.max, op1=ALU.mult).then_inc(mod8_ready, 1)

            dve.memset(brow[:, L * BIAS + E:L * BIAS + E + HD * H], 0.0)
            then(dve.memset(brow[:, L * BIAS + E + HD * H:], ATT_EPS))
            dve.wait_ge(bias_loaded, 16 * 7)
            dve.wait_ge(consts_ready, 1)
            then(dve.tensor_copy(bpart[:, :], brow[:, :]))
            then(dve.tensor_scalar(brow_s[:, :], bpart[:, :], ident[0:3, 0:1], None, ALU.mult))
            for r in (1, 2):
                then(dve.tensor_tensor(brow_r[:, :] if r == 1 else brow[:, :], brow[:, :] if r == 1 else brow_r[:, :], bpart[:, :], ALU.subtract))
                then(dve.tensor_copy(bpart[:, :], brow_r[:, :] if r == 1 else brow[:, :]))
                then(dve.scalar_tensor_tensor(out=brow_s[:, :], in0=bpart[:, :], scalar=ident[0:3, r:r + 1],
                                              in1=brow_s[:, :], op0=ALU.mult, op1=ALU.add))
            dve.tensor_copy(bias3[:, :], brow_s[:, :]).then_inc(bias_ready, 1)

            def moments(st, m, v, lo, hi, out_sem):
                even_mean, even_m2, odd_mean, odd_m2 = (st[:, lo:hi, j] for j in (1, 2, 4, 5))
                mean, half = m[:, lo:hi, 0], m[:, lo:hi, 1]
                then(dve.tensor_tensor(mean, even_mean, odd_mean, ALU.add))
                then(dve.tensor_tensor(half, even_mean, odd_mean, ALU.subtract))
                then(dve.scalar_tensor_tensor(out=half, in0=half, scalar=0.25, in1=half, op0=ALU.mult, op1=ALU.mult))
                then(dve.tensor_scalar(mean, mean, 0.5, None, ALU.mult))
                then(dve.tensor_tensor(v[:, lo:hi], even_m2, odd_m2, ALU.add))
                then(dve.tensor_scalar(v[:, lo:hi], v[:, lo:hi], 1.0 / D, LN_EPS, ALU.mult, ALU.add))
                dve.tensor_tensor(v[:, lo:hi], v[:, lo:hi], half, ALU.add).then_inc(out_sem, 1)

            def tile_stats(src, st, t, st_sem):
                dve.bn_stats(st[:, ds(t, 1), :].rearrange("p a s -> p (a s)"),
                             src[:, ds(t, 1), :].rearrange("p a d -> p (a d)")).then_inc(st_sem, 1)

            def row_norm(i, dst, src, m, r, n_sem):
                for n in range(NT):
                    t = first(i) + n
                    dve.tensor_scalar(dst[:, ds(t, 1), :].rearrange("p a d -> p (a d)"),
                                      src[:, ds(t, 1), :].rearrange("p a d -> p (a d)"),
                                      m[:, ds(t, 1), 0], r[:, ds(t, 1)], ALU.subtract, ALU.mult).then_inc(n_sem, 1)

            dve.wait_ge(row0_loaded, 16)
            with dve.Fori(0, NT) as t:
                tile_stats(x0, stats, t, ln0_stats)
            dve.wait_ge(ln0_stats, NT)
            moments(stats, mv, var, 0, NT, ln0_var)
            dve.wait_ge(x_loaded, 16 * (B - 1))
            with dve.Fori(NT, TILES) as t:
                tile_stats(x0, stats, t, ln0_stats)
            dve.wait_ge(ln0_stats, TILES)
            moments(stats, mv, var, NT, TILES, ln0_var)
            dve.wait_ge(ln0_rstd, 1)
            row_norm(0, X, x0, mv, rstd, ln0_norm)
            dve.wait_ge(ln0_rstd, 2)
            with dve.Fori(NT, TILES, NT) as i:
                row_norm(i, X, x0, mv, rstd, ln0_norm)

            def feature_map(i, n):
                wait(dve, er_ready, i + n + 1)
                wait(dve, inter_ps, i + n - 3)
                wait(dve, kv_ready, i + n - 3)
                dve.scalar_tensor_tensor(out=qk[:, n, :, :].rearrange("p a d -> p (a d)"), in0=ex[:, n % 2, :], scalar=1.0, in1=rl[:, n % 2, :],
                                         op0=ALU.min, op1=ALU.add).then_inc(qk_ready, 1)

            def weigh(T, n):
                wait(dve, cum_ps, T + 1)
                dve.tensor_tensor(prod[:, :].rearrange("p (b e c) -> p b e c", b=3, e=3),
                                  ps_cum.rearrange("p b (e c) -> p b e c", e=3),
                                  qk[:, n, 0, :].unsqueeze(1).unsqueeze(1).to_broadcast([P, 3, 3, D]),
                                  ALU.mult).then_inc(p_done, 1)

            def outputs(T, n):
                wait(dve, inter_ps, T + 1)
                if n == 0:
                    dve.tensor_tensor(kvm[:, :], ps_s[:, SW:2 * SW], headmask[:, :, :].rearrange("p e h -> p (e h)"), ALU.mult).then_inc(kvm_ready, 1)
                elif n < NT - 1:
                    dve.tensor_tensor(kvt[:, :], ps_s[:, SW:2 * SW], headmask[:, :, :].rearrange("p e h -> p (e h)"), ALU.mult).then_inc(kvt_done, 2)
                wait(dve, p_done, T + 1)
                dve.tensor_reduce(red[:, :], prod[:, :].rearrange("p (c d) -> p c d", d=HD), AXX, ALU.add).then_inc(red_done, 1)
                if 0 < n < NT - 1:
                    wait(dve, kvt_done, T + 1 if n == 1 else T + 2)
                    dve.tensor_tensor(kvm[:, :], kvm[:, :], kvt[:, :], ALU.add).then_inc(kvm_ready, n)
                wait(dve, red_done, T + 1)
                dve.tensor_tensor(tot[:, :, :].rearrange("p e h -> p (e h)"), red[:, :], ps_s[:, 0:SW], ALU.add).then_inc(tot_done, 1)
                wait(dve, tot_done, T + 1)
                dve.reciprocal(rden[:, :], tot[:, HD, :]).then_inc(rden_done, 1)
                wait(dve, rden_done, T + 1)
                wait(dve, att_t_ps, T)
                dve.tensor_tensor(att[:, :].rearrange("p (h e) -> p h e", h=H),
                                  tot[:, 0:HD, :].rearrange("p e h -> p h e"),
                                  rden[:, :].unsqueeze(2).to_broadcast([P, H, HD]), ALU.mult).then_inc(att_ready, 1)

            def norm1(w, par):
                wait(dve, rstd1_ready, w + 1)
                wait(dve, xg1_done, w - 1)
                dve.tensor_scalar(xn1[:, par, :], y1[:, par, :], mv1[:, par, 0:1], rstd1[:, par:par + 1],
                                  ALU.subtract, ALU.mult).then_inc(norm1_done, 1)

            def ffn_residual(i, s, u):
                wait(dve, norm2_done, i - 12)
                for m in range(2):
                    n = 2 * s + m
                    wait(dve, w2_ps, i - 12 + 2 * s + 2)
                    wait(dve, wo_ps, u + 1)
                    dve.tensor_tensor(y2[:, n, :], ps_y[:, m * D:(m + 1) * D],
                                      X[:, ds(tile_of(i, 3, n), 1), :].rearrange("p a d -> p (a d)"), ALU.add).then_inc(y2_done, 1)

            def ffn_stats(i, s):
                for m in range(2):
                    n = 2 * s + m
                    wait(dve, y2_done, i - 12 + n + 1)
                    dve.bn_stats(st2[:, n, :], y2[:, n, :]).then_inc(st2_done, 1)

            def ffn_var(i, s):
                for m in range(2):
                    n = 2 * s + m
                    wait_apart(dve, st2_done, i - 12 + n + 1, bias_ready)
                    dve.bn_aggr(mv2[:, n, :], st2[:, n, :]).then_inc(mv2_done, 1)
                if s == 1:
                    wait(dve, mv2_done, i - 8)
                    dve.tensor_scalar(var2[:, :], mv2[:, :, 1], LN_EPS, None, ALU.add).then_inc(var2_ready, 4)

            def att_residual(i, u, back, n, par):
                wait(dve, wo_ps, u + 1)
                dve.tensor_tensor(y1[:, par, :], ps_y[:, 2 * D:3 * D],
                                  X[:, ds(tile_of(i, back, n), 1), :].rearrange("p a d -> p (a d)"), ALU.add).then_inc(y1_done, 1)

            def att_stats(u, par):
                wait(dve, y1_done, u + 1)
                dve.bn_stats(st1[:, par, :], y1[:, par, :]).then_inc(st1_done, 1)
                wait_apart(dve, st1_done, u + 1, bias_ready)
                dve.bn_aggr(mv1[:, par, :], st1[:, par, :]).then_inc(mv1_done, 1)
                wait(dve, mv1_done, u + 1)
                wait(dve, rstd1_ready, u - 1)
                dve.tensor_scalar(var1[:, par:par + 1], mv1[:, par, 1:2], LN_EPS, None, ALU.add).then_inc(var1_ready, 1)

            def norm2(i):
                wait(dve, rstd2_ready, i - 8)
                wait(dve, xg2_done, i - 12)
                for n in range(NT):
                    dve.tensor_scalar(xn2[:, n, :], y2[:, n, :], mv2[:, n, 0:1], rstd2[:, n:n + 1],
                                      ALU.subtract, ALU.mult).then_inc(norm2_done, 1)

            def step(i):
                for s in range(4):
                    back, n = (1, 2 + s) if s < 2 else (0, s - 2)
                    T = i - 2 + s
                    u_back, u_n = (1, 1 + s) if s < 3 else (0, 0)
                    if s < 2 and active(i, 0):
                        feature_map(i, 2 * s)
                    if active(i, back):
                        weigh(T, n)
                    if active(i, 1):
                        norm1(T - 2, s % 2)
                    if active(i, back):
                        outputs(T, n)
                    if s < 2 and active(i, 0):
                        feature_map(i, 2 * s + 1)
                    u = T - 1
                    if s < 2 and active(i, 3):
                        ffn_residual(i, s, u if active(i, 1) else TILES * L - 1)
                    if active(i, u_back):
                        att_residual(i, u, u_back, u_n, (s + 1) % 2)
                    if s < 2 and active(i, 3):
                        ffn_stats(i, s)
                    if active(i, u_back):
                        att_stats(u, (s + 1) % 2)
                    if s < 2 and active(i, 3):
                        ffn_var(i, s)
                    if s == 2 and active(i, 3):
                        norm2(i)
            steps(dve, step)
            dve_tail(dve, moments, tile_stats, row_norm)


_INS = ['L0_attn_x', 'L0_attn_Wq', 'L0_attn_bq', 'L0_attn_Wk', 'L0_attn_bk', 'L0_attn_Wv', 'L0_attn_bv', 'L0_attn_Wo', 'L0_attn_bo', 'L0_attn_W1', 'L0_attn_b1', 'L0_attn_W2', 'L0_attn_b2', 'L0_attn_g1', 'L0_attn_be1', 'L0_attn_g2', 'L0_attn_be2', 'L0_attn_gf', 'L0_attn_bef', 'L0_ffn_router_w', 'L0_ffn_router_b', 'L0_ffn_w_gate', 'L0_ffn_w_up', 'L0_ffn_w_down', 'L0_ffn_sw_gate', 'L0_ffn_sw_up', 'L0_ffn_sw_down', 'L0_c', 'L0_wmod']
_OUTS = [((8, 512, 128), 'float32')]


def kernel(**inputs):
    import numpy as _np
    import concourse.bacc as _bacc
    from concourse import mybir as _mybir
    from concourse.bass_utils import run_bass_kernel_spmd as _run

    nc = _bacc.Bacc("TRN2", target_bir_lowering=False, num_devices=1)
    arrays, args = {}, []
    for name in _INS:
        a = _np.ascontiguousarray(inputs[name])
        arrays[f"in_{name}_dram"] = a
        args.append(nc.dram_tensor(f"in_{name}_dram", a.shape, _mybir.dt.from_np(a.dtype), kind="ExternalInput").ap())
    for i, (shape, dtype) in enumerate(_OUTS):
        dt = _mybir.dt.from_np(_np.dtype(dtype))
        args.append(nc.dram_tensor(f"out_{i}_dram", shape, dt, kind="ExternalOutput").ap())
    adaln_block_kernel(nc, *args)
    r = _run(nc, [arrays], core_ids=[0])
    got = tuple(r.results[0][f"out_{i}_dram"] for i in range(len(_OUTS)))
    return got[0]
```

```python
import numpy as np

import concourse.bass as bass
from concourse import mybir
from contextlib import ExitStack

F32 = mybir.dt.float32
BF16 = mybir.dt.bfloat16
U32 = mybir.dt.uint32
ALU = mybir.AluOpType
ACT = mybir.ActivationFunctionType
AXX = mybir.AxisListType.X
ds = bass.ds

P = 128
B, S, D = 8, 512, 128
L, H, HD, FF = 4, 16, 8, 512
NT = S // P
TILES = B * NT
EV = HD + 1
CW = EV * D
CB = CW // 3
SW = EV * H
FC = FF // P
STEPS = L * B
LN_EPS, ATT_EPS = 1e-5, 1e-6
NB = 3 * D
BIAS = NB + 2 * D


def bf16_parts(value):
    parts, rest = [], np.float32(value)
    for _ in range(3):
        bits = rest.view(np.uint32)
        part = np.uint32((int(bits) + 0x7FFF + ((int(bits) >> 16) & 1)) & 0xFFFF0000).view(np.float32)
        parts.append(float(part))
        rest = np.float32(rest - part)
    return parts


def wait(engine, sem, value):
    if isinstance(value, int) and value <= 0:
        return
    engine.wait_ge(sem, value)


def wait_apart(engine, sem, value, ready, *more):
    waits = ((sem, value),) + more
    for _, value in waits:
        if not isinstance(value, int):
            engine.compute_val(value)
    engine.wait_ge(ready, 1)
    for sem, value in waits:
        wait(engine, sem, value)


def adaln_block_kernel(nc, x, Wq, bq, Wk, bk, Wv, bv, Wo, bo, W1, b1, W2, b2, g1, be1, g2, be2, gf, bef,
                       router_w, router_b, w_gate, w_up, w_down, sw_gate, sw_up, sw_down, c, wmod, out):
    E = router_w.shape[1]
    F = w_gate.shape[2]
    FA, FB = P, F - P
    HB = P // 2
    assert FB <= HB
    TOK = B * S
    CAP = -(-5 * 2 * TOK // (4 * E))
    CT = CAP // P
    HC = CAP // 2
    assert CAP % (2 * P) in (0, P) and HC <= 512 and CAP % P == 0
    ROWS = E * CAP
    MODS = 6 * D

    x_v = x.rearrange("b (n p) d -> b p n d", p=P)
    out_v = out.rearrange("b (n p) d -> b p n d", p=P)
    mod_dram = nc.dram_tensor("mod_scratch", [B, MODS], F32, kind="Internal").ap()
    xe_dram = nc.dram_tensor("expert_in_scratch", [ROWS + 2 * TOK, D], F32, kind="Internal").ap()
    ye_dram = nc.dram_tensor("expert_out_scratch", [ROWS, D], F32, kind="Internal").ap()
    xe_tiles = xe_dram[0:ROWS, :].rearrange("(e p j) d -> e p (j d)", e=E, p=P)
    ye_tiles = ye_dram.rearrange("(e p j) d -> e p (j d)", e=E, p=P)

    with ExitStack() as ctx:
        def sb(name, shape, dt=F32):
            return ctx.enter_context(nc.sbuf_tensor(name, shape, dt))

        def sem(name):
            return ctx.enter_context(nc.semaphore(name))

        ident = sb("ident", [P, P])
        tri = sb("tri", [P, P])
        tri_before = sb("tri_before", [P, P], BF16)
        ones_bf = sb("ones_bf", [P, P], BF16)
        ones3 = sb("ones3", [3, P], BF16)
        headmask = sb("headmask", [P, EV, H])
        halfneg = sb("halfneg", [P, 4 * B])
        rank16 = sb("rank16", [P, E])
        expert_base = sb("expert_base", [P, E])
        trash = sb("trash", [P, TILES])
        iota_i = sb("iota_i", [P, 64], mybir.dt.int32)
        wqkv = sb("wqkv", [P, L, NB])
        wo = sb("wo", [P, L, D])
        w1 = sb("w1", [P, L, FF])
        w2 = sb("w2", [P, L, FC, D])
        b1c = sb("b1c", [P, L, FC])
        gains = sb("gains", [P, 4, L, D])
        gfb = sb("gfb", [P, 2, D])
        BR = 1 + 5 * L * D // 32
        assert 2 * E == 32
        bias3 = sb("bias3", [3, BR * 32], BF16)
        bias3_l = bias3[:, 32:].rearrange("r (n l d) -> r n l d", n=5, l=L)
        rb3 = bias3[:, 0:E]
        eps3 = sb("eps3", [3, SW], BF16)
        bias_f = sb("bias_f", [BR, 32])
        bias_parts = sb("bias_parts", [BR, 3, 32], BF16)
        cT = sb("cT", [P, B])
        csT = sb("csT", [P, B])
        wmod_s = sb("wmod_s", [P, MODS])
        mod8 = sb("mod8", [B, MODS])
        gsign = sb("gsign", [B, 2, D])
        mod = sb("mod", [P, B, 6, D])
        x0 = sb("x0", [P, TILES, D])
        X = sb("X", [P, TILES, D])
        xs = sb("xs", [P, NT, D])
        x1s = sb("x1s", [P, NT, D])
        w1s = sb("w1s", [P, FF])
        xT = sb("xT", [P, NT, P])
        x1T = sb("x1T", [P, S])
        ex = sb("ex", [P, 2, 2 * D])
        rl = sb("rl", [P, 2, 2 * D])
        qk = sb("qk", [P, NT, 2, D])
        v1 = sb("v1", [P, NT, EV, H])
        kv = sb("kv", [P, NT, CW])
        qT = sb("qT", [P, P])
        kvm = sb("kvm", [P, SW])
        kvt = sb("kvt", [P, SW])
        room = sb("room", [P, 5 * TILES * E])
        prod = sb("prod", [P, CW])
        red = sb("red", [P, SW])
        tot = sb("tot", [P, EV, H])
        rden = sb("rden", [P, H])
        att = sb("att", [P, D])
        attT = sb("attT", [P, P])
        y1 = sb("y1", [P, 2, D])
        st1 = sb("st1", [P, 2, 6])
        mv1 = sb("mv1", [P, 2, 2])
        var1 = sb("var1", [P, 2])
        rstd1 = sb("rstd1", [P, 2])
        shift1 = sb("shift1", [P, 2])
        xn1 = sb("xn1", [P, 2, D])
        xg1 = sb("xg1", [P, D])
        hT = sb("hT", [P, FC, S])
        y2 = sb("y2", [P, NT, D])
        st2 = sb("st2", [P, NT, 6])
        mv2 = sb("mv2", [P, NT, 2])
        var2 = sb("var2", [P, NT])
        rstd2 = sb("rstd2", [P, NT])
        less_mean2 = sb("less_mean2", [P, NT])
        shift2 = sb("shift2", [P, NT])
        xn2 = sb("xn2", [P, NT, D])
        xg2 = sb("xg2", [P, NT, D])

        ps = ctx.enter_context(nc.psum_tensor("ps", [P, 8, 512], F32))
        ps_cum = ps[:, 0:3, 0:CB]
        ps_qkv = ps[:, 3, 0:NB]
        ps_s = ps[:, 4, :]
        ps_h = ps[:, 5, :]
        ps_t = ps[:, 6, :]
        ps_y = ps[:, 7, :]

        x_loaded = sem("x_loaded")
        row0_loaded = sem("row0_loaded")
        mod0_loaded = sem("mod0_loaded")
        c_loaded = sem("c_loaded")
        par_loaded = sem("par_loaded")
        w12_loaded = sem("w12_loaded")
        bias_loaded = sem("bias_loaded")
        b1_loaded = sem("b1_loaded")
        qkv_loaded = sem("qkv_loaded")
        bias_split = sem("bias_split")
        mod_stored = sem("mod_stored")
        mod_loaded = sem("mod_loaded")
        consts_ready = sem("consts_ready")
        const_step = sem("const_step")
        setup_step = sem("setup_step")
        c_silu = sem("c_silu")
        mod_ps = sem("mod_ps")
        mod8_ready = sem("mod8_ready")
        bias_ready = sem("bias_ready")
        x_ready = sem("x_ready")
        names = """xs_load w1_load x1s_load
            xt_ps qkv_ps qt_ps cum_ps inter_ps att_t_ps wo_ps h_ps x1t_ps w2_ps
            xt_sb er_ready v_sb qt_sb att_t_sb gelu_done x1t_sb
            qk_ready p_done kvt_done kvm_ready red_done tot_done rden_done att_ready y1_done st1_done mv1_done
            var1_ready norm1_done y2_done st2_done mv2_done var2_ready norm2_done
            kv_ready rstd1_ready shift1_ready less_mean2_ready shift2_ready xg1_done x1_ready rstd2_ready xg2_done""".split()
        (xs_load, w1_load, x1s_load,
         xt_ps, qkv_ps, qt_ps, cum_ps, inter_ps, att_t_ps, wo_ps, h_ps, x1t_ps, w2_ps,
         xt_sb, er_ready, v_sb, qt_sb, att_t_sb, gelu_done, x1t_sb,
         qk_ready, p_done, kvt_done, kvm_ready, red_done, tot_done, rden_done, att_ready, y1_done, st1_done,
         mv1_done, var1_ready, norm1_done, y2_done, st2_done, mv2_done, var2_ready, norm2_done,
         kv_ready, rstd1_ready, shift1_ready, less_mean2_ready, shift2_ready, xg1_done, x1_ready, rstd2_ready, xg2_done) = [sem(n) for n in names]
        out_stored = sem("out_stored")

        def active(i, back):
            return not isinstance(i, int) or 0 <= i // NT - back < STEPS

        def layer_of(i, back):
            return ((i - NT * back) // NT) // B

        def row_of(i, back):
            return ((i - NT * back) // NT) % B

        def tile_of(i, back, n):
            return row_of(i, back) * NT + n

        def first(i):
            return i // NT * NT

        HEAD = ((0, 1, 2), (3,), (4, 5), (6, 7), (8,), ())
        DRAIN = ((0,), (1,), (2,), (3,))

        def steps(engine, body, head_step, tail_step):
            for j in HEAD[0]:
                head_step(j)
            for k in range(-1, 4):
                body(k * NT)
                for j in HEAD[k + 2]:
                    head_step(j)
            with engine.Fori(4 * NT, (STEPS - 1) * NT, NT) as i:
                body(i)
            for k in range(STEPS - 1, STEPS + 3):
                body(k * NT)
                for j in DRAIN[k - STEPS + 1]:
                    tail_step(j)
            for j in range(DRAIN[-1][-1] + 1, B + 3):
                tail_step(j)


        Hr = x0
        hT_all = kv[:, :, :].rearrange("p n c -> p (n c)")[:, 0:TILES * D]
        f_st, g_st = (sb(f"{n}_st", [P, NT, 6]) for n in "fg")
        f_mean_var, g_mean_var = (sb(f"{n}_mean_var", [P, NT, 2]) for n in "fg")
        f_small, g_small = (sb(f"{n}_small", [P, 4, NT]) for n in "fg")
        z_st = sb("z_st", [P, NT, 6])
        z_mean_var = sb("z_mean_var", [P, NT, 2])
        z_small = sb("z_small", [P, 4, NT])
        z_xn = room[:, 0:S].rearrange("p (n d) -> p n d", n=NT)
        f_xn, g_xn = (room[:, n * S:(n + 1) * S].rearrange("p (n d) -> p n d", n=NT) for n in (1, 2))
        bef_ga = room[:, S:S + B * D].rearrange("p (b d) -> p b d", b=B)
        gh = xs
        rw = sb("rw", [P, E])
        swg = sb("swg", [P, 3 * P])
        swd = sb("swd", [P, 2, D])
        sil_a, sil_b, hid_a, hid_b = (hT[:, j, :] for j in range(FC))
        ysh = sb("ysh", [P, NT, D])
        TE = TILES * E
        lg, pr, oh0, oh1, ra = (room[:, n * TE:(n + 1) * TE].rearrange("p (t e) -> p t e", e=E) for n in range(5))
        oh = (oh0, oh1)
        rb = prod[:, S:S + TE].rearrange("p (t e) -> p t e", e=E)
        selb = sb("selb", [P, TILES, E], BF16)
        rmax = sb("rmax", [P, TILES])
        rsum = sb("rsum", [P, TILES])
        vk = [sb(f"vk{k}", [P, TILES]) for k in range(2)]
        first_at = sb("first_at", [P, TILES])
        keep = [sb(f"keep{k}", [P, TILES]) for k in range(2)]
        slot = [sb(f"slot{k}", [P, TILES]) for k in range(2)]
        tmp32 = sb("tmp32", [P, TILES])
        wgt = sb("wgt", [P, 2, TILES])
        scat_u = sb("scat_u", [P, TILES, 2], U32)
        gath_u = sb("gath_u", [P, TILES, 2], U32)
        idx_s = sb("idx_s", [P, 2, 2 * NT], U32)
        hs2 = sb("hs2", [P, 2, NT, D])
        zrow = room[:, 3 * S:3 * S + CT * D]
        ewg = sb("ewg", [P, 2, 3 * P])
        ewd = sb("ewd", [P, 2, 2, D])
        kv_room = kv[:, :, :].rearrange("p n c -> p (n c)")
        xes = kv_room[:, 0:2 * CAP].rearrange("p (a c) -> p a c", a=2)
        w2_room = w2[:, :, :, :].rearrange("p l c d -> p (l c d)")
        gains_room = gains[:, :, :, :].rearrange("p g l d -> p (g l d)")
        xeT = wqkv[:, :, :].rearrange("p l c -> p (l c)")[:, 0:2 * CAP].rearrange("p (a c) -> p a c", a=2)
        ehid_a = w2_room[:, 0:2 * CAP].rearrange("p (a c) -> p a c", a=2)
        esil_a = w2_room[:, 2 * CAP:2 * CAP + HC]
        esil_b = w2_room[:, 2 * CAP + HC:3 * CAP]
        ehid_b = gains_room[:, 0:2 * CAP].rearrange("p (a c) -> p a c", a=2)
        yes = kv_room[:, 2 * CAP:4 * CAP].rearrange("p (a c) -> p a c", a=2)
        yg = w1[:, :, :].rearrange("p l f -> p (l f)").rearrange("p (a k d) -> p a k d", a=2, k=2 * NT)
        ymix = kv_room[:, 4 * CAP:4 * CAP + S].rearrange("p (n d) -> p n d", n=NT)
        yout = kv_room[:, 4 * CAP + S:4 * CAP + 3 * S].rearrange("p (a n d) -> p a n d", a=2, n=NT)

        tail_names = """z_stats z_mv z_var z_less_mean z_rstd z_shift z_norm z_scaled f_stats f_mv f_var f_less_mean f_rstd f_shift f_norm f_gain x2_ready gf_ga_ready bef_ga_ready
            x0_shifted g_stats g_mv g_var g_less_mean g_rstd g_shift g_norm g_scaled h_ready gh_done xh_ready
            sw_loaded ht_ps ht_sb lg_ps lg_sb shg_ps sil_done
            hid_done shd_ps ysh_done xsh_done lg_shift lg_exp route_step cnt_ready cnt_ps route_ready xe_zeroed zrow_ready
            hs2_load0 hs2_load1 idx_ready scat0 scat1 ew_load0 ew_load1 ewd_load0 ewd_load1 xe_load0 xe_load1 xet_ps xet_sb ga_ps gub_ps
            ua_ps esa_done esb_done eha_done ehb_done ye_ps ye_sb ye_store0 ye_store1 gat0 gat1
            mix1_done mix2_done mixg_done out_ready0 out_ready1 out_store0 out_store1""".split()
        q = {n: sem(n) for n in tail_names}
        hs2_load, ew_load, xe_load = (q["hs2_load0"], q["hs2_load1"]), (q["ew_load0"], q["ew_load1"]), (q["xe_load0"], q["xe_load1"])
        ewd_load = (q["ewd_load0"], q["ewd_load1"])
        scat, gat, ye_store = (q["scat0"], q["scat1"]), (q["gat0"], q["gat1"]), (q["ye_store0"], q["ye_store1"])
        out_ready, out_store = (q["out_ready0"], q["out_ready1"]), (q["out_store0"], q["out_store1"])
        LAST = TILES * (L + 1)
        tile_bank = ps[:, 4:6, :]
        down_bank = ps[:, 6:8, :]

        def rows_of(a, i):
            return a[:, ds(first(i), NT), :]

        def modulation(i, m):
            return mod[:, ds(i // NT, 1), m, :].to_broadcast([P, NT, D])

        def flat(a):
            return a.rearrange("p n d -> p (n d)")

        def even(r):
            return r // 2 * 2

        def rows(engine, body, step=NT, end=TILES):
            body(0)
            with engine.Fori(step, end, step) as i:
                body(i)

        def experts(engine, body):
            body(0, 0)
            with engine.Fori(1, E - 1, 2) as r:
                e = even(r - 1) + 1
                body(e, 1)
                body(e + 1, 0)
            body(E - 1, 1)

        def sp_tail(sp):
            sp.wait_ge(q["h_ready"], B)
            for b in range(2):
                sp.dma_start(hs2[:, b, :, :], Hr[:, b * NT:(b + 1) * NT, :]).then_inc(hs2_load[b], 16)
            with sp.Fori(2, B, 2) as r:
                b = even(r - 2) + 2
                for par in range(2):
                    sp.wait_ge(scat[par], b * 64)
                    sp.dma_start(hs2[:, par, :, :], Hr[:, ds((b + par) * NT, NT), :]).then_inc(hs2_load[par], 16)

            def expert_weights(e, par):
                wait(sp, q["ua_ps"], B + 2 * e - 2 if not isinstance(e, int) or e > 1 else 0)
                gate, up = (w[ds(e, 1)].rearrange("a k f -> (a k) f") for w in (w_gate, w_up))
                sp.dma_start(ewg[:, par, 0:F], gate).then_inc(ew_load[par], 16)
                sp.dma_start(ewg[:, par, 2 * P:], up[:, 0:FA]).then_inc(ew_load[par], 16)
                sp.dma_start(ewg[:, par, P + HB:P + HB + FB], up[:, FA:F]).then_inc(ew_load[par], 16)
                wait(sp, q["ye_ps"], e - 1)
                sp.dma_start(ewd[:, par, 0, :], w_down[ds(e, 1), 0:FA, :].rearrange("a k f -> (a k) f")).then_inc(ewd_load[par], 16)
                sp.dma_start(ewd[0:FB, par, 1, :], w_down[ds(e, 1), FA:F, :].rearrange("a k f -> (a k) f")).then_inc(ewd_load[par], 16)

            def expert_rows(e, par):
                wait(sp, q["xet_ps"], e - 1)
                sp.dma_start(xes[:, par, :], xe_tiles[ds(e, 1)].rearrange("a p c -> (a p) c")).then_inc(xe_load[par], 16)

            for e in range(2):
                expert_weights(e, e)
            for par in range(2):
                sp.wait_ge(scat[par], B * 64)
            sp.wait_ge(q["ua_ps"], B)
            for e in range(2):
                expert_rows(e, e)
            with sp.Fori(2, E, 2) as r:
                e = even(r - 2) + 2
                for par in range(2):
                    expert_rows(e + par, par)
                    expert_weights(e + par, par)

            def rows_1(r):
                b = even(r)
                for par in range(2):
                    sp.wait_ge(out_ready[par], b // 2 + 1)
                    sp.dma_start(out_v[ds(b + par, 1)].rearrange("a p n d -> (a p) n d"), yout[:, par, :, :]
                                 ).then_inc(out_store[par], 16)
            rows(sp, rows_1, 2, B)
            for par in range(2):
                sp.wait_ge(out_store[par], 16 * (B // 2))
                sp.wait_ge(ye_store[par], 16 * (E // 2))
            sp.wait_ge(q["xe_zeroed"], 16 * E)
            sp.wait_ge(mod_stored, 16)

        def tile_rows(b):
            return slice(b * NT, (b + 1) * NT)

        def wide(a):
            return a.to_broadcast([P, NT, D])

        def dve_statistics(dve, b, name, source, st):
            wait(dve, q[name + "_mv"], b * NT)
            for n in range(NT):
                dve.bn_stats(st[:, n, :], source[:, b * NT + n, :]).then_inc(q[name + "_stats"], 1)

        def dve_moments(dve, b, name, st, mean_var):
            dve.wait_ge(q[name + "_stats"], (b + 1) * NT)
            wait(dve, q[name + "_norm"], b)
            for n in range(NT):
                dve.bn_aggr(mean_var[:, n, :], st[:, n, :]).then_inc(q[name + "_mv"], 1)

        def pool_root_and_shift(pool, b, name, mean_var, small):
            pool.wait_ge(q[name + "_mv"], (b + 1) * NT)
            wait(pool, q[name + "_norm"], b)
            pool.tensor_scalar(small[:, 0, :], mean_var[:, :, 1], LN_EPS, None, ALU.add).then_inc(q[name + "_var"], 1)
            pool.tensor_scalar(small[:, 1, :], mean_var[:, :, 0], -1.0, None, ALU.mult).then_inc(q[name + "_less_mean"], 1)
            pool.wait_ge(q[name + "_var"], b + 1)
            pool.tensor_tensor(small[:, 2, :], small[:, 0, :], halfneg[:, 0:NT], ALU.pow).then_inc(q[name + "_rstd"], 1)
            pool.wait_ge(q[name + "_rstd"], b + 1)
            pool.wait_ge(q[name + "_less_mean"], b + 1)
            pool.tensor_tensor(small[:, 3, :], small[:, 1, :], small[:, 2, :], ALU.mult).then_inc(q[name + "_shift"], 1)

        def act_normalise(act, b, name, source, small, xn, used):
            act.wait_ge(q[name + "_shift"], b + 1)
            wait(act, q[used], b)
            for n in range(NT):
                ins = act.activation(xn[:, n, :], source[:, b * NT + n, :], ACT.Identity, bias=small[:, 3, n:n + 1],
                                     scale=small[:, 2, n:n + 1])
            ins.then_inc(q[name + "_norm"], 1)

        def dve_head_step(dve, j):
            if j > 0:
                b = j - 1
                dve.wait_ge(q["z_norm"], b + 1)
                dve.wait_ge(mod_loaded if b else mod0_loaded, 16 * (B - 1) if b else 16)
                dve.tensor_tensor(X[:, tile_rows(b), :], z_xn[:, :, :], wide(mod[:, b:b + 1, 1, :]), ALU.mult).then_inc(q["z_scaled"], 1)
            if j < B:
                dve.wait_ge(x_loaded if j else row0_loaded, 16 * (B - 1) if j else 16)
                dve_statistics(dve, j, "z", x0, z_st)
            if j > 0:
                dve.wait_ge(q["z_scaled"], j)
                dve.tensor_tensor(X[:, tile_rows(j - 1), :], X[:, tile_rows(j - 1), :], wide(mod[:, j - 1:j, 0, :]), ALU.add
                                  ).then_inc(x_ready, NT)
            if j < B:
                dve_moments(dve, j, "z", z_st, z_mean_var)

        def pool_head_step(pool, j):
            if j < B:
                pool_root_and_shift(pool, j, "z", z_mean_var, z_small)

        def act_head_step(act, j):
            if j < B:
                act_normalise(act, j, "z", x0, z_small, z_xn, "z_scaled")

        def dve_tail_step(dve, j):
            if 0 <= j - 1 < B:
                b = j - 1
                dve.wait_ge(q["f_norm"], b + 1)
                dve.wait_ge(q["gf_ga_ready"], 1)
                dve.tensor_tensor(X[:, tile_rows(b), :], f_xn[:, :, :], wide(mod[:, b:b + 1, 2, :]), ALU.mult).then_inc(q["f_gain"], 1)
            if j < B:
                dve.wait_ge(x_ready, LAST - TILES + (j + 1) * NT)
                dve_statistics(dve, j, "f", X, f_st)
            if 0 <= j - 1 < B:
                b = j - 1
                dve.wait_ge(q["x0_shifted"], b + 1)
                dve.wait_ge(q["f_gain"], b + 1)
                dve.tensor_tensor(X[:, tile_rows(b), :], X[:, tile_rows(b), :], x0[:, tile_rows(b), :], ALU.add).then_inc(q["x2_ready"], 1)
            if j < B:
                dve_moments(dve, j, "f", f_st, f_mean_var)
            if 0 <= j - 2 < B:
                b = j - 2
                dve.wait_ge(q["g_norm"], b + 1)
                dve.tensor_tensor(Hr[:, tile_rows(b), :], g_xn[:, :, :], wide(mod[:, b:b + 1, 4, :]), ALU.mult).then_inc(q["g_scaled"], 1)
            if 0 <= j - 1 < B:
                b = j - 1
                dve.wait_ge(q["x2_ready"], b + 1)
                dve_statistics(dve, b, "g", X, g_st)
            if 0 <= j - 2 < B:
                b = j - 2
                dve.wait_ge(q["g_scaled"], b + 1)
                dve.tensor_tensor(Hr[:, tile_rows(b), :], Hr[:, tile_rows(b), :], wide(mod[:, b:b + 1, 3, :]), ALU.add).then_inc(q["h_ready"], 1)
            if 0 <= j - 1 < B:
                dve_moments(dve, j - 1, "g", g_st, g_mean_var)

        def pool_tail_step(pool, j):
            if j < B:
                pool_root_and_shift(pool, j, "f", f_mean_var, f_small)
            if 0 <= j - 1 < B:
                pool_root_and_shift(pool, j - 1, "g", g_mean_var, g_small)

        def shift_input(pool, k):
            if k == 1:
                pool.wait_ge(mod0_loaded, 16)
                pool.wait_ge(mod_loaded, 16 * (B - 1))
                pool.tensor_tensor(bef_ga[:, :, :], mod[:, :, 2, :], gfb[:, 1:2, :].to_broadcast([P, B, D]), ALU.mult
                                   ).then_inc(q["bef_ga_ready"], 1)
                pool.wait_ge(q["bef_ga_ready"], 1)
                pool.tensor_tensor(mod[:, :, 2, :], mod[:, :, 2, :], gfb[:, 0:1, :].to_broadcast([P, B, D]), ALU.mult
                                   ).then_inc(q["gf_ga_ready"], 1)
                return
            for b in range((k - 2) * (B // 2), (k - 1) * (B // 2)):
                pool.wait_ge(q["z_norm"], b + 1)
                pool.tensor_tensor(x0[:, tile_rows(b), :], x0[:, tile_rows(b), :], wide(bef_ga[:, b:b + 1, :]), ALU.add).then_inc(q["x0_shifted"], 1)

        def act_tail_step(act, j):
            if j < B:
                act_normalise(act, j, "f", X, f_small, f_xn, "f_gain")
            if 0 <= j - 1 < B:
                act_normalise(act, j - 1, "g", X, g_small, g_xn, "g_scaled")
            b = j - 3
            if 0 <= b < B:
                act.wait_ge(q["ht_ps"], b + 1)
                act.activation(hT_all[:, b * S:(b + 1) * S], ps[:, 3, :], ACT.Copy).then_inc(q["ht_sb"], 1)
                act.wait_ge(q["lg_ps"], b + 1)
                act.activation(lg[:, tile_rows(b), :].rearrange("p t e -> p (t e)"), ps[:, 0, 0:NT * E], ACT.Copy).then_inc(q["lg_sb"], 1)

        def pe_tail_step(pe, j):
            b = j - 3
            if not 0 <= b < B:
                return
            if b == 0:
                pe.wait_ge(q["sw_loaded"], 16 * 6)
                pe.wait_ge(v_sb, TILES * L)
                pe.wait_ge(p_done, TILES * L)
            pe.wait_ge(q["h_ready"], b + 1)
            wait(pe, q["ht_sb"], b)
            for n in range(NT):
                mm = pe.transpose(ps[:, 3, n * P:(n + 1) * P], Hr[:, b * NT + n, :], ident[:, :])
            mm.then_inc(q["ht_ps"], 1)
            pe.wait_ge(q["ht_sb"], b + 1)
            wait(pe, q["lg_sb"], b)
            for n in range(NT):
                o = ps[:, 0, n * E:(n + 1) * E]
                pe.matmul(o, ones3[:, :], rb3, start=True, stop=False)
                mm = pe.matmul(o, hT_all[:, (b * NT + n) * P:(b * NT + n + 1) * P], rw[:, :], start=False, stop=True)
            mm.then_inc(q["lg_ps"], 1)

        def pool_tail(pool):
            pool.wait_ge(xt_ps, TILES * L)
            pool.wait_ge(q["g_norm"], B)

            def add_h(i):
                wait_apart(pool, q["h_ready"], i // NT + 1, consts_ready, (q["xh_ready"], i // NT))
                pool.tensor_tensor(gh[:, :, :], rows_of(Hr, i), modulation(i, 5), ALU.mult).then_inc(q["gh_done"], 1)
                wait_apart(pool, q["gh_done"], i // NT + 1, consts_ready)
                pool.tensor_tensor(rows_of(X, i), rows_of(X, i), gh[:, :, :], ALU.add).then_inc(q["xh_ready"], 1)
            rows(pool, add_h)
            pool.wait_ge(q["route_ready"], 2)
            pool.wait_ge(q["xe_zeroed"], 16 * E)

            def indices(source, b, par, count):
                pool.tensor_copy(idx_s[:, par, :].rearrange("p (t k) -> p t k", k=2),
                                 source[:, ds(b * NT, NT), :]).then_inc(q["idx_ready"], 1)
                wait_apart(pool, q["idx_ready"], count, consts_ready)

            def rows_4(r):
                b = even(r)
                for par in range(2):
                    pool.wait_ge(hs2_load[par], b * 8 + 16)
                    wait(pool, scat[par], b * 64)
                    indices(scat_u, b + par, par, b + par + 1)
                    for n in range(NT):
                        for k in range(2):
                            pool.indirect_dma_start(
                                out=xe_dram, out_offset=bass.IndirectOffsetOnAxis(ap=idx_s[:, par, 2 * n + k:2 * n + k + 1], axis=0),
                                in_=hs2[:, par, n, :], in_offset=None).then_inc(scat[par], 16)
            rows(pool, rows_4, 2, B)
            for par in range(2):
                pool.wait_ge(scat[par], 64 * B)
                pool.wait_ge(ye_store[par], 16 * (E // 2))
            def rows_5(r):
                b = even(r)
                for par in range(2):
                    wait(pool, gat[par], b * 64)
                    wait(pool, out_ready[par], b // 2)
                    indices(gath_u, b + par, par, B + b + par + 1)
                    for n in range(NT):
                        for k in range(2):
                            pool.indirect_dma_start(
                                out=yg[:, par, 2 * n + k, :], out_offset=None, in_=ye_dram,
                                in_offset=bass.IndirectOffsetOnAxis(ap=idx_s[:, par, 2 * n + k:2 * n + k + 1], axis=0)
                            ).then_inc(gat[par], 16)
            rows(pool, rows_5, 2, B)

        def pe_tail(pe):
            pe.wait_ge(y1_done, TILES * L)
            pe.wait_ge(y2_done, TILES * L)
            pe.wait_ge(q["lg_sb"], B)
            pe.wait_ge(q["ht_sb"], B)

            def gate_up(rhs, weights, columns, use):
                for bank, lhs, before, after in ((0, weights[:, 0:P], (("esa_done", use),), "ga_ps"),
                                                 (1, weights[:, P:2 * P], (("ehb_done", use),), "gub_ps"),
                                                 (2, weights[:, 2 * P:], (("eha_done", use),), "ua_ps")):
                    for name, count in before:
                        wait_apart(pe, q[name], count, consts_ready)
                    pe.matmul(ps[:, bank, 0:columns], lhs, rhs, start=True, stop=True).then_inc(q[after], 1)

            def shared(i):
                gate_up(hT_all[:, ds(first(i) * P, S)], swg, S, i // NT)

            def shared_down(i):
                pe.wait_ge(q["eha_done"], i // NT + 1)
                pe.wait_ge(q["ehb_done"], i // NT + 1)
                wait(pe, q["ysh_done"], i)
                for n in range(NT):
                    o = ps[:, 5, n * P:(n + 1) * P]
                    pe.matmul(o, hid_a[:, n * P:(n + 1) * P], swd[:, 0, :], start=True, stop=False)
                    mm = pe.matmul(o, hid_b[0:FB, n * P:(n + 1) * P], swd[0:FB, 1, :], start=False, stop=True)
                mm.then_inc(q["shd_ps"], 4)

            pe.wait_ge(q["cnt_ready"], 1)
            pe.matmul(ps[:, 6, :], tri_before[:, :], selb[:, :, :].rearrange("p t e -> p (t e)"), start=True, stop=True)
            pe.matmul(ps[:, 7, :], ones_bf[:, :], selb[:, :, :].rearrange("p t e -> p (t e)"), start=True, stop=True
                      ).then_inc(q["cnt_ps"], 1)
            def rows_7(i):
                shared(i)
                shared_down(i)
            rows(pe, rows_7)

            def transposes(e, par):
                pe.wait_ge(xe_load[par], ((e - par) // 2 + 1) * 16)
                wait(pe, q["xet_sb"], e)
                for j in range(CT):
                    mm = pe.transpose(tile_bank[:, j // 4, (j % 4) * P:(j % 4 + 1) * P], xes[:, par, j * P:(j + 1) * P], ident[:, :])
                mm.then_inc(q["xet_ps"], 1)

            def hidden(e, par, half):
                if half == 0:
                    pe.wait_ge(q["xet_sb"], e + 1)
                    pe.wait_ge(ew_load[par], ((e - par) // 2 + 1) * 16 * 3)
                gate_up(xeT[:, par, half * HC:(half + 1) * HC], ewg[:, par], HC, B + 2 * e + half)

            def down(e, par):
                pe.wait_ge(q["eha_done"], B + 2 * e + 2)
                pe.wait_ge(q["ehb_done"], B + 2 * e + 2)
                pe.wait_ge(ewd_load[par], ((e - par) // 2 + 1) * 16 * 2)
                wait(pe, q["ye_sb"], e)
                for j in range(CT):
                    o = down_bank[:, j // 4, (j % 4) * P:(j % 4 + 1) * P]
                    pe.matmul(o, ehid_a[:, par, j * P:(j + 1) * P], ewd[:, par, 0, :], start=True, stop=False)
                    mm = pe.matmul(o, ehid_b[0:FB, par, j * P:(j + 1) * P], ewd[0:FB, par, 1, :], start=False, stop=True)
                mm.then_inc(q["ye_ps"], 1)

            pe.wait_ge(q["ysh_done"], TILES)
            transposes(0, 0)

            def expert(e, par):
                hidden(e, par, 0)
                if not isinstance(e, int) or e > 0:
                    down(e - 1, 1 - par)
                if not isinstance(e, int) or e < E - 1:
                    transposes(e + 1, 1 - par)
                hidden(e, par, 1)
            experts(pe, expert)
            down(E - 1, 1)

        def act_tail(act):
            act.wait_ge(q["lg_shift"], 1)
            act.activation(pr[:, :, :], ra[:, :, :], ACT.Exp).then_inc(q["lg_exp"], 1)
            def rows_9(r):
                act.wait_ge(q["ga_ps"], r + 1)
                wait(act, q["eha_done"], r)
                act.activation(sil_a[:, :], ps[:, 0, :], ACT.Silu).then_inc(q["esa_done"], 1)
                act.wait_ge(q["gub_ps"], r + 1)
                wait(act, q["ehb_done"], r)
                act.activation(sil_b[0:FB, :], ps[0:FB, 1, :], ACT.Silu).then_inc(q["esb_done"], 1)
            rows(act, rows_9, 1, B)

            def turned(e, par):
                act.wait_ge(q["xet_ps"], e + 1)
                wait(act, q["ua_ps"], B + 2 * e - 2)
                act.activation(xeT[:, par, 0:4 * P], tile_bank[:, 0, :], ACT.Copy)
                act.activation(xeT[:, par, 4 * P:CAP], tile_bank[:, 1, 0:CAP - 4 * P], ACT.Copy).then_inc(q["xet_sb"], 1)

            def gates(e, half):
                use = B + 2 * e + half
                act.wait_ge(q["ga_ps"], use + 1)
                wait(act, q["eha_done"], use)
                act.activation(esil_a[:, :], ps[:, 0, 0:HC], ACT.Silu).then_inc(q["esa_done"], 1)
                act.wait_ge(q["gub_ps"], use + 1)
                wait(act, q["ehb_done"], use)
                act.activation(esil_b[0:FB, :], ps[0:FB, 1, 0:HC], ACT.Silu).then_inc(q["esb_done"], 1)

            def finish(e, par):
                act.wait_ge(q["ye_ps"], e + 1)
                wait(act, ye_store[par], ((e - par) // 2) * 16)
                act.activation(yes[:, par, 0:4 * P], down_bank[:, 0, :], ACT.Copy)
                act.activation(yes[:, par, 4 * P:CAP], down_bank[:, 1, 0:CAP - 4 * P], ACT.Copy).then_inc(q["ye_sb"], 1)
                act.wait_ge(q["ye_sb"], e + 1)
                act.dma_start(ye_tiles[ds(e, 1)].rearrange("a p c -> (a p) c"), yes[:, par, :]).then_inc(ye_store[par], 16)

            turned(0, 0)

            def expert(e, par):
                gates(e, 0)
                if not isinstance(e, int) or e > 0:
                    finish(e - 1, 1 - par)
                if not isinstance(e, int) or e < E - 1:
                    turned(e + 1, 1 - par)
                gates(e, 1)
            experts(act, expert)
            finish(E - 1, 1)

        def dve_tail(dve):
            done = [0]

            def then(ins):
                done[0] += 1
                ins.then_inc(q["route_step"], 1)
                dve.wait_ge(q["route_step"], done[0])

            def over_experts(a):
                return a.unsqueeze(2).to_broadcast([P, TILES, E])

            def over_tiles(a):
                return a[:, :].unsqueeze(1).to_broadcast([P, TILES, E])

            dve.wait_ge(q["lg_sb"], B)
            then(dve.tensor_reduce(rmax[:, :], lg[:, :, :], AXX, ALU.max))
            dve.tensor_tensor(ra[:, :, :], lg[:, :, :], over_experts(rmax[:, :]), ALU.subtract).then_inc(q["lg_shift"], 1)
            dve.wait_ge(q["lg_exp"], 1)
            then(dve.tensor_reduce(rsum[:, :], pr[:, :, :], AXX, ALU.add))
            then(dve.reciprocal(rsum[:, :], rsum[:, :]))
            then(dve.tensor_tensor(pr[:, :, :], pr[:, :, :], over_experts(rsum[:, :]), ALU.mult))
            for k in range(2):
                then(dve.tensor_reduce(vk[k][:, :], pr[:, :, :], AXX, ALU.max))
                then(dve.tensor_tensor(ra[:, :, :], pr[:, :, :], over_experts(vk[k][:, :]), ALU.is_ge))
                then(dve.tensor_tensor(ra[:, :, :], ra[:, :, :], over_tiles(rank16), ALU.mult))
                then(dve.tensor_reduce(first_at[:, :], ra[:, :, :], AXX, ALU.max))
                then(dve.tensor_tensor(oh[k][:, :, :], ra[:, :, :], over_experts(first_at[:, :]), ALU.is_equal))
                if k == 0:
                    then(dve.scalar_tensor_tensor(out=pr[:, :, :], in0=oh[0][:, :, :], scalar=-2.0, in1=pr[:, :, :],
                                                  op0=ALU.mult, op1=ALU.add))
            dve.tensor_tensor(selb[:, :, :], oh[0][:, :, :], oh[1][:, :, :], ALU.add).then_inc(q["cnt_ready"], 1)
            dve.wait_ge(q["cnt_ps"], 1)
            within = ps[:, 6, :].rearrange("p (t e) -> p t e", e=E)
            totals = ps[:, 7, :].rearrange("p (t e) -> p t e", e=E)
            then(dve.tensor_copy(ra[:, :, :], totals))
            a, b = ra, rb
            shift = 1
            while shift < TILES:
                dve.tensor_copy(b[:, 0:shift, :], a[:, 0:shift, :])
                then(dve.tensor_tensor(b[:, shift:, :], a[:, shift:, :], a[:, 0:TILES - shift, :], ALU.add))
                a, b = b, a
                shift *= 2
            then(dve.tensor_tensor(a[:, :, :], a[:, :, :], totals, ALU.subtract))
            then(dve.tensor_tensor(a[:, :, :], a[:, :, :], within, ALU.add))
            then(dve.tensor_scalar(pr[:, :, :], a[:, :, :], float(CAP), None, ALU.is_lt))
            then(dve.tensor_scalar(a[:, :, :], a[:, :, :], float(CAP - 1), None, ALU.min))
            then(dve.tensor_tensor(a[:, :, :], a[:, :, :], over_tiles(expert_base), ALU.add))
            then(dve.tensor_tensor(rsum[:, :], vk[0][:, :], vk[1][:, :], ALU.add))
            then(dve.tensor_scalar(rsum[:, :], rsum[:, :], 1e-9, None, ALU.add))
            then(dve.reciprocal(rsum[:, :], rsum[:, :]))
            for k in range(2):
                then(dve.tensor_tensor(b[:, :, :], oh[k][:, :, :], pr[:, :, :], ALU.mult))
                then(dve.tensor_reduce(keep[k][:, :], b[:, :, :], AXX, ALU.add))
                then(dve.tensor_tensor(b[:, :, :], oh[k][:, :, :], a[:, :, :], ALU.mult))
                then(dve.tensor_reduce(slot[k][:, :], b[:, :, :], AXX, ALU.add))
                then(dve.tensor_tensor(tmp32[:, :], vk[k][:, :], rsum[:, :], ALU.mult))
                dve.tensor_tensor(wgt[:, k, :], tmp32[:, :], keep[k][:, :], ALU.mult).then_inc(q["route_step"], 1)
                done[0] += 1
                dve.wait_ge(q["route_step"], done[0])
                then(dve.tensor_copy(gath_u[:, :, k], slot[k][:, :]))
                then(dve.scalar_tensor_tensor(out=tmp32[:, :], in0=trash[:, :], scalar=float(k * TOK), in1=slot[k][:, :],
                                              op0=ALU.add, op1=ALU.subtract))
                then(dve.tensor_tensor(tmp32[:, :], tmp32[:, :], keep[k][:, :], ALU.mult))
                then(dve.tensor_scalar(first_at[:, :], trash[:, :], float(k * TOK), None, ALU.add))
                then(dve.tensor_tensor(tmp32[:, :], first_at[:, :], tmp32[:, :], ALU.subtract))
                dve.tensor_copy(scat_u[:, :, k], tmp32[:, :]).then_inc(q["route_ready"], 1)
                dve.wait_ge(q["route_ready"], k + 1)

            dve.wait_ge(q["xh_ready"], B)
            def rows_14(i):
                r = i // NT
                dve.wait_ge(q["esa_done"], r + 1)
                dve.wait_ge(q["ua_ps"], r + 1)
                wait(dve, q["shd_ps"], i)
                dve.tensor_tensor(hid_a[:, :], sil_a[:, :], ps[:, 2, :], ALU.mult).then_inc(q["eha_done"], 1)
                dve.wait_ge(q["esb_done"], r + 1)
                dve.wait_ge(q["gub_ps"], r + 1)
                dve.tensor_tensor(hid_b[0:FB, :], sil_b[0:FB, :], ps[HB:HB + FB, 1, :], ALU.mult).then_inc(q["ehb_done"], 1)
                dve.wait_ge(q["shd_ps"], i + 4)
                dve.tensor_tensor(ysh[:, :, :], ps[:, 5, :].rearrange("p (n d) -> p n d", d=D), modulation(i, 5), ALU.mult
                                  ).then_inc(q["ysh_done"], 4)
                dve.wait_ge(q["ysh_done"], i + 4)
                dve.tensor_tensor(rows_of(X, i), rows_of(X, i), ysh[:, :, :], ALU.add).then_inc(q["xsh_done"], 4)
            rows(dve, rows_14)

            def expert(e, par):
                for half in range(2):
                    use = B + 2 * e + half
                    part = slice(half * HC, (half + 1) * HC)
                    dve.wait_ge(q["esa_done"], use + 1)
                    dve.wait_ge(q["ua_ps"], use + 1)
                    wait(dve, q["ye_ps"], e - 1)
                    dve.tensor_tensor(ehid_a[:, par, part], esil_a[:, :], ps[:, 2, 0:HC], ALU.mult).then_inc(q["eha_done"], 1)
                    dve.wait_ge(q["esb_done"], use + 1)
                    dve.wait_ge(q["gub_ps"], use + 1)
                    dve.tensor_tensor(ehid_b[0:FB, par, part], esil_b[0:FB, :], ps[HB:HB + FB, 1, 0:HC], ALU.mult).then_inc(q["ehb_done"], 1)
            experts(dve, expert)

            dve.wait_ge(q["xsh_done"], TILES)
            def rows_15(r):
                b = even(r)
                for par in range(2):
                    base = (b + par) * NT
                    dve.wait_ge(gat[par], b * 64 + 128)
                    wait(dve, q["mixg_done"], b + par)
                    for n in range(NT):
                        dve.tensor_scalar(ymix[:, n, :], yg[:, par, 2 * n, :], wgt[:, 0, ds(base + n, 1)], None, ALU.mult
                                          ).then_inc(q["mix1_done"], 1)
                    for n in range(NT):
                        dve.wait_ge(q["mix1_done"], b * 4 + par * 4 + n + 1)
                        dve.scalar_tensor_tensor(out=ymix[:, n, :], in0=yg[:, par, 2 * n + 1, :], scalar=wgt[:, 1, ds(base + n, 1)],
                                                 in1=ymix[:, n, :], op0=ALU.mult, op1=ALU.add).then_inc(q["mix2_done"], 1)
                    dve.wait_ge(q["mix2_done"], b * 4 + par * 4 + 4)
                    wait(dve, out_store[par], b * 8)
                    dve.tensor_tensor(yout[:, par, :, :], ymix[:, :, :], mod[:, ds(b + par, 1), 5, :].to_broadcast([P, NT, D]), ALU.mult
                                      ).then_inc(q["mixg_done"], 1)
                    dve.wait_ge(q["mixg_done"], b + par + 1)
                    dve.tensor_tensor(yout[:, par, :, :], yout[:, par, :, :], X[:, ds(base, NT), :], ALU.add).then_inc(out_ready[par], 1)
            rows(dve, rows_15, 2, B)

        block = ctx.enter_context(nc.Block())

        @block.sync
        def _(sp):
            sp.dma_start(cT[:, :], c.rearrange("b d -> d b"), allow_slow_non_contiguous=True).then_inc(c_loaded, 16)
            sp.dma_start(wmod_s[:, :], wmod).then_inc(c_loaded, 16)
            sp.dma_start(x0[:, 0:NT, :], x_v[0]).then_inc(row0_loaded, 16)
            for n, w in enumerate((Wq, Wk, Wv)):
                sp.dma_start(wqkv[:, :, n * D:(n + 1) * D], w.rearrange("l k n -> k l n")).then_inc(qkv_loaded, 16)
            for b in range(1, B):
                sp.dma_start(x0[:, b * NT:(b + 1) * NT, :], x_v[b]).then_inc(x_loaded, 16)
            sp.wait_ge(mod8_ready, 1)
            sp.dma_start(mod_dram, mod8[:, :]).then_inc(mod_stored, 16)
            sp.wait_ge(mod_stored, 16)
            sp.dma_start(mod[:, 0, :, :].rearrange("p m d -> p (m d)"), mod_dram[0:1, :].to_broadcast([P, MODS])
                         ).then_inc(mod0_loaded, 16)
            sp.wait_ge(bias_split, 3)
            for r in range(3):
                sp.dma_start(bias3[r:r + 1, :], bias_parts[:, r, :]).then_inc(bias_ready, 16)
            for b in range(1, B):
                sp.dma_start(mod[:, b, :, :].rearrange("p m d -> p (m d)"), mod_dram[b:b + 1, :].to_broadcast([P, MODS])
                             ).then_inc(mod_loaded, 16)

            def first_loads(k):
                if k == -1:
                    sp.dma_start(wo[:, :, :], Wo.rearrange("l k n -> k l n")).then_inc(par_loaded, 16)
                    for n, g in enumerate((g1, be1, g2, be2)):
                        sp.dma_start(gains[:, n, :, :].rearrange("p l d -> p (l d)"),
                                     g.rearrange("(a l) d -> a (l d)", a=1).to_broadcast([P, L * D])).then_inc(par_loaded, 16)
                    for n, g in enumerate((gf, bef)):
                        sp.dma_start(gfb[:, n, :], g.rearrange("(a d) -> a d", a=1).to_broadcast([P, D])).then_inc(par_loaded, 16)
                if k == 0:
                    sp.dma_start(w1[:, :, :], W1.rearrange("l k n -> k l n")).then_inc(w12_loaded, 16)
                    sp.dma_start(w2[:, :, :, :].rearrange("p l c n -> p (l c) n"),
                                 W2.rearrange("l (c p) n -> p (l c) n", p=P)).then_inc(w12_loaded, 16)
                    sp.dma_start(rw[:, :], router_w).then_inc(q["sw_loaded"], 16)
                    sp.dma_start(swg[:, 0:F], sw_gate).then_inc(q["sw_loaded"], 16)
                    sp.dma_start(swg[:, 2 * P:], sw_up[:, 0:FA]).then_inc(q["sw_loaded"], 16)
                    sp.dma_start(swg[:, P + HB:P + HB + FB], sw_up[:, FA:F]).then_inc(q["sw_loaded"], 16)
                    sp.dma_start(swd[:, 0, :], sw_down[0:FA, :]).then_inc(q["sw_loaded"], 16)
                    sp.dma_start(swd[0:FB, 1, :], sw_down[FA:F, :]).then_inc(q["sw_loaded"], 16)
                if k >= 0:
                    sp.wait_ge(q["zrow_ready"], 1)
                    for e in range(k * E // NT, (k + 1) * E // NT):
                        sp.dma_start(xe_tiles[e], zrow[:, :]).then_inc(q["xe_zeroed"], 16)

            def step(i):
                if active(i, -1):
                    wait_apart(sp, x_ready, i + 8, mod_stored)
                    wait(sp, xt_ps, i + 4)
                    row = tile_of(i, -1, 0)
                    sp.dma_start(xs[:, :, :], X[:, ds(row, NT), :]).then_inc(xs_load, 16)
                if isinstance(i, int) and i < NT * NT:
                    first_loads(i // NT)
                if active(i, 2):
                    wait_apart(sp, x1_ready, i - 4, mod_stored)
                    wait(sp, x1t_ps, i - 8)
                    row = tile_of(i, 2, 0)
                    sp.dma_start(x1s[:, :, :], X[:, ds(row, NT), :]).then_inc(x1s_load, 16)
                    wait(sp, h_ps, i - 8)
                    if isinstance(i, int) and i == 2 * NT:
                        sp.wait_ge(w12_loaded, 16 * 2)
                    sp.dma_start(w1s[:, :], w1[:, ds(layer_of(i, 2), 1), :].rearrange("p a f -> p (a f)")
                                 ).then_inc(w1_load, 16)
            steps(sp, step, lambda j: None, lambda j: None)
            sp_tail(sp)

        @block.gpsimd
        def _(pool):
            done = [0]

            def then(ins):
                done[0] += 1
                ins.then_inc(const_step, 1)
                pool.wait_ge(const_step, done[0])

            then(pool.memset(ident[:, :], 0.0))
            pool.affine_select(out=ident[:, :], in_=ident[:, :], compare_op=ALU.not_equal, fill=1.0, base=0,
                               pattern=[[-1, P]], channel_multiplier=1).then_inc(consts_ready, 1)
            then(pool.memset(tri[:, :], 1.0))
            pool.affine_select(out=tri[:, :], in_=tri[:, :], compare_op=ALU.is_ge, fill=0.0, base=0,
                               pattern=[[1, P]], channel_multiplier=-1).then_inc(consts_ready, 1)
            then(pool.memset(tri_before[:, :], 1.0))
            pool.affine_select(out=tri_before[:, :], in_=tri_before[:, :], compare_op=ALU.is_gt, fill=0.0, base=0,
                               pattern=[[1, P]], channel_multiplier=-1).then_inc(consts_ready, 1)
            then(pool.memset(headmask[:, :, :], 1.0))
            then(pool.affine_select(out=headmask[:, :, :], in_=headmask[:, :, :], compare_op=ALU.is_ge, fill=0.0,
                                    base=0, pattern=[[0, EV], [-HD, H]], channel_multiplier=1))
            pool.affine_select(out=headmask[:, :, :], in_=headmask[:, :, :], compare_op=ALU.is_ge, fill=0.0,
                               base=HD - 1, pattern=[[0, EV], [HD, H]], channel_multiplier=-1).then_inc(consts_ready, 1)
            lead, middle, last = bf16_parts(ATT_EPS)
            then(pool.memset(eps3[:, :], lead))
            for r, part in ((1, middle), (2, last)):
                then(pool.affine_select(out=eps3[:, :], in_=eps3[:, :], compare_op=ALU.is_gt, fill=part, base=r,
                                        pattern=[[0, SW]], channel_multiplier=-1))
            pool.affine_select(out=eps3[:, :], in_=eps3[:, :], compare_op=ALU.is_ge, fill=0.0, base=-HD * H,
                               pattern=[[1, SW]], channel_multiplier=0).then_inc(consts_ready, 1)
            for a in (swg[:, F:P + HB], swg[:, P + HB + FB:2 * P], ewg[:, :, F:P + HB], ewg[:, :, P + HB + FB:2 * P]):
                pool.memset(a, 0.0).then_inc(consts_ready, 1)
            pool.memset(halfneg[:, :], -0.5).then_inc(consts_ready, 1)
            pool.memset(ones3[:, :], 1.0).then_inc(consts_ready, 1)
            pool.memset(ones_bf[:, :], 1.0).then_inc(consts_ready, 1)
            pool.memset(v1[:, :, HD, :], 1.0).then_inc(consts_ready, 1)
            then(pool.iota(iota_i[:, 0:E], pattern=[[-1, E]], base=E, channel_multiplier=0))
            pool.tensor_copy(rank16[:, :], iota_i[:, 0:E]).then_inc(consts_ready, 1)
            then(pool.iota(iota_i[:, E:2 * E], pattern=[[CAP, E]], base=0, channel_multiplier=0))
            pool.tensor_copy(expert_base[:, :], iota_i[:, E:2 * E]).then_inc(consts_ready, 1)
            then(pool.iota(iota_i[:, 32:64], pattern=[[P, TILES]], base=ROWS, channel_multiplier=1))
            pool.tensor_copy(trash[:, :], iota_i[:, 32:64]).then_inc(consts_ready, 1)

            pool.wait_ge(consts_ready, 16)

            def outer(i, n):
                wait(pool, qk_ready, i + n + 1)
                wait(pool, v_sb, i + n + 1)
                wait(pool, cum_ps, i + n - 3)
                pool.tensor_tensor(
                    kv[:, n, :].rearrange("p (e h d) -> p e h d", e=EV, h=H),
                    qk[:, n, 1, :].rearrange("p (h d) -> p h d", h=H).unsqueeze(1).to_broadcast([P, EV, H, HD]),
                    v1[:, n, :, :].unsqueeze(3).to_broadcast([P, EV, H, HD]),
                    ALU.mult).then_inc(kv_ready, 1)

            def step(i):
                if isinstance(i, int) and i == NT:
                    pool.wait_ge(par_loaded, 16 * 7)
                if isinstance(i, int) and NT <= i < 4 * NT:
                    shift_input(pool, i // NT)
                for s in range(4):
                    if active(i, 1):
                        w, par = i + s - 4, s % 2
                        wait_apart(pool, mv1_done, w + 1, consts_ready)
                        pool.tensor_scalar(var1[:, par:par + 1], mv1[:, par, 1:2], LN_EPS, None, ALU.add).then_inc(var1_ready, 1)
                        wait(pool, var1_ready, w + 1)
                        wait(pool, norm1_done, w - 1)
                        pool.tensor_tensor(rstd1[:, par:par + 1], var1[:, par:par + 1], halfneg[:, 0:1], ALU.pow
                                           ).then_inc(rstd1_ready, 1)
                        wait_apart(pool, rstd1_ready, w + 1, consts_ready)
                        pool.tensor_scalar(shift1[:, par:par + 1], mv1[:, par, 0:1], rstd1[:, par:par + 1], -1.0,
                                           ALU.mult, ALU.mult).then_inc(shift1_ready, 1)
                    if active(i, 0):
                        outer(i, s)
                    if s == 2 and active(i, 3):
                        wait_apart(pool, mv2_done, i - 8, consts_ready, (norm2_done, i - 12))
                        pool.tensor_scalar(var2[:, :], mv2[:, :, 1], LN_EPS, None, ALU.add).then_inc(var2_ready, 4)
                        pool.tensor_scalar(less_mean2[:, :], mv2[:, :, 0], -1.0, None, ALU.mult).then_inc(less_mean2_ready, 4)
                        wait(pool, var2_ready, i - 8)
                        pool.tensor_tensor(rstd2[:, :], var2[:, :], halfneg[:, 0:NT], ALU.pow).then_inc(rstd2_ready, 4)
                        wait(pool, rstd2_ready, i - 8)
                        wait(pool, less_mean2_ready, i - 8)
                        pool.tensor_tensor(shift2[:, :], less_mean2[:, :], rstd2[:, :], ALU.mult).then_inc(shift2_ready, 4)
                    if active(i, 1):
                        layer = layer_of(i, 1)
                        wait_apart(pool, norm1_done, w + 1, consts_ready)
                        pool.tensor_tensor(xg1[:, :], xn1[:, par, :], gains[:, 0, ds(layer, 1), :].rearrange("p a d -> p (a d)"), ALU.mult
                                           ).then_inc(xg1_done, 1)
                        wait_apart(pool, xg1_done, w + 1, consts_ready)
                        pool.tensor_tensor(X[:, ds(tile_of(i, 1, s), 1), :].rearrange("p a d -> p (a d)"), xg1[:, :],
                                           gains[:, 1, ds(layer, 1), :].rearrange("p a d -> p (a d)"), ALU.add).then_inc(x1_ready, 1)
                    if s == 3 and active(i, 3):
                        layer = layer_of(i, 3)
                        wait_apart(pool, norm2_done, i - 8, consts_ready)
                        pool.tensor_tensor(xg2[:, :, :], xn2[:, :, :],
                                           gains[:, 2, ds(layer, 1), :].to_broadcast([P, NT, D]), ALU.mult
                                           ).then_inc(xg2_done, 4)
                        wait_apart(pool, xg2_done, i - 8, consts_ready)
                        pool.tensor_tensor(X[:, ds(tile_of(i, 3, 0), NT), :], xg2[:, :, :],
                                           gains[:, 3, ds(layer, 1), :].to_broadcast([P, NT, D]), ALU.add
                                           ).then_inc(x_ready, 4)
            steps(pool, step, lambda j: pool_head_step(pool, j), lambda j: pool_tail_step(pool, j))
            pool_tail(pool)

        @block.tensor
        def _(pe):
            pe.wait_ge(c_silu, 1)
            pe.wait_ge(c_loaded, 32)
            for n in range(2):
                mm = pe.matmul(ps[0:B, n, 0:NB], csT[:, :], wmod_s[:, n * NB:(n + 1) * NB], start=True, stop=True)
            mm.then_inc(mod_ps, 1)

            pe.wait_ge(consts_ready, 16)

            def qkv(i, n):
                if isinstance(i, int) and i == 0 and n == 0:
                    pe.wait_ge(qkv_loaded, 16 * 3)
                    pe.wait_ge(bias_ready, 16 * 3)
                wait_apart(pe, v_sb, i + n, consts_ready)
                if n == 0:
                    wait(pe, xt_sb, i + 4)
                layer = layer_of(i, 0)
                pe.matmul(ps_qkv.rearrange("p (n d) -> p n d", n=3), ones3[:, :], bias3_l[:, 0:3, ds(layer, 1), :].rearrange("r n a d -> r n (a d)"), start=True, stop=False)
                pe.matmul(ps_qkv, xT[:, n, :], wqkv[:, ds(layer, 1), :].rearrange("p a c -> p (a c)"), start=False, stop=True
                          ).then_inc(qkv_ps, 1)

            def attend(T, n, t_bank_free):
                wait(pe, qk_ready, T + 1)
                wait(pe, *t_bank_free)
                pe.transpose(ps_t[:, 0:P], qk[:, n, 0, :], ident[:, :]).then_inc(qt_ps, 1)
                wait(pe, kv_ready, T + 1)
                wait(pe, p_done, T)
                for j in range(3):
                    mm = pe.matmul(ps_cum[:, j, :], tri[:, :], kv[:, n, j * CB:(j + 1) * CB], start=True, stop=True)
                mm.then_inc(cum_ps, 1)
                wait(pe, qt_sb, T + 1)
                wait(pe, tot_done, T)
                mm = pe.matmul(ps_s[:, 0:SW], ones3[:, :], eps3[:, :], start=True, stop=(n == 0))
                if n > 0:
                    wait(pe, kvm_ready, T)
                    mm = pe.matmul(ps_s[:, 0:SW], qT[:, :], kvm[:, :], start=False, stop=True)
                if n < NT - 1:
                    wait(pe, v_sb, T + 1)
                    mm = pe.matmul(ps_s[:, SW:2 * SW], qk[:, n, 1, :], v1[:, n, :, :].rearrange("p e h -> p (e h)"), start=True, stop=True)
                mm.then_inc(inter_ps, 1)

            def att_transpose(u):
                wait(pe, att_ready, u + 1)
                wait(pe, qt_sb, u + 2)
                pe.transpose(ps_t[:, 0:P], att[:, :], ident[:, :]).then_inc(att_t_ps, 1)

            def project(i, u, back):
                if isinstance(u, int) and u == 0:
                    pe.wait_ge(par_loaded, 16 * 7)
                wait_apart(pe, att_t_sb, u + 1, consts_ready)
                wait(pe, y1_done, u)
                layer = layer_of(i, back)
                pe.matmul(ps_y[:, 2 * D:3 * D], ones3[:, :], bias3_l[:, 3, ds(layer, 1), :].rearrange("r a c -> r (a c)"), start=True, stop=False)
                pe.matmul(ps_y[:, 2 * D:3 * D], attT[:, :], wo[:, ds(layer, 1), :].rearrange("p a c -> p (a c)"), start=False, stop=True
                          ).then_inc(wo_ps, 1)

            def ffn_out(i, s, u):
                if isinstance(i, int) and i == 3 * NT and s == 0:
                    pe.wait_ge(w12_loaded, 16 * 2)
                layer = layer_of(i, 3)
                wait_apart(pe, gelu_done, i - 8, consts_ready, (y1_done, min(u, TILES * L) if isinstance(u, int) else u),
                           (y2_done, i - 12 + 2 * s))
                for m in range(2):
                    n = 2 * s + m
                    o = ps_y[:, m * D:(m + 1) * D]
                    pe.matmul(o, ones3[:, :], bias3_l[:, 4, ds(layer, 1), :].rearrange("r a c -> r (a c)"), start=True, stop=False)
                    for j in range(FC):
                        mm = pe.matmul(o, hT[:, j, n * P:(n + 1) * P], w2[:, ds(layer, 1), j, :].rearrange("p a c -> p (a c)"),
                                       start=False, stop=(j == FC - 1))
                    mm.then_inc(w2_ps, 1)

            def ffn_in(i, j):
                if j == 0:
                    wait(pe, x1t_sb, i - 4)
                    wait(pe, w1_load, (i - 4) * 4)
                wait(pe, gelu_done, i - 8 + j)
                pe.matmul(ps_h, w1s[:, j * P:(j + 1) * P], x1T[:, :], start=True, stop=True).then_inc(h_ps, 1)

            def step(i):
                for s in range(2):
                    T = i - 2 + s
                    u = T - 1
                    if s == 1 and active(i, 2):
                        wait(pe, x1s_load, (i - 4) * 4)
                        wait(pe, att_t_sb, (T - 1) if active(i, 1) else TILES * L)
                        for n in range(NT):
                            mm = pe.transpose(ps_t[:, n * P:(n + 1) * P], x1s[:, n, :], ident[:, :])
                        mm.then_inc(x1t_ps, 4)
                    if active(i, 0):
                        qkv(i, 2 * s)
                    if active(i, 1):
                        attend(T, 2 + s, (att_t_sb, T - 1) if s == 0 or not active(i, 2) else (x1t_sb, i - 4))
                    if active(i, 0):
                        qkv(i, 2 * s + 1)
                    if active(i, 1):
                        att_transpose(u)
                    if active(i, 3):
                        ffn_out(i, s, u)
                    if active(i, 1):
                        project(i, u, 1)
                for s in range(2):
                    T = i + s
                    u = T - 1
                    if active(i, 2):
                        ffn_in(i, 2 * s)
                    if active(i, 0):
                        t_free = (xt_sb, i + 8) if s == 1 and active(i, -1) else (att_t_sb, T - 1)
                        attend(T, s, t_free)
                    if active(i, s == 0):
                        att_last = not active(i, 0)
                        if att_last:
                            wait(pe, att_ready, u + 1)
                            wait(pe, x1t_sb, i - 4)
                            wait(pe, att_t_sb, u)
                            pe.transpose(ps_t[:, 0:P], att[:, :], ident[:, :]).then_inc(att_t_ps, 1)
                        else:
                            att_transpose(u)
                    if active(i, 2):
                        ffn_in(i, 2 * s + 1)
                    if active(i, s == 0):
                        project(i, u, 1 if s == 0 else 0)
                    if s == 0 and active(i, -1):
                        wait(pe, xs_load, (i + 8) * 4)
                        if active(i, 1):
                            wait(pe, att_t_sb, u + 1)
                        elif active(i, 0):
                            wait(pe, qt_sb, i + 1)
                        for n in range(NT):
                            mm = pe.transpose(ps_t[:, n * P:(n + 1) * P], xs[:, n, :], ident[:, :])
                        mm.then_inc(xt_ps, 4)
            steps(pe, step, lambda j: None, lambda j: pe_tail_step(pe, j))
            pe_tail(pe)

        @block.scalar
        def _(act):
            act.wait_ge(c_loaded, 32)
            act.activation(csT[:, :], cT[:, :], ACT.Silu).then_inc(c_silu, 1)
            act.dma_start(bias_f[0:1, 0:E], router_b.rearrange("(a d) -> a d", a=1)).then_inc(bias_loaded, 16)
            rows_each = L * D // 32
            for n, v in enumerate((bq, bk, bv, bo, b2)):
                act.dma_start(bias_f[1 + n * rows_each:1 + (n + 1) * rows_each, :], v.rearrange("l (a d) -> (l a) d", d=32)
                              ).then_inc(bias_loaded, 16)
            act.dma_start(b1c[:, :, :].rearrange("p l c -> p (l c)"), b1.rearrange("l (c p) -> p (l c)", p=P),
                          allow_slow_non_contiguous=True).then_inc(b1_loaded, 16)

            act.wait_ge(consts_ready, 16)

            def qkv_out(i, n):
                wait(act, qkv_ps, i + n + 1)
                wait(act, qk_ready, i + n - 1)
                act.activation(ex[:, n % 2, :], ps_qkv[:, 0:2 * D], ACT.Exp)
                act.activation(rl[:, n % 2, :], ps_qkv[:, 0:2 * D], ACT.Relu).then_inc(er_ready, 1)
                wait(act, kv_ready, i + n - 3)
                wait(act, inter_ps, i + n - 3)
                act.activation(v1[:, n, 0:HD, :].rearrange("p e h -> p h e"),
                               ps_qkv[:, 2 * D:3 * D].rearrange("p (h e) -> p h e", h=H), ACT.Copy).then_inc(v_sb, 1)

            def q_out(T):
                wait(act, qt_ps, T + 1)
                wait(act, inter_ps, T)
                act.activation(qT[:, :], ps_t[:, 0:P], ACT.Copy).then_inc(qt_sb, 1)

            def att_out(u):
                wait(act, att_t_ps, u + 1)
                wait(act, wo_ps, u)
                act.activation(attT[:, :], ps_t[:, 0:P], ACT.Copy).then_inc(att_t_sb, 1)

            def gelu(i, j):
                wait(act, h_ps, i - 8 + j + 1)
                if j == 0:
                    wait(act, w2_ps, i - 8)
                    if isinstance(i, int) and i == 2 * NT:
                        act.wait_ge(b1_loaded, 16)
                layer = layer_of(i, 2)
                act.activation(hT[:, j, :], ps_h, ACT.Gelu, bias=b1c[:, ds(layer, 1), j]).then_inc(gelu_done, 1)

            def norm1(w, par):
                wait(act, shift1_ready, w + 1)
                wait(act, xg1_done, w - 1)
                act.activation(xn1[:, par, :], y1[:, par, :], ACT.Identity, bias=shift1[:, par:par + 1],
                               scale=rstd1[:, par:par + 1]).then_inc(norm1_done, 1)

            def norm2(i):
                wait(act, xg2_done, i - 12)
                wait(act, shift2_ready, i - 8)
                for n in range(NT):
                    act.activation(xn2[:, n, :], y2[:, n, :], ACT.Identity, bias=shift2[:, n:n + 1],
                                   scale=rstd2[:, n:n + 1]).then_inc(norm2_done, 1)

            def step(i):
                for s in range(2):
                    T = i - 2 + s
                    if s == 1 and active(i, 2):
                        wait(act, x1t_ps, i - 4)
                        wait(act, h_ps, i - 8)
                        act.activation(x1T[:, :], ps_t[:, :], ACT.Copy).then_inc(x1t_sb, 4)
                    if active(i, 1):
                        q_out(T)
                    if active(i, 0):
                        qkv_out(i, 2 * s)
                        qkv_out(i, 2 * s + 1)
                    if active(i, 1):
                        att_out(T - 1)
                        norm1(i + s - 4, s % 2)
                for s in range(2):
                    T = i + s
                    if active(i, 0):
                        q_out(T)
                    if active(i, 2):
                        gelu(i, 2 * s)
                    if active(i, s == 0):
                        att_out(T - 1)
                    if active(i, 1) and s == 1:
                        norm1(i + s - 2, s % 2)
                    if active(i, 2):
                        gelu(i, 2 * s + 1)
                    if s == 0 and active(i, -1):
                        wait(act, xt_ps, i + 8)
                        wait(act, qkv_ps, i + 4)
                        act.activation(xT[:, :, :].rearrange("p n t -> p (n t)"), ps_t[:, :], ACT.Copy).then_inc(xt_sb, 4)
                    if active(i, 1) and s == 0:
                        norm1(i + s - 2, s % 2)
                    if s == 0 and active(i, 3):
                        norm2(i)
            steps(act, step, lambda j: act_head_step(act, j), lambda j: act_tail_step(act, j))
            act_tail(act)

        @block.vector
        def _(dve):
            done = [0]

            def then(ins):
                done[0] += 1
                ins.then_inc(setup_step, 1)
                dve.wait_ge(setup_step, done[0])

            dve_head_step(dve, 0)

            dve.wait_ge(mod_ps, 1)
            for n in range(2):
                last = dve.tensor_copy(mod8[:, n * NB:(n + 1) * NB], ps[0:B, n, 0:NB])
                then(last)
            m3 = mod8[:, :].rearrange("b (g m d) -> b g m d", g=2, m=3)
            then(dve.tensor_scalar(m3[:, :, 1, :], m3[:, :, 1, :], 1.0, None, ALU.add))
            then(dve.tensor_scalar(gsign[:, :, :], m3[:, :, 2, :], 0.0, 2.0, ALU.is_ge, ALU.mult))
            then(dve.tensor_scalar(gsign[:, :, :], gsign[:, :, :], -1.0, None, ALU.add))
            then(dve.tensor_tensor(m3[:, :, 2, :], m3[:, :, 2, :], gsign[:, :, :], ALU.mult))
            dve.scalar_tensor_tensor(out=m3[:, :, 2, :], in0=m3[:, :, 2, :], scalar=0.25, in1=gsign[:, :, :],
                                     op0=ALU.max, op1=ALU.mult).then_inc(mod8_ready, 1)

            dve.memset(zrow[:, :], 0.0).then_inc(q["zrow_ready"], 1)
            then(dve.memset(bias_f[0:1, E:2 * E], 0.0))
            dve.wait_ge(bias_loaded, 16 * 6)
            for r in range(3):
                dve.tensor_copy(bias_parts[:, r, :], bias_f[:, :]).then_inc(bias_split, 1)
                dve.wait_ge(bias_split, r + 1)
                if r < 2:
                    then(dve.tensor_tensor(bias_f[:, :], bias_f[:, :], bias_parts[:, r, :], ALU.subtract))
            def feature_map(i, n):
                wait(dve, er_ready, i + n + 1)
                wait(dve, inter_ps, i + n - 3)
                wait(dve, kv_ready, i + n - 3)
                dve.scalar_tensor_tensor(out=qk[:, n, :, :].rearrange("p a d -> p (a d)"), in0=ex[:, n % 2, :], scalar=1.0, in1=rl[:, n % 2, :],
                                         op0=ALU.min, op1=ALU.add).then_inc(qk_ready, 1)

            def weigh(T, n):
                wait(dve, cum_ps, T + 1)
                dve.tensor_tensor(prod[:, :].rearrange("p (b e c) -> p b e c", b=3, e=3),
                                  ps_cum.rearrange("p b (e c) -> p b e c", e=3),
                                  qk[:, n, 0, :].unsqueeze(1).unsqueeze(1).to_broadcast([P, 3, 3, D]),
                                  ALU.mult).then_inc(p_done, 1)

            def outputs(T, n):
                wait(dve, inter_ps, T + 1)
                if n == 0:
                    dve.tensor_tensor(kvm[:, :], ps_s[:, SW:2 * SW], headmask[:, :, :].rearrange("p e h -> p (e h)"), ALU.mult).then_inc(kvm_ready, 1)
                elif n < NT - 1:
                    dve.tensor_tensor(kvt[:, :], ps_s[:, SW:2 * SW], headmask[:, :, :].rearrange("p e h -> p (e h)"), ALU.mult).then_inc(kvt_done, 2)
                wait(dve, p_done, T + 1)
                dve.tensor_reduce(red[:, :], prod[:, :].rearrange("p (c d) -> p c d", d=HD), AXX, ALU.add).then_inc(red_done, 1)
                if 0 < n < NT - 1:
                    wait(dve, kvt_done, T + 1 if n == 1 else T + 2)
                    dve.tensor_tensor(kvm[:, :], kvm[:, :], kvt[:, :], ALU.add).then_inc(kvm_ready, n)
                wait(dve, red_done, T + 1)
                dve.tensor_tensor(tot[:, :, :].rearrange("p e h -> p (e h)"), red[:, :], ps_s[:, 0:SW], ALU.add).then_inc(tot_done, 1)
                wait(dve, tot_done, T + 1)
                dve.reciprocal(rden[:, :], tot[:, HD, :]).then_inc(rden_done, 1)
                wait(dve, rden_done, T + 1)
                wait(dve, att_t_ps, T)
                dve.tensor_tensor(att[:, :].rearrange("p (h e) -> p h e", h=H),
                                  tot[:, 0:HD, :].rearrange("p e h -> p h e"),
                                  rden[:, :].unsqueeze(2).to_broadcast([P, H, HD]), ALU.mult).then_inc(att_ready, 1)

            def ffn_residual(i, s, u):
                wait(dve, norm2_done, i - 12)
                for m in range(2):
                    n = 2 * s + m
                    wait(dve, w2_ps, i - 12 + 2 * s + 2)
                    wait(dve, wo_ps, u + 1)
                    dve.tensor_tensor(y2[:, n, :], ps_y[:, m * D:(m + 1) * D],
                                      X[:, ds(tile_of(i, 3, n), 1), :].rearrange("p a d -> p (a d)"), ALU.add).then_inc(y2_done, 1)

            def ffn_stats(i, s):
                for m in range(2):
                    n = 2 * s + m
                    wait(dve, y2_done, i - 12 + n + 1)
                    dve.bn_stats(st2[:, n, :], y2[:, n, :]).then_inc(st2_done, 1)

            def ffn_moments(i, s):
                for m in range(2):
                    n = 2 * s + m
                    wait_apart(dve, st2_done, i - 12 + n + 1, consts_ready)
                    dve.bn_aggr(mv2[:, n, :], st2[:, n, :]).then_inc(mv2_done, 1)

            def att_residual(i, u, back, n, par):
                wait(dve, wo_ps, u + 1)
                wait(dve, norm1_done, u - 1)
                dve.tensor_tensor(y1[:, par, :], ps_y[:, 2 * D:3 * D],
                                  X[:, ds(tile_of(i, back, n), 1), :].rearrange("p a d -> p (a d)"), ALU.add).then_inc(y1_done, 1)

            def att_stats(u, par):
                wait(dve, y1_done, u + 1)
                dve.bn_stats(st1[:, par, :], y1[:, par, :]).then_inc(st1_done, 1)

            def att_moments(u, par):
                wait_apart(dve, st1_done, u + 1, consts_ready)
                dve.bn_aggr(mv1[:, par, :], st1[:, par, :]).then_inc(mv1_done, 1)

            def step(i):
                for s in range(4):
                    back, n = (1, 2 + s) if s < 2 else (0, s - 2)
                    T = i - 2 + s
                    u_back, u_n = (1, 1 + s) if s < 3 else (0, 0)
                    if s < 2 and active(i, 0):
                        feature_map(i, 2 * s)
                    if active(i, back):
                        weigh(T, n)
                    if active(i, back):
                        outputs(T, n)
                    if s < 2 and active(i, 0):
                        feature_map(i, 2 * s + 1)
                    u = T - 1
                    if s < 2 and active(i, 3):
                        ffn_residual(i, s, u if active(i, 1) else TILES * L - 1)
                    if active(i, u_back):
                        att_residual(i, u, u_back, u_n, (s + 1) % 2)
                    if s < 2 and active(i, 3):
                        ffn_stats(i, s)
                    if active(i, u_back):
                        att_stats(u, (s + 1) % 2)
                    if s < 2 and active(i, 3):
                        ffn_moments(i, s)
                    if active(i, u_back):
                        att_moments(u, (s + 1) % 2)
            steps(dve, step, lambda j: dve_head_step(dve, j) if j else None, lambda j: dve_tail_step(dve, j))
            dve_tail(dve)


_INS = ['L0_attn_x', 'L0_attn_Wq', 'L0_attn_bq', 'L0_attn_Wk', 'L0_attn_bk', 'L0_attn_Wv', 'L0_attn_bv', 'L0_attn_Wo', 'L0_attn_bo', 'L0_attn_W1', 'L0_attn_b1', 'L0_attn_W2', 'L0_attn_b2', 'L0_attn_g1', 'L0_attn_be1', 'L0_attn_g2', 'L0_attn_be2', 'L0_attn_gf', 'L0_attn_bef', 'L0_ffn_router_w', 'L0_ffn_router_b', 'L0_ffn_w_gate', 'L0_ffn_w_up', 'L0_ffn_w_down', 'L0_ffn_sw_gate', 'L0_ffn_sw_up', 'L0_ffn_sw_down', 'L0_c', 'L0_wmod']
_OUTS = [((8, 512, 128), 'float32')]


def kernel(**inputs):
    import numpy as _np
    import concourse.bacc as _bacc
    from concourse import mybir as _mybir
    from concourse.bass_utils import run_bass_kernel_spmd as _run

    nc = _bacc.Bacc("TRN2", target_bir_lowering=False, num_devices=1)
    arrays, args = {}, []
    for name in _INS:
        a = _np.ascontiguousarray(inputs[name])
        arrays[f"in_{name}_dram"] = a
        args.append(nc.dram_tensor(f"in_{name}_dram", a.shape, _mybir.dt.from_np(a.dtype), kind="ExternalInput").ap())
    for i, (shape, dtype) in enumerate(_OUTS):
        dt = _mybir.dt.from_np(_np.dtype(dtype))
        args.append(nc.dram_tensor(f"out_{i}_dram", shape, dt, kind="ExternalOutput").ap())
    adaln_block_kernel(nc, *args)
    r = _run(nc, [arrays], core_ids=[0])
    got = tuple(r.results[0][f"out_{i}_dram"] for i in range(len(_OUTS)))
    return got[0]
```

```python
import numpy as np

import concourse.bass as bass
from concourse import mybir
from contextlib import ExitStack

F32 = mybir.dt.float32
BF16 = mybir.dt.bfloat16
U32 = mybir.dt.uint32
ALU = mybir.AluOpType
ACT = mybir.ActivationFunctionType
AXX = mybir.AxisListType.X
ds = bass.ds

P = 128
B, S, D = 8, 512, 128
L, H, HD, FF = 4, 16, 8, 512
NT = S // P
TILES = B * NT
EV = HD + 1
CW = EV * D
CB = CW // 3
SW = EV * H
FC = FF // P
STEPS = L * B
LN_EPS, ATT_EPS = 1e-5, 1e-6
NB = 3 * D
BIAS = NB + 2 * D


def bf16_parts(value):
    parts, rest = [], np.float32(value)
    for _ in range(3):
        bits = rest.view(np.uint32)
        part = np.uint32((int(bits) + 0x7FFF + ((int(bits) >> 16) & 1)) & 0xFFFF0000).view(np.float32)
        parts.append(float(part))
        rest = np.float32(rest - part)
    return parts


def wait(engine, sem, value):
    if isinstance(value, int) and value <= 0:
        return
    engine.wait_ge(sem, value)


def wait_apart(engine, sem, value, ready, *more):
    waits = ((sem, value),) + more
    for _, value in waits:
        if not isinstance(value, int):
            engine.compute_val(value)
    engine.wait_ge(ready, 1)
    for sem, value in waits:
        wait(engine, sem, value)


def adaln_block_kernel(nc, x, Wq, bq, Wk, bk, Wv, bv, Wo, bo, W1, b1, W2, b2, g1, be1, g2, be2, gf, bef,
                       router_w, router_b, w_gate, w_up, w_down, sw_gate, sw_up, sw_down, c, wmod, out):
    E = router_w.shape[1]
    F = w_gate.shape[2]
    FA, FB = P, F - P
    HB = P // 2
    assert FB <= HB
    TOK = B * S
    CAP = -(-5 * 2 * TOK // (4 * E))
    CT = CAP // P
    HC = CAP // 2
    assert CAP % (2 * P) in (0, P) and HC <= 512 and CAP % P == 0
    ROWS = E * CAP
    MODS = 6 * D

    x_v = x.rearrange("b (n p) d -> b p n d", p=P)
    out_v = out.rearrange("b (n p) d -> b p n d", p=P)
    mod_dram = nc.dram_tensor("mod_scratch", [B, MODS], F32, kind="Internal").ap()
    xe_dram = nc.dram_tensor("expert_in_scratch", [ROWS + 2 * TOK, D], F32, kind="Internal").ap()
    ye_dram = nc.dram_tensor("expert_out_scratch", [ROWS, D], F32, kind="Internal").ap()
    xe_tiles = xe_dram[0:ROWS, :].rearrange("(e p j) d -> e p (j d)", e=E, p=P)
    ye_tiles = ye_dram.rearrange("(e p j) d -> e p (j d)", e=E, p=P)

    with ExitStack() as ctx:
        def sb(name, shape, dt=F32):
            return ctx.enter_context(nc.sbuf_tensor(name, shape, dt))

        def sem(name):
            return ctx.enter_context(nc.semaphore(name))

        ident = sb("ident", [P, P])
        tri = sb("tri", [P, P])
        tri_before = sb("tri_before", [P, P], BF16)
        ones_bf = sb("ones_bf", [P, P], BF16)
        ones3 = sb("ones3", [3, P], BF16)
        headmask = sb("headmask", [P, EV, H])
        halfneg = sb("halfneg", [P, 4 * B])
        rank16 = sb("rank16", [P, E])
        expert_base = sb("expert_base", [P, E])
        trash = sb("trash", [P, 2, TILES])
        iota_i = sb("iota_i", [P, 96], mybir.dt.int32)
        wqkv = sb("wqkv", [P, L, NB])
        wo = sb("wo", [P, L, D])
        w1 = sb("w1", [P, L, FF])
        w2 = sb("w2", [P, L, FC, D])
        b1c = sb("b1c", [P, L, FC])
        gains = sb("gains", [P, 4, L, D])
        gfb = sb("gfb", [P, 2, D])
        BR = 1 + 5 * L * D // 32
        assert 2 * E == 32
        bias3 = sb("bias3", [3, BR * 32], BF16)
        bias3_l = bias3[:, 32:].rearrange("r (n l d) -> r n l d", n=5, l=L)
        rb3 = bias3[:, 0:E]
        eps3 = sb("eps3", [3, SW], BF16)
        bias_f = sb("bias_f", [BR, 32])
        bias_parts = sb("bias_parts", [BR, 3, 32], BF16)
        cT = sb("cT", [P, B])
        csT = sb("csT", [P, B])
        table_use = sb("table_use", [P, 1])
        wmod_s = sb("wmod_s", [P, MODS])
        mod8 = sb("mod8", [B, MODS])
        gsign = sb("gsign", [B, 2, D])
        mod = sb("mod", [P, B, 6, D])
        x0 = sb("x0", [P, TILES, D])
        X = sb("X", [P, TILES, D])
        xs = sb("xs", [P, NT, D])
        x1s = sb("x1s", [P, NT, D])
        w1s = sb("w1s", [P, FF])
        xT = sb("xT", [P, NT, P])
        x1T = sb("x1T", [P, S])
        ex = sb("ex", [P, 2, 2 * D])
        rl = sb("rl", [P, 2, 2 * D])
        qk = sb("qk", [P, NT, 2, D])
        v1 = sb("v1", [P, NT, EV, H])
        kv = sb("kv", [P, NT, CW])
        qT = sb("qT", [P, P])
        kvm = sb("kvm", [P, SW])
        kvt = sb("kvt", [P, SW])
        room = sb("room", [P, 5 * TILES * E])
        prod = sb("prod", [P, CW])
        red = sb("red", [P, SW])
        tot = sb("tot", [P, EV, H])
        rden = sb("rden", [P, H])
        att = sb("att", [P, D])
        attT = sb("attT", [P, P])
        y1 = sb("y1", [P, 2, D])
        st1 = sb("st1", [P, 2, 6])
        mv1 = sb("mv1", [P, 2, 2])
        var1 = sb("var1", [P, 2])
        rstd1 = sb("rstd1", [P, 2])
        shift1 = sb("shift1", [P, 2])
        xn1 = sb("xn1", [P, 2, D])
        xg1 = sb("xg1", [P, D])
        hT = sb("hT", [P, FC, S])
        y2 = sb("y2", [P, NT, D])
        st2 = sb("st2", [P, NT, 6])
        mv2 = sb("mv2", [P, NT, 2])
        var2 = sb("var2", [P, NT])
        rstd2 = sb("rstd2", [P, NT])
        less_mean2 = sb("less_mean2", [P, NT])
        shift2 = sb("shift2", [P, NT])
        xn2 = sb("xn2", [P, NT, D])
        xg2 = sb("xg2", [P, NT, D])

        ps = ctx.enter_context(nc.psum_tensor("ps", [P, 8, 512], F32))
        ps_cum = ps[:, 0:3, 0:CB]
        ps_qkv = ps[:, 3, 0:NB]
        ps_s = ps[:, 4, :]
        ps_h = ps[:, 5, :]
        ps_t = ps[:, 6, :]
        ps_y = ps[:, 7, :]

        x_loaded = sem("x_loaded")
        row0_loaded = sem("row0_loaded")
        mod01_loaded = sem("mod01_loaded")
        c_loaded = sem("c_loaded")
        par_loaded = sem("par_loaded")
        w12_loaded = sem("w12_loaded")
        bias_loaded = sem("bias_loaded")
        b1_loaded = sem("b1_loaded")
        qkv_loaded = sem("qkv_loaded")
        bias_split = sem("bias_split")
        mod_stored = sem("mod_stored")
        mod_loaded = sem("mod_loaded")
        consts_ready = sem("consts_ready")
        const_step = sem("const_step")
        setup_step = sem("setup_step")
        c_silu = sem("c_silu")
        mod_ps = sem("mod_ps")
        mod8_ready = sem("mod8_ready")
        bias_ready = sem("bias_ready")
        x_ready = sem("x_ready")
        names = """xs_load w1_load x1s_load
            xt_ps qkv_ps qt_ps cum_ps inter_ps att_t_ps wo_ps h_ps x1t_ps w2_ps
            xt_sb er_ready v_sb qt_sb att_t_sb gelu_done x1t_sb
            qk_ready p_done kvt_done kvm_ready red_done tot_done rden_done att_ready y1_done st1_done mv1_done
            var1_ready norm1_done y2_done st2_done mv2_done var2_ready norm2_done
            kv_ready rstd1_ready shift1_ready less_mean2_ready shift2_ready xg1_done x1_ready rstd2_ready xg2_done""".split()
        (xs_load, w1_load, x1s_load,
         xt_ps, qkv_ps, qt_ps, cum_ps, inter_ps, att_t_ps, wo_ps, h_ps, x1t_ps, w2_ps,
         xt_sb, er_ready, v_sb, qt_sb, att_t_sb, gelu_done, x1t_sb,
         qk_ready, p_done, kvt_done, kvm_ready, red_done, tot_done, rden_done, att_ready, y1_done, st1_done,
         mv1_done, var1_ready, norm1_done, y2_done, st2_done, mv2_done, var2_ready, norm2_done,
         kv_ready, rstd1_ready, shift1_ready, less_mean2_ready, shift2_ready, xg1_done, x1_ready, rstd2_ready, xg2_done) = [sem(n) for n in names]
        out_stored = sem("out_stored")

        def active(i, back):
            return not isinstance(i, int) or 0 <= i // NT - back < STEPS

        def layer_of(i, back):
            return ((i - NT * back) // NT) // B

        def row_of(i, back):
            return ((i - NT * back) // NT) % B

        def tile_of(i, back, n):
            return row_of(i, back) * NT + n

        def first(i):
            return i // NT * NT

        ROUTE_AFTER = 7
        DRAIN = ((), (0,), (1,), (2,))

        def is_first(i):
            return isinstance(i, int) and i == -NT

        def head_row(i, s):
            if isinstance(i, int) and i == s == 0:
                return 2
            if isinstance(i, int) and 0 <= i < 3 * NT and s in (1, 3):
                return 3 + 2 * (i // NT) + (s == 3)
            return None

        def steps(engine, body, head_step, tail_step, route):
            head_step(0)
            body(-NT)
            head_step(1)
            for k in range(4):
                body(k * NT)
            with engine.Fori(4 * NT, (STEPS - 1) * NT, NT) as i:
                body(i)
            for k in range(STEPS - 1, STEPS + 3):
                body(k * NT)
                for j in DRAIN[k - STEPS + 1]:
                    tail_step(j)
            for j in range(DRAIN[-1][-1] + 1, B + 3):
                tail_step(j)
                if j == ROUTE_AFTER:
                    route(0)
            route(1)

        Hr = x0
        hT_all = kv[:, :, :].rearrange("p n c -> p (n c)")[:, 0:TILES * D]
        f_st, g_st = (sb(f"{n}_st", [P, NT, 6]) for n in "fg")
        f_mean_var, g_mean_var = (sb(f"{n}_mean_var", [P, NT, 2]) for n in "fg")
        f_small, g_small = (sb(f"{n}_small", [P, 4, NT]) for n in "fg")
        z_st = sb("z_st", [P, NT, 6])
        z_mean_var = sb("z_mean_var", [P, NT, 2])
        z_small = sb("z_small", [P, 4, NT])
        z_xn = room[:, 0:S].rearrange("p (n d) -> p n d", n=NT)
        f_xn = ex[:, :, :].rearrange("p a c -> p (a c)").rearrange("p (n d) -> p n d", n=NT)
        g_xn = xT
        bef_ga = room[:, S:S + B * D].rearrange("p (b d) -> p b d", b=B)
        rw = sb("rw", [P, E])
        swg = sb("swg", [P, 3 * P])
        swd = sb("swd", [P, 2, D])
        sil_a, sil_b, hid_a, hid_b = (hT[:, j, :] for j in range(FC))

        ysh = sb("ysh", [P, NT, D])
        gh = xs
        TE = TILES * E
        lg, pr, ra = (room[:, n * TE:(n + 1) * TE].rearrange("p (t e) -> p t e", e=E) for n in (0, 1, 4))
        oh = room[:, 2 * TE:4 * TE].rearrange("p (k t e) -> p k t e", k=2, e=E)
        TH = TILES // 2
        picked = prod[:, 0:2 * TH * E].rearrange("p (k t e) -> p k t e", k=2, e=E)
        selb = sb("selb", [P, TILES, E], BF16)
        rmax = sb("rmax", [P, TILES])
        rsum = sb("rsum", [P, TILES])
        first_at = sb("first_at", [P, TILES])
        prob, keep, slot, tmp2 = (sb(n, [P, 2, TILES]) for n in ("prob", "keep", "slot", "tmp2"))
        wgt = sb("wgt", [P, 2, TILES])
        scat_u = sb("scat_u", [P, TILES, 2], U32)
        gath_u = sb("gath_u", [P, TILES, 2], U32)
        idx_s = sb("idx_s", [P, 2, 2 * NT], U32)
        hs2 = sb("hs2", [P, 2, NT, D])
        zrow = room[:, 3 * S:3 * S + CT * D]
        ewg = sb("ewg", [P, 2, 3 * P])
        ewd = sb("ewd", [P, 2, 2, D])
        kv_room = kv[:, :, :].rearrange("p n c -> p (n c)")
        xes = kv_room[:, 0:2 * CAP].rearrange("p (a c) -> p a c", a=2)
        w2_room = w2[:, :, :, :].rearrange("p l c d -> p (l c d)")
        gains_room = gains[:, :, :, :].rearrange("p g l d -> p (g l d)")
        xeT = wqkv[:, :, :].rearrange("p l c -> p (l c)")[:, 0:2 * CAP].rearrange("p (a c) -> p a c", a=2)
        ehid_a = w2_room[:, 0:2 * CAP].rearrange("p (a c) -> p a c", a=2)
        esil_a = w2_room[:, 2 * CAP:2 * CAP + HC]
        esil_b = w2_room[:, 2 * CAP + HC:3 * CAP]
        ehid_b = gains_room[:, 0:2 * CAP].rearrange("p (a c) -> p a c", a=2)
        yes = kv_room[:, 2 * CAP:4 * CAP].rearrange("p (a c) -> p a c", a=2)
        yg = w1[:, :, :].rearrange("p l f -> p (l f)").rearrange("p (a k d) -> p a k d", a=2, k=2 * NT)
        ymix = kv_room[:, 4 * CAP:4 * CAP + S].rearrange("p (n d) -> p n d", n=NT)
        yout = kv_room[:, 4 * CAP + S:4 * CAP + 3 * S].rearrange("p (a n d) -> p a n d", a=2, n=NT)

        tail_names = """z_stats z_mv z_var z_less_mean z_rstd z_shift z_norm z_scaled f_stats f_mv f_var f_less_mean f_rstd f_shift f_norm f_gain x2_ready gf_ga_ready bef_ga_ready
            x0_shifted g_stats g_mv g_var g_less_mean g_rstd g_shift g_norm g_scaled h_ready gh_done xh_ready
            sw_loaded ht_ps ht_sb lg_ps lg_sb
            shd_ps ysh_done xsh_done lg_shift lg_exp route_step cnt_ready cnt_ps route_ready xe_zeroed zrow_ready
            hs2_load0 hs2_load1 idx_ready scat0 scat1 ew_load0 ew_load1 ewd_load0 ewd_load1 xe_load0 xe_load1 xet_ps xet_sb ga_ps gub_ps
            ua_ps esa_done esb_done eha_done ehb_done ye_ps ye_sb ye_store0 ye_store1 gat0 gat1
            mix1_done mix2_done mixg_done out_ready0 out_ready1 out_store0 out_store1""".split()
        q = {n: sem(n) for n in tail_names}
        hs2_load, ew_load, xe_load = (q["hs2_load0"], q["hs2_load1"]), (q["ew_load0"], q["ew_load1"]), (q["xe_load0"], q["xe_load1"])
        ewd_load = (q["ewd_load0"], q["ewd_load1"])
        scat, gat, ye_store = (q["scat0"], q["scat1"]), (q["gat0"], q["gat1"]), (q["ye_store0"], q["ye_store1"])
        out_ready, out_store = (q["out_ready0"], q["out_ready1"]), (q["out_store0"], q["out_store1"])
        LAST = TILES * (L + 1)
        tile_bank = ps[:, 4:6, :]
        down_bank = ps[:, 6:8, :]

        def rows_of(a, i):
            return a[:, ds(first(i), NT), :]

        def modulation(i, m):
            return mod[:, ds(i // NT, 1), m, :].to_broadcast([P, NT, D])

        def even(r):
            return r // 2 * 2

        def rows(engine, body, step=NT, end=TILES):
            body(0)
            with engine.Fori(step, end, step) as i:
                body(i)

        def experts(engine, body):
            body(0, 0)
            with engine.Fori(1, E - 1, 2) as r:
                e = even(r - 1) + 1
                body(e, 1)
                body(e + 1, 0)
            body(E - 1, 1)

        def sp_tail(sp):
            for b in range(2):
                sp.wait_ge(q["h_ready"], b + 1)
                sp.dma_start(hs2[:, b, :, :], Hr[:, b * NT:(b + 1) * NT, :]).then_inc(hs2_load[b], 16)
            with sp.Fori(2, B, 2) as r:
                b = even(r - 2) + 2
                for par in range(2):
                    sp.wait_ge(q["h_ready"], b + par + 1)
                    sp.wait_ge(scat[par], b * 64)
                    sp.dma_start(hs2[:, par, :, :], Hr[:, ds((b + par) * NT, NT), :]).then_inc(hs2_load[par], 16)

            def expert_weights(e, par):
                wait(sp, q["ua_ps"], B + 2 * e - 2 if not isinstance(e, int) or e > 1 else 0)
                gate, up = (w[ds(e, 1)].rearrange("a k f -> (a k) f") for w in (w_gate, w_up))
                sp.dma_start(ewg[:, par, 0:F], gate).then_inc(ew_load[par], 16)
                sp.dma_start(ewg[:, par, 2 * P:], up[:, 0:FA]).then_inc(ew_load[par], 16)
                sp.dma_start(ewg[:, par, P + HB:P + HB + FB], up[:, FA:F]).then_inc(ew_load[par], 16)
                wait(sp, q["ye_ps"], e - 1)
                sp.dma_start(ewd[:, par, 0, :], w_down[ds(e, 1), 0:FA, :].rearrange("a k f -> (a k) f")).then_inc(ewd_load[par], 16)
                sp.dma_start(ewd[0:FB, par, 1, :], w_down[ds(e, 1), FA:F, :].rearrange("a k f -> (a k) f")).then_inc(ewd_load[par], 16)

            def expert_rows(e, par):
                wait(sp, q["xet_ps"], e - 1)
                sp.dma_start(xes[:, par, :], xe_tiles[ds(e, 1)].rearrange("a p c -> (a p) c")).then_inc(xe_load[par], 16)

            for e in range(2):
                expert_weights(e, e)
            for par in range(2):
                sp.wait_ge(scat[par], B * 64)
            sp.wait_ge(q["ua_ps"], B)
            for e in range(2):
                expert_rows(e, e)
            with sp.Fori(2, E, 2) as r:
                e = even(r - 2) + 2
                for par in range(2):
                    expert_rows(e + par, par)
                    expert_weights(e + par, par)

            def store_rows(r):
                b = even(r)
                for par in range(2):
                    sp.wait_ge(out_ready[par], b // 2 + 1)
                    sp.dma_start(out_v[ds(b + par, 1)].rearrange("a p n d -> (a p) n d"), yout[:, par, :, :]
                                 ).then_inc(out_store[par], 16)
            rows(sp, store_rows, 2, B)
            for par in range(2):
                sp.wait_ge(out_store[par], 16 * (B // 2))
                sp.wait_ge(ye_store[par], 16 * (E // 2))
            sp.wait_ge(q["xe_zeroed"], 16 * E)
            sp.wait_ge(mod_stored, 16)

        def tile_rows(b):
            return slice(b * NT, (b + 1) * NT)

        def wide(a):
            return a.to_broadcast([P, NT, D])

        def dve_statistics(dve, b, name, source, st):
            wait(dve, q[name + "_mv"], b * NT)
            for n in range(NT):
                dve.bn_stats(st[:, n, :], source[:, b * NT + n, :]).then_inc(q[name + "_stats"], 1)

        def dve_moments(dve, b, name, st, mean_var):
            dve.wait_ge(q[name + "_stats"], (b + 1) * NT)
            wait(dve, q[name + "_norm"], b)
            for n in range(NT):
                dve.bn_aggr(mean_var[:, n, :], st[:, n, :]).then_inc(q[name + "_mv"], 1)

        def pool_root_and_shift(pool, b, name, mean_var, small):
            pool.wait_ge(q[name + "_mv"], (b + 1) * NT)
            wait(pool, q[name + "_norm"], b)
            pool.tensor_scalar(small[:, 0, :], mean_var[:, :, 1], LN_EPS, None, ALU.add).then_inc(q[name + "_var"], 1)
            pool.tensor_scalar(small[:, 1, :], mean_var[:, :, 0], -1.0, None, ALU.mult).then_inc(q[name + "_less_mean"], 1)
            pool.wait_ge(q[name + "_var"], b + 1)
            pool.tensor_tensor(small[:, 2, :], small[:, 0, :], halfneg[:, 0:NT], ALU.pow).then_inc(q[name + "_rstd"], 1)
            pool.wait_ge(q[name + "_rstd"], b + 1)
            pool.wait_ge(q[name + "_less_mean"], b + 1)
            pool.tensor_tensor(small[:, 3, :], small[:, 1, :], small[:, 2, :], ALU.mult).then_inc(q[name + "_shift"], 1)

        def act_normalise(act, b, name, source, small, xn, used):
            act.wait_ge(q[name + "_shift"], b + 1)
            wait(act, q[used], b)
            for n in range(NT):
                ins = act.activation(xn[:, n, :], source[:, b * NT + n, :], ACT.Identity, bias=small[:, 3, n:n + 1],
                                     scale=small[:, 2, n:n + 1])
            ins.then_inc(q[name + "_norm"], 1)

        def dve_head_step(dve, j):
            if j > 0:
                b = j - 1
                dve.wait_ge(q["z_norm"], b + 1)
                dve.wait_ge(mod01_loaded if b < 2 else mod_loaded, 16)
                dve.tensor_tensor(X[:, tile_rows(b), :], z_xn[:, :, :], wide(mod[:, b:b + 1, 1, :]), ALU.mult).then_inc(q["z_scaled"], 1)
            if j < B:
                dve.wait_ge(x_loaded if j else row0_loaded, 16 * (B - 1) if j else 16)
                dve_statistics(dve, j, "z", x0, z_st)
            if j > 0:
                dve.wait_ge(q["z_scaled"], j)
                dve.tensor_tensor(X[:, tile_rows(j - 1), :], X[:, tile_rows(j - 1), :], wide(mod[:, j - 1:j, 0, :]), ALU.add
                                  ).then_inc(x_ready, NT)
            if j < B:
                dve_moments(dve, j, "z", z_st, z_mean_var)

        def pool_head_step(pool, j):
            if j < B:
                pool_root_and_shift(pool, j, "z", z_mean_var, z_small)

        def act_head_step(act, j):
            if j < B:
                act_normalise(act, j, "z", x0, z_small, z_xn, "z_scaled")

        def dve_tail_step(dve, j):
            if j < B:
                dve.wait_ge(x_ready, LAST - TILES + (j + 1) * NT)
                dve_statistics(dve, j, "f", X, f_st)
                dve_moments(dve, j, "f", f_st, f_mean_var)
            if 0 <= j - 1 < B:
                b = j - 1
                dve.wait_ge(q["f_norm"], b + 1)
                dve.wait_ge(q["gf_ga_ready"], 1)
                dve.tensor_tensor(X[:, tile_rows(b), :], f_xn[:, :, :], wide(mod[:, b:b + 1, 2, :]), ALU.mult
                                  ).then_inc(q["f_gain"], 1)
                dve.wait_ge(q["x0_shifted"], b + 1)
                dve.wait_ge(q["f_gain"], b + 1)
                dve.tensor_tensor(X[:, tile_rows(b), :], X[:, tile_rows(b), :], x0[:, tile_rows(b), :], ALU.add
                                  ).then_inc(q["x2_ready"], 1)
                dve.wait_ge(q["x2_ready"], b + 1)
                dve_statistics(dve, b, "g", X, g_st)
            if 0 <= j - 2 < B:
                b = j - 2
                dve.wait_ge(q["g_norm"], b + 1)
                dve.tensor_tensor(Hr[:, tile_rows(b), :], g_xn[:, :, :], wide(mod[:, b:b + 1, 4, :]), ALU.mult
                                  ).then_inc(q["g_scaled"], 1)
            if 0 <= j - 1 < B:
                dve_moments(dve, j - 1, "g", g_st, g_mean_var)
            if 0 <= j - 2 < B:
                b = j - 2
                dve.wait_ge(q["g_scaled"], b + 1)
                dve.tensor_tensor(Hr[:, tile_rows(b), :], Hr[:, tile_rows(b), :], wide(mod[:, b:b + 1, 3, :]), ALU.add
                                  ).then_inc(q["h_ready"], 1)

        def pool_tail_step(pool, j):
            if j < B:
                pool_root_and_shift(pool, j, "f", f_mean_var, f_small)
            if 0 <= j - 1 < B:
                pool_root_and_shift(pool, j - 1, "g", g_mean_var, g_small)

        def shift_input(pool, k, s):
            if (k, s) == (0, 1):
                pool.wait_ge(par_loaded, 16 * 7)
                pool.wait_ge(mod01_loaded, 16)
                pool.wait_ge(mod_loaded, 16)
                pool.tensor_tensor(bef_ga[:, :, :], mod[:, :, 2, :], gfb[:, 1:2, :].to_broadcast([P, B, D]), ALU.mult
                                   ).then_inc(q["bef_ga_ready"], 1)
            if (k, s) == (0, 3):
                pool.wait_ge(q["bef_ga_ready"], 1)
                pool.tensor_tensor(mod[:, :, 2, :], mod[:, :, 2, :], gfb[:, 0:1, :].to_broadcast([P, B, D]), ALU.mult
                                   ).then_inc(q["gf_ga_ready"], 1)
            if k >= 2:
                if (k, s) == (2, 0):
                    pool.wait_ge(q["bef_ga_ready"], 1)
                b = NT * (k - 2) + s
                pool.wait_ge(q["z_norm"], b + 1)
                pool.tensor_tensor(x0[:, tile_rows(b), :], x0[:, tile_rows(b), :], wide(bef_ga[:, b:b + 1, :]), ALU.add).then_inc(q["x0_shifted"], 1)

        def act_tail_step(act, j):
            if j == 0:
                act.wait_ge(qk_ready, TILES * L)
                act.wait_ge(qkv_ps, TILES * L)
            if j < B:
                act_normalise(act, j, "f", X, f_small, f_xn, "f_gain")
            if 0 <= j - 1 < B:
                act_normalise(act, j - 1, "g", X, g_small, g_xn, "g_scaled")
            b = j - 3
            if 0 <= b < B:
                act.wait_ge(q["ht_ps"], b + 1)
                act.activation(hT_all[:, b * S:(b + 1) * S], ps[:, 3, :], ACT.Copy).then_inc(q["ht_sb"], 1)
                act.wait_ge(q["lg_ps"], b + 1)
                act.activation(lg[:, tile_rows(b), :].rearrange("p t e -> p (t e)"), ps[:, 0, 0:NT * E], ACT.Copy).then_inc(q["lg_sb"], 1)

        def pe_tail_step(pe, j):
            b = j - 3
            if not 0 <= b < B:
                return
            if b == 0:
                pe.wait_ge(q["sw_loaded"], 16 * 6)
                pe.wait_ge(v_sb, TILES * L)
                pe.wait_ge(p_done, TILES * L)
            pe.wait_ge(q["h_ready"], b + 1)
            wait(pe, q["ht_sb"], b)
            for n in range(NT):
                mm = pe.transpose(ps[:, 3, n * P:(n + 1) * P], Hr[:, b * NT + n, :], ident[:, :])
            mm.then_inc(q["ht_ps"], 1)
            pe.wait_ge(q["ht_sb"], b + 1)
            wait(pe, q["lg_sb"], b)
            for n in range(NT):
                o = ps[:, 0, n * E:(n + 1) * E]
                pe.matmul(o, ones3[:, :], rb3, start=True, stop=False)
                mm = pe.matmul(o, hT_all[:, (b * NT + n) * P:(b * NT + n + 1) * P], rw[:, :], start=False, stop=True)
            mm.then_inc(q["lg_ps"], 1)

        route_steps = [0]

        def dve_route(dve, half):
            part = slice(half * TH, (half + 1) * TH)
            logits, probs, room_a = lg[:, part, :], pr[:, part, :], ra[:, part, :]

            def then(ins):
                route_steps[0] += 1
                ins.then_inc(q["route_step"], 1)
                dve.wait_ge(q["route_step"], route_steps[0])

            def over_experts(a):
                return a.unsqueeze(2).to_broadcast([P, TH, E])

            def over_tiles(a):
                return a[:, :].unsqueeze(1).to_broadcast([P, TH, E])

            def twice(a):
                return a.unsqueeze(1).to_broadcast([P, 2, TH, E])

            dve.wait_ge(q["lg_sb"], (half + 1) * B // 2)
            then(dve.tensor_reduce(rmax[:, part], logits, AXX, ALU.max))
            dve.tensor_tensor(room_a, logits, over_experts(rmax[:, part]), ALU.subtract).then_inc(q["lg_shift"], 1)
            dve.wait_ge(q["lg_exp"], half + 1)
            then(dve.tensor_reduce(rsum[:, part], probs, AXX, ALU.add))
            then(dve.reciprocal(rsum[:, part], rsum[:, part]))
            then(dve.tensor_tensor(probs, probs, over_experts(rsum[:, part]), ALU.mult))
            for k in range(2):
                largest = prob[:, k, part]
                then(dve.tensor_reduce(largest, probs, AXX, ALU.max))
                then(dve.tensor_tensor(room_a, probs, over_experts(largest), ALU.is_ge))
                then(dve.tensor_tensor(room_a, room_a, over_tiles(rank16), ALU.mult))
                then(dve.tensor_reduce(first_at[:, part], room_a, AXX, ALU.max))
                then(dve.tensor_tensor(oh[:, k, part, :], room_a, over_experts(first_at[:, part]), ALU.is_equal))
                if k == 0:
                    then(dve.scalar_tensor_tensor(out=probs, in0=oh[:, 0, part, :], scalar=-2.0, in1=probs,
                                                  op0=ALU.mult, op1=ALU.add))
            dve.tensor_tensor(selb[:, part, :], oh[:, 0, part, :], oh[:, 1, part, :], ALU.add).then_inc(q["cnt_ready"], 1)
            then(dve.tensor_tensor(rsum[:, part], prob[:, 0, part], prob[:, 1, part], ALU.add))
            then(dve.tensor_scalar(rsum[:, part], rsum[:, part], 1e-9, None, ALU.add))
            then(dve.reciprocal(rsum[:, part], rsum[:, part]))
            then(dve.tensor_tensor(tmp2[:, :, part], prob[:, :, part], rsum[:, part].unsqueeze(1).to_broadcast([P, 2, TH]), ALU.mult))
            dve.wait_ge(q["cnt_ps"], half + 1)
            before = ps[:, 6, half * TH * E:(half + 1) * TH * E].rearrange("p (t e) -> p t e", e=E)
            dve.tensor_scalar(probs, before, float(CAP), None, ALU.is_lt)
            then(dve.scalar_tensor_tensor(out=room_a, in0=before, scalar=float(CAP - 1), in1=over_tiles(expert_base),
                                          op0=ALU.min, op1=ALU.add))
            then(dve.tensor_tensor(picked, oh[:, :, part, :], twice(probs), ALU.mult))
            then(dve.tensor_reduce(keep[:, :, part], picked, AXX, ALU.add))
            then(dve.tensor_tensor(picked, oh[:, :, part, :], twice(room_a), ALU.mult))
            then(dve.tensor_reduce(slot[:, :, part], picked, AXX, ALU.add))
            then(dve.tensor_tensor(wgt[:, :, part], tmp2[:, :, part], keep[:, :, part], ALU.mult))
            dve.tensor_copy(gath_u[:, part, :].rearrange("p t k -> p k t"), slot[:, :, part])
            then(dve.tensor_tensor(tmp2[:, :, part], trash[:, :, part], slot[:, :, part], ALU.subtract))
            then(dve.tensor_tensor(tmp2[:, :, part], tmp2[:, :, part], keep[:, :, part], ALU.mult))
            then(dve.tensor_tensor(tmp2[:, :, part], trash[:, :, part], tmp2[:, :, part], ALU.subtract))
            dve.tensor_copy(scat_u[:, part, :].rearrange("p t k -> p k t"), tmp2[:, :, part]).then_inc(q["route_ready"], 1)

        def act_route(act, half):
            part = slice(half * TH, (half + 1) * TH)
            act.wait_ge(q["lg_shift"], half + 1)
            act.activation(pr[:, part, :], ra[:, part, :], ACT.Exp).then_inc(q["lg_exp"], 1)

        def pe_route(pe, half):
            if half == 0:
                pe.wait_ge(y1_done, TILES * L)
                pe.wait_ge(y2_done, TILES * L)
                pe.wait_ge(att_t_sb, TILES * L)
                pe.wait_ge(x1t_sb, TILES * L)
            pe.wait_ge(q["cnt_ready"], half + 1)
            first_tile, last_tile = half * TH, (half + 1) * TH
            counts = ps[:, 6, first_tile * E:last_tile * E]
            pe.matmul(counts, tri_before[:, :], selb[:, first_tile:last_tile, :].rearrange("p t e -> p (t e)"), start=True, stop=False)
            for t in range(last_tile - 1):
                later = max(t + 1, first_tile)
                mm = pe.matmul(ps[:, 6, later * E:last_tile * E].rearrange("p (t e) -> p t e", e=E), ones_bf[:, :],
                               selb[:, t:t + 1, :].to_broadcast([P, last_tile - later, E]), start=False, stop=(t == last_tile - 2))
            mm.then_inc(q["cnt_ps"], 1)

        def pool_tail(pool):
            pool.wait_ge(q["xe_zeroed"], 16 * E)

            def indices(source, b, par, count):
                pool.tensor_copy(idx_s[:, par, :].rearrange("p (t k) -> p t k", k=2),
                                 source[:, ds(b * NT, NT), :]).then_inc(q["idx_ready"], 1)
                wait_apart(pool, q["idx_ready"], count, consts_ready)

            def scatter_rows(r):
                b = even(r)
                for par in range(2):
                    pool.wait_ge(hs2_load[par], b * 8 + 16)
                    wait(pool, scat[par], b * 64)
                    indices(scat_u, b + par, par, b + par + 1)
                    for n in range(NT):
                        for k in range(2):
                            pool.indirect_dma_start(
                                out=xe_dram, out_offset=bass.IndirectOffsetOnAxis(ap=idx_s[:, par, 2 * n + k:2 * n + k + 1], axis=0),
                                in_=hs2[:, par, n, :], in_offset=None).then_inc(scat[par], 16)
            pool.wait_ge(q["route_ready"], 1)
            for b in range(0, B // 2, 2):
                scatter_rows(b)
            pool.wait_ge(q["route_ready"], 2)
            with pool.Fori(B // 2, B, 2) as r:
                scatter_rows(r)

            pool.wait_ge(xt_ps, TILES * L)

            def add_h(i):
                wait_apart(pool, q["xsh_done"], i + 4, consts_ready, (q["xh_ready"], i // NT))
                pool.tensor_tensor(gh[:, :, :], rows_of(Hr, i), modulation(i, 5), ALU.mult).then_inc(q["gh_done"], 1)
                wait_apart(pool, q["gh_done"], i // NT + 1, consts_ready)
                pool.tensor_tensor(rows_of(X, i), rows_of(X, i), gh[:, :, :], ALU.add).then_inc(q["xh_ready"], 1)
            rows(pool, add_h)

            for par in range(2):
                pool.wait_ge(scat[par], 64 * B)
                pool.wait_ge(ye_store[par], 16 * (E // 2))

            def gather_rows(r):
                b = even(r)
                for par in range(2):
                    wait(pool, gat[par], b * 64)
                    wait(pool, out_ready[par], b // 2)
                    indices(gath_u, b + par, par, B + b + par + 1)
                    for n in range(NT):
                        for k in range(2):
                            pool.indirect_dma_start(
                                out=yg[:, par, 2 * n + k, :], out_offset=None, in_=ye_dram,
                                in_offset=bass.IndirectOffsetOnAxis(ap=idx_s[:, par, 2 * n + k:2 * n + k + 1], axis=0)
                            ).then_inc(gat[par], 16)
            rows(pool, gather_rows, 2, B)

        def pe_tail(pe):
            def gate_up(rhs, weights, columns, use):
                wait_apart(pe, q["esa_done"], use, consts_ready)
                pe.matmul(ps[:, 0, 0:columns], weights[:, 0:P], rhs, start=True, stop=True).then_inc(q["ga_ps"], 1)
                wait_apart(pe, q["ehb_done"], use, consts_ready)
                pe.matmul(ps[:, 1, 0:columns], weights[:, P:2 * P], rhs, start=True, stop=True).then_inc(q["gub_ps"], 1)
                wait_apart(pe, q["eha_done"], use, consts_ready)
                pe.matmul(ps[:, 2, 0:columns], weights[:, 2 * P:], rhs, start=True, stop=True).then_inc(q["ua_ps"], 1)

            def shared(i):
                gate_up(hT_all[:, ds(first(i) * P, S)], swg, S, i // NT)

            def shared_down(i):
                pe.wait_ge(q["eha_done"], i // NT + 1)
                pe.wait_ge(q["ehb_done"], i // NT + 1)
                wait(pe, q["ysh_done"], i)
                for n in range(NT):
                    o = ps[:, 5, n * P:(n + 1) * P]
                    pe.matmul(o, hid_a[:, n * P:(n + 1) * P], swd[:, 0, :], start=True, stop=False)
                    mm = pe.matmul(o, hid_b[0:FB, n * P:(n + 1) * P], swd[0:FB, 1, :], start=False, stop=True)
                mm.then_inc(q["shd_ps"], 4)

            def shared_step(i):
                shared(i)
                shared_down(i - NT)

            shared(0)
            shared_step(NT)
            with pe.Fori(2 * NT, TILES, NT) as i:
                shared_step(i)
            shared_down(TILES - NT)

            def transposes(e, par):
                pe.wait_ge(xe_load[par], ((e - par) // 2 + 1) * 16)
                wait(pe, q["xet_sb"], e)
                for j in range(CT):
                    mm = pe.transpose(tile_bank[:, j // 4, (j % 4) * P:(j % 4 + 1) * P], xes[:, par, j * P:(j + 1) * P], ident[:, :])
                mm.then_inc(q["xet_ps"], 1)

            def hidden(e, par, half):
                if half == 0:
                    pe.wait_ge(q["xet_sb"], e + 1)
                    pe.wait_ge(ew_load[par], ((e - par) // 2 + 1) * 16 * 3)
                gate_up(xeT[:, par, half * HC:(half + 1) * HC], ewg[:, par], HC, B + 2 * e + half)

            def down(e, par):
                pe.wait_ge(q["eha_done"], B + 2 * e + 2)
                pe.wait_ge(q["ehb_done"], B + 2 * e + 2)
                pe.wait_ge(ewd_load[par], ((e - par) // 2 + 1) * 16 * 2)
                wait(pe, q["ye_sb"], e)
                for j in range(CT):
                    o = down_bank[:, j // 4, (j % 4) * P:(j % 4 + 1) * P]
                    pe.matmul(o, ehid_a[:, par, j * P:(j + 1) * P], ewd[:, par, 0, :], start=True, stop=False)
                    mm = pe.matmul(o, ehid_b[0:FB, par, j * P:(j + 1) * P], ewd[0:FB, par, 1, :], start=False, stop=True)
                mm.then_inc(q["ye_ps"], 1)

            pe.wait_ge(q["ysh_done"], TILES)
            transposes(0, 0)

            def expert(e, par):
                hidden(e, par, 0)
                if not isinstance(e, int) or e > 0:
                    down(e - 1, 1 - par)
                if not isinstance(e, int) or e < E - 1:
                    transposes(e + 1, 1 - par)
                hidden(e, par, 1)
            experts(pe, expert)
            down(E - 1, 1)

        def act_tail(act):
            def shared_gates(r):
                act.wait_ge(q["ga_ps"], r + 1)
                wait(act, q["eha_done"], r)
                act.activation(sil_a[:, :], ps[:, 0, :], ACT.Silu).then_inc(q["esa_done"], 1)
                act.wait_ge(q["gub_ps"], r + 1)
                wait(act, q["ehb_done"], r)
                act.activation(sil_b[0:FB, :], ps[0:FB, 1, :], ACT.Silu).then_inc(q["esb_done"], 1)
            rows(act, shared_gates, 1, B)

            def turned(e, par):
                act.wait_ge(q["xet_ps"], e + 1)
                wait(act, q["ua_ps"], B + 2 * e - 2)
                act.activation(xeT[:, par, 0:4 * P], tile_bank[:, 0, :], ACT.Copy)
                act.activation(xeT[:, par, 4 * P:CAP], tile_bank[:, 1, 0:CAP - 4 * P], ACT.Copy).then_inc(q["xet_sb"], 1)

            def gates(e, half):
                use = B + 2 * e + half
                act.wait_ge(q["ga_ps"], use + 1)
                wait(act, q["eha_done"], use)
                act.activation(esil_a[:, :], ps[:, 0, 0:HC], ACT.Silu).then_inc(q["esa_done"], 1)
                act.wait_ge(q["gub_ps"], use + 1)
                wait(act, q["ehb_done"], use)
                act.activation(esil_b[0:FB, :], ps[0:FB, 1, 0:HC], ACT.Silu).then_inc(q["esb_done"], 1)

            def store(e, par):
                act.wait_ge(q["ye_sb"], e + 1)
                act.dma_start(ye_tiles[ds(e, 1)].rearrange("a p c -> (a p) c"), yes[:, par, :]).then_inc(ye_store[par], 16)

            turned(0, 0)

            def expert(e, par):
                gates(e, 0)
                if not isinstance(e, int) or e < E - 1:
                    turned(e + 1, 1 - par)
                gates(e, 1)
                if not isinstance(e, int) or e > 0:
                    store(e - 1, 1 - par)
            experts(act, expert)
            store(E - 1, 1)

        def dve_tail(dve):
            def shared_hidden(r):
                dve.wait_ge(q["esb_done"], r + 1)
                dve.wait_ge(q["gub_ps"], r + 1)
                wait(dve, q["shd_ps"], r * NT)
                dve.tensor_tensor(hid_b[0:FB, :], sil_b[0:FB, :], ps[HB:HB + FB, 1, :], ALU.mult).then_inc(q["ehb_done"], 1)
                dve.wait_ge(q["esa_done"], r + 1)
                dve.wait_ge(q["ua_ps"], r + 1)
                dve.tensor_tensor(hid_a[:, :], sil_a[:, :], ps[:, 2, :], ALU.mult).then_inc(q["eha_done"], 1)

            def shared_out(i):
                dve.wait_ge(q["shd_ps"], i + 4)
                wait(dve, q["xsh_done"], i)
                dve.tensor_tensor(ysh[:, :, :], ps[:, 5, :].rearrange("p (n d) -> p n d", d=D), modulation(i, 5), ALU.mult
                                  ).then_inc(q["ysh_done"], 4)
                dve.wait_ge(q["ysh_done"], i + 4)
                dve.tensor_tensor(rows_of(X, i), rows_of(X, i), ysh[:, :, :], ALU.add).then_inc(q["xsh_done"], 4)

            shared_hidden(0)
            dve.wait_ge(q["g_norm"], B)
            shared_hidden(1)
            shared_out(0)
            with dve.Fori(2 * NT, TILES, NT) as i:
                shared_hidden(i // NT)
                shared_out(i - NT)
            shared_out(TILES - NT)

            def finish(e, par):
                dve.wait_ge(q["ye_ps"], e + 1)
                wait(dve, ye_store[par], ((e - par) // 2) * 16)
                dve.tensor_copy(yes[:, par, 0:4 * P], down_bank[:, 0, :])
                dve.tensor_copy(yes[:, par, 4 * P:CAP], down_bank[:, 1, 0:CAP - 4 * P]).then_inc(q["ye_sb"], 1)

            def expert(e, par):
                for half in range(2):
                    if half == 1 and (not isinstance(e, int) or e > 0):
                        finish(e - 1, 1 - par)
                    use = B + 2 * e + half
                    part = slice(half * HC, (half + 1) * HC)
                    dve.wait_ge(q["esb_done"], use + 1)
                    dve.wait_ge(q["gub_ps"], use + 1)
                    wait(dve, q["ye_ps"], e - 1)
                    dve.tensor_tensor(ehid_b[0:FB, par, part], esil_b[0:FB, :], ps[HB:HB + FB, 1, 0:HC], ALU.mult).then_inc(q["ehb_done"], 1)
                    dve.wait_ge(q["esa_done"], use + 1)
                    dve.wait_ge(q["ua_ps"], use + 1)
                    dve.tensor_tensor(ehid_a[:, par, part], esil_a[:, :], ps[:, 2, 0:HC], ALU.mult).then_inc(q["eha_done"], 1)
            experts(dve, expert)
            finish(E - 1, 1)

            dve.wait_ge(q["xh_ready"], B)

            def mix_rows(r):
                b = even(r)
                for par in range(2):
                    base = (b + par) * NT
                    dve.wait_ge(gat[par], b * 64 + 128)
                    wait(dve, q["mixg_done"], b + par)
                    for n in range(NT):
                        dve.tensor_scalar(ymix[:, n, :], yg[:, par, 2 * n, :], wgt[:, 0, ds(base + n, 1)], None, ALU.mult
                                          ).then_inc(q["mix1_done"], 1)
                    for n in range(NT):
                        dve.wait_ge(q["mix1_done"], b * 4 + par * 4 + n + 1)
                        dve.scalar_tensor_tensor(out=ymix[:, n, :], in0=yg[:, par, 2 * n + 1, :], scalar=wgt[:, 1, ds(base + n, 1)],
                                                 in1=ymix[:, n, :], op0=ALU.mult, op1=ALU.add).then_inc(q["mix2_done"], 1)
                    dve.wait_ge(q["mix2_done"], b * 4 + par * 4 + 4)
                    wait(dve, out_store[par], b * 8)
                    dve.tensor_tensor(yout[:, par, :, :], ymix[:, :, :], mod[:, ds(b + par, 1), 5, :].to_broadcast([P, NT, D]), ALU.mult
                                      ).then_inc(q["mixg_done"], 1)
                    dve.wait_ge(q["mixg_done"], b + par + 1)
                    dve.tensor_tensor(yout[:, par, :, :], yout[:, par, :, :], X[:, ds(base, NT), :], ALU.add).then_inc(out_ready[par], 1)
            rows(dve, mix_rows, 2, B)

        block = ctx.enter_context(nc.Block())

        @block.sync
        def _(sp):
            sp.dma_start(cT[:, :], c.rearrange("b d -> d b"), allow_slow_non_contiguous=True).then_inc(c_loaded, 16)
            sp.dma_start(wmod_s[:, :], wmod).then_inc(c_loaded, 16)
            sp.dma_start(x0[:, 0:NT, :], x_v[0]).then_inc(row0_loaded, 16)
            for n, w in enumerate((Wq, Wk, Wv)):
                sp.dma_start(wqkv[:, :, n * D:(n + 1) * D], w.rearrange("l k n -> k l n")).then_inc(qkv_loaded, 16)
            for b in range(1, B):
                sp.dma_start(x0[:, b * NT:(b + 1) * NT, :], x_v[b]).then_inc(x_loaded, 16)
            sp.wait_ge(mod8_ready, 1)
            sp.dma_start(mod_dram, mod8[:, :]).then_inc(mod_stored, 16)
            sp.wait_ge(mod_stored, 16)
            sp.dma_start(mod[:, 0:2, :, :].rearrange("p b m d -> p (b m d)"),
                         mod_dram[0:2, :].rearrange("(a b) n -> a (b n)", a=1).to_broadcast([P, 2 * MODS])
                         ).then_inc(mod01_loaded, 16)
            sp.wait_ge(bias_split, 3)
            for r in range(3):
                sp.dma_start(bias3[r:r + 1, :], bias_parts[:, r, :]).then_inc(bias_ready, 16)

            def first_loads(k):
                if k == -1:
                    sp.dma_start(mod[:, 2:B, :, :].rearrange("p b m d -> p (b m d)"),
                                 mod_dram[2:B, :].rearrange("(a b) n -> a (b n)", a=1).to_broadcast([P, (B - 2) * MODS])
                                 ).then_inc(mod_loaded, 16)
                    sp.dma_start(wo[:, :, :], Wo.rearrange("l k n -> k l n")).then_inc(par_loaded, 16)
                    for n, g in enumerate((g1, be1, g2, be2)):
                        sp.dma_start(gains[:, n, :, :].rearrange("p l d -> p (l d)"),
                                     g.rearrange("(a l) d -> a (l d)", a=1).to_broadcast([P, L * D])).then_inc(par_loaded, 16)
                    for n, g in enumerate((gf, bef)):
                        sp.dma_start(gfb[:, n, :], g.rearrange("(a d) -> a d", a=1).to_broadcast([P, D])).then_inc(par_loaded, 16)
                if k == 0:
                    sp.dma_start(w1[:, :, :], W1.rearrange("l k n -> k l n")).then_inc(w12_loaded, 16)
                    sp.dma_start(w2[:, :, :, :].rearrange("p l c n -> p (l c) n"),
                                 W2.rearrange("l (c p) n -> p (l c) n", p=P)).then_inc(w12_loaded, 16)
                    sp.dma_start(rw[:, :], router_w).then_inc(q["sw_loaded"], 16)
                    sp.dma_start(swg[:, 0:F], sw_gate).then_inc(q["sw_loaded"], 16)
                    sp.dma_start(swg[:, 2 * P:], sw_up[:, 0:FA]).then_inc(q["sw_loaded"], 16)
                    sp.dma_start(swg[:, P + HB:P + HB + FB], sw_up[:, FA:F]).then_inc(q["sw_loaded"], 16)
                    sp.dma_start(swd[:, 0, :], sw_down[0:FA, :]).then_inc(q["sw_loaded"], 16)
                    sp.dma_start(swd[0:FB, 1, :], sw_down[FA:F, :]).then_inc(q["sw_loaded"], 16)
                if k >= 0:
                    sp.wait_ge(q["zrow_ready"], 1)
                    for e in range(k * E // NT, (k + 1) * E // NT):
                        sp.dma_start(xe_tiles[e], zrow[:, :]).then_inc(q["xe_zeroed"], 16)

            def step(i):
                if active(i, -1) and not is_first(i):
                    wait_apart(sp, x_ready, i + 8, mod_stored)
                    wait(sp, xt_ps, i + 4)
                    row = tile_of(i, -1, 0)
                    sp.dma_start(xs[:, :, :], X[:, ds(row, NT), :]).then_inc(xs_load, 16)
                if isinstance(i, int) and i < NT * NT:
                    first_loads(i // NT)
                if active(i, 2):
                    wait_apart(sp, x1_ready, i - 4, mod_stored)
                    wait(sp, x1t_ps, i - 8)
                    row = tile_of(i, 2, 0)
                    sp.dma_start(x1s[:, :, :], X[:, ds(row, NT), :]).then_inc(x1s_load, 16)
                    wait(sp, h_ps, i - 8)
                    if isinstance(i, int) and i == 2 * NT:
                        sp.wait_ge(w12_loaded, 16 * 2)
                    sp.dma_start(w1s[:, :], w1[:, ds(layer_of(i, 2), 1), :].rearrange("p a f -> p (a f)")
                                 ).then_inc(w1_load, 16)
            steps(sp, step, lambda j: None, lambda j: None, lambda half: None)
            sp_tail(sp)

        @block.gpsimd
        def _(pool):
            done = [0]

            def then(ins):
                done[0] += 1
                ins.then_inc(const_step, 1)
                pool.wait_ge(const_step, done[0])

            then(pool.memset(ident[:, :], 0.0))
            pool.affine_select(out=ident[:, :], in_=ident[:, :], compare_op=ALU.not_equal, fill=1.0, base=0,
                               pattern=[[-1, P]], channel_multiplier=1).then_inc(consts_ready, 1)
            then(pool.memset(tri[:, :], 1.0))
            pool.affine_select(out=tri[:, :], in_=tri[:, :], compare_op=ALU.is_ge, fill=0.0, base=0,
                               pattern=[[1, P]], channel_multiplier=-1).then_inc(consts_ready, 1)
            then(pool.memset(tri_before[:, :], 1.0))
            pool.affine_select(out=tri_before[:, :], in_=tri_before[:, :], compare_op=ALU.is_gt, fill=0.0, base=0,
                               pattern=[[1, P]], channel_multiplier=-1).then_inc(consts_ready, 1)
            then(pool.memset(headmask[:, :, :], 1.0))
            then(pool.affine_select(out=headmask[:, :, :], in_=headmask[:, :, :], compare_op=ALU.is_ge, fill=0.0,
                                    base=0, pattern=[[0, EV], [-HD, H]], channel_multiplier=1))
            pool.affine_select(out=headmask[:, :, :], in_=headmask[:, :, :], compare_op=ALU.is_ge, fill=0.0,
                               base=HD - 1, pattern=[[0, EV], [HD, H]], channel_multiplier=-1).then_inc(consts_ready, 1)
            lead, middle, last = bf16_parts(ATT_EPS)
            then(pool.memset(eps3[:, :], lead))
            for r, part in ((1, middle), (2, last)):
                then(pool.affine_select(out=eps3[:, :], in_=eps3[:, :], compare_op=ALU.is_gt, fill=part, base=r,
                                        pattern=[[0, SW]], channel_multiplier=-1))
            pool.affine_select(out=eps3[:, :], in_=eps3[:, :], compare_op=ALU.is_ge, fill=0.0, base=-HD * H,
                               pattern=[[1, SW]], channel_multiplier=0).then_inc(consts_ready, 1)
            for a in (swg[:, F:P + HB], swg[:, P + HB + FB:2 * P], ewg[:, :, F:P + HB], ewg[:, :, P + HB + FB:2 * P]):
                pool.memset(a, 0.0).then_inc(consts_ready, 1)
            pool.memset(halfneg[:, :], -0.5).then_inc(consts_ready, 1)
            pool.memset(ones3[:, :], 1.0).then_inc(consts_ready, 1)
            pool.memset(ones_bf[:, :], 1.0).then_inc(consts_ready, 1)
            pool.memset(v1[:, :, HD, :], 1.0).then_inc(consts_ready, 1)
            then(pool.iota(iota_i[:, 0:E], pattern=[[-1, E]], base=E, channel_multiplier=0))
            pool.tensor_copy(rank16[:, :], iota_i[:, 0:E]).then_inc(consts_ready, 1)
            then(pool.iota(iota_i[:, E:2 * E], pattern=[[CAP, E]], base=0, channel_multiplier=0))
            pool.tensor_copy(expert_base[:, :], iota_i[:, E:2 * E]).then_inc(consts_ready, 1)
            then(pool.iota(iota_i[:, 32:96], pattern=[[TOK, 2], [P, TILES]], base=ROWS, channel_multiplier=1))
            pool.tensor_copy(trash[:, :, :].rearrange("p k t -> p (k t)"), iota_i[:, 32:96]).then_inc(consts_ready, 1)

            pool.wait_ge(consts_ready, 16)

            def outer(i, n):
                wait(pool, qk_ready, i + n + 1)
                wait(pool, v_sb, i + n + 1)
                wait(pool, cum_ps, i + n - 3)
                pool.tensor_tensor(
                    kv[:, n, :].rearrange("p (e h d) -> p e h d", e=EV, h=H),
                    qk[:, n, 1, :].rearrange("p (h d) -> p h d", h=H).unsqueeze(1).to_broadcast([P, EV, H, HD]),
                    v1[:, n, :, :].unsqueeze(3).to_broadcast([P, EV, H, HD]),
                    ALU.mult).then_inc(kv_ready, 1)

            def step(i):
                if isinstance(i, int) and i == NT:
                    pool.wait_ge(par_loaded, 16 * 7)
                for s in range(4):
                    if active(i, 1):
                        w, par = i + s - 4, s % 2
                        wait_apart(pool, mv1_done, w + 1, consts_ready)
                        pool.tensor_scalar(var1[:, par:par + 1], mv1[:, par, 1:2], LN_EPS, None, ALU.add).then_inc(var1_ready, 1)
                        wait(pool, var1_ready, w + 1)
                        wait(pool, norm1_done, w - 1)
                        pool.tensor_tensor(rstd1[:, par:par + 1], var1[:, par:par + 1], halfneg[:, 0:1], ALU.pow
                                           ).then_inc(rstd1_ready, 1)
                        wait_apart(pool, rstd1_ready, w + 1, consts_ready)
                        pool.tensor_scalar(shift1[:, par:par + 1], mv1[:, par, 0:1], rstd1[:, par:par + 1], -1.0,
                                           ALU.mult, ALU.mult).then_inc(shift1_ready, 1)
                    if active(i, 0):
                        outer(i, s)
                    if s == 2 and active(i, 3):
                        wait_apart(pool, mv2_done, i - 8, consts_ready, (norm2_done, i - 12))
                        pool.tensor_scalar(var2[:, :], mv2[:, :, 1], LN_EPS, None, ALU.add).then_inc(var2_ready, 4)
                        pool.tensor_scalar(less_mean2[:, :], mv2[:, :, 0], -1.0, None, ALU.mult).then_inc(less_mean2_ready, 4)
                        wait(pool, var2_ready, i - 8)
                        pool.tensor_tensor(rstd2[:, :], var2[:, :], halfneg[:, 0:NT], ALU.pow).then_inc(rstd2_ready, 4)
                        wait(pool, rstd2_ready, i - 8)
                        wait(pool, less_mean2_ready, i - 8)
                        pool.tensor_tensor(shift2[:, :], less_mean2[:, :], rstd2[:, :], ALU.mult).then_inc(shift2_ready, 4)
                    if active(i, 1):
                        layer = layer_of(i, 1)
                        wait_apart(pool, norm1_done, w + 1, consts_ready)
                        pool.tensor_tensor(xg1[:, :], xn1[:, par, :], gains[:, 0, ds(layer, 1), :].rearrange("p a d -> p (a d)"), ALU.mult
                                           ).then_inc(xg1_done, 1)
                        wait_apart(pool, xg1_done, w + 1, consts_ready)
                        pool.tensor_tensor(X[:, ds(tile_of(i, 1, s), 1), :].rearrange("p a d -> p (a d)"), xg1[:, :],
                                           gains[:, 1, ds(layer, 1), :].rearrange("p a d -> p (a d)"), ALU.add).then_inc(x1_ready, 1)
                    if s == 3 and active(i, 3):
                        layer = layer_of(i, 3)
                        wait_apart(pool, norm2_done, i - 8, consts_ready)
                        pool.tensor_tensor(xg2[:, :, :], xn2[:, :, :],
                                           gains[:, 2, ds(layer, 1), :].to_broadcast([P, NT, D]), ALU.mult
                                           ).then_inc(xg2_done, 4)
                        wait_apart(pool, xg2_done, i - 8, consts_ready)
                        pool.tensor_tensor(X[:, ds(tile_of(i, 3, 0), NT), :], xg2[:, :, :],
                                           gains[:, 3, ds(layer, 1), :].to_broadcast([P, NT, D]), ALU.add
                                           ).then_inc(x_ready, 4)
                    if head_row(i, s):
                        pool_head_step(pool, head_row(i, s))
                    if isinstance(i, int) and 0 <= i < 4 * NT:
                        shift_input(pool, i // NT, s)
            steps(pool, step, lambda j: pool_head_step(pool, j), lambda j: pool_tail_step(pool, j), lambda half: None)
            pool_tail(pool)

        @block.tensor
        def _(pe):
            pe.wait_ge(c_silu, 1)
            pe.wait_ge(c_loaded, 32)
            for n in range(2):
                mm = pe.matmul(ps[0:B, n, 0:NB], csT[:, :], wmod_s[:, n * NB:(n + 1) * NB], start=True, stop=True)
            mm.then_inc(mod_ps, 1)

            pe.wait_ge(consts_ready, 16)

            def qkv(i, n):
                if isinstance(i, int) and i == 0 and n == 0:
                    pe.wait_ge(qkv_loaded, 16 * 3)
                    pe.wait_ge(bias_ready, 16 * 3)
                wait_apart(pe, v_sb, i + n, consts_ready)
                if n == 0:
                    wait(pe, xt_sb, i + 4)
                layer = layer_of(i, 0)
                pe.matmul(ps_qkv.rearrange("p (n d) -> p n d", n=3), ones3[:, :], bias3_l[:, 0:3, ds(layer, 1), :].rearrange("r n a d -> r n (a d)"), start=True, stop=False)
                pe.matmul(ps_qkv, xT[:, n, :], wqkv[:, ds(layer, 1), :].rearrange("p a c -> p (a c)"), start=False, stop=True
                          ).then_inc(qkv_ps, 1)

            def attend(T, n, t_bank_free):
                wait(pe, qk_ready, T + 1)
                wait(pe, *t_bank_free)
                pe.transpose(ps_t[:, 0:P], qk[:, n, 0, :], ident[:, :]).then_inc(qt_ps, 1)
                wait(pe, kv_ready, T + 1)
                wait(pe, p_done, T)
                for j in range(3):
                    mm = pe.matmul(ps_cum[:, j, :], tri[:, :], kv[:, n, j * CB:(j + 1) * CB], start=True, stop=True)
                mm.then_inc(cum_ps, 1)
                wait(pe, qt_sb, T + 1)
                wait(pe, tot_done, T)
                mm = pe.matmul(ps_s[:, 0:SW], ones3[:, :], eps3[:, :], start=True, stop=(n == 0))
                if n > 0:
                    wait(pe, kvm_ready, T)
                    mm = pe.matmul(ps_s[:, 0:SW], qT[:, :], kvm[:, :], start=False, stop=True)
                if n < NT - 1:
                    wait(pe, v_sb, T + 1)
                    mm = pe.matmul(ps_s[:, SW:2 * SW], qk[:, n, 1, :], v1[:, n, :, :].rearrange("p e h -> p (e h)"), start=True, stop=True)
                mm.then_inc(inter_ps, 1)

            def att_transpose(u):
                wait(pe, att_ready, u + 1)
                wait(pe, qt_sb, u + 2)
                pe.transpose(ps_t[:, 0:P], att[:, :], ident[:, :]).then_inc(att_t_ps, 1)

            def project(i, u, back):
                if isinstance(u, int) and u == 0:
                    pe.wait_ge(par_loaded, 16 * 7)
                wait_apart(pe, att_t_sb, u + 1, consts_ready)
                wait(pe, y1_done, u)
                layer = layer_of(i, back)
                pe.matmul(ps_y[:, 2 * D:3 * D], ones3[:, :], bias3_l[:, 3, ds(layer, 1), :].rearrange("r a c -> r (a c)"), start=True, stop=False)
                pe.matmul(ps_y[:, 2 * D:3 * D], attT[:, :], wo[:, ds(layer, 1), :].rearrange("p a c -> p (a c)"), start=False, stop=True
                          ).then_inc(wo_ps, 1)

            def ffn_out(i, s, u):
                if isinstance(i, int) and i == 3 * NT and s == 0:
                    pe.wait_ge(w12_loaded, 16 * 2)
                layer = layer_of(i, 3)
                wait_apart(pe, gelu_done, i - 8, consts_ready, (y1_done, min(u, TILES * L) if isinstance(u, int) else u),
                           (y2_done, i - 12 + 2 * s))
                for m in range(2):
                    n = 2 * s + m
                    o = ps_y[:, m * D:(m + 1) * D]
                    pe.matmul(o, ones3[:, :], bias3_l[:, 4, ds(layer, 1), :].rearrange("r a c -> r (a c)"), start=True, stop=False)
                    for j in range(FC):
                        mm = pe.matmul(o, hT[:, j, n * P:(n + 1) * P], w2[:, ds(layer, 1), j, :].rearrange("p a c -> p (a c)"),
                                       start=False, stop=(j == FC - 1))
                    mm.then_inc(w2_ps, 1)

            def ffn_in(i, j):
                if j == 0:
                    wait(pe, x1t_sb, i - 4)
                    wait(pe, w1_load, (i - 4) * 4)
                wait(pe, gelu_done, i - 8 + j)
                pe.matmul(ps_h, w1s[:, j * P:(j + 1) * P], x1T[:, :], start=True, stop=True).then_inc(h_ps, 1)

            def step(i):
                for s in range(2):
                    T = i - 2 + s
                    u = T - 1
                    if s == 1 and active(i, 2):
                        wait(pe, x1s_load, (i - 4) * 4)
                        wait(pe, att_t_sb, (T - 1) if active(i, 1) else TILES * L)
                        for n in range(NT):
                            mm = pe.transpose(ps_t[:, n * P:(n + 1) * P], x1s[:, n, :], ident[:, :])
                        mm.then_inc(x1t_ps, 4)
                    if active(i, 0):
                        qkv(i, 2 * s)
                    if active(i, 1):
                        attend(T, 2 + s, (att_t_sb, T - 1) if s == 0 or not active(i, 2) else (x1t_sb, i - 4))
                    if active(i, 0):
                        qkv(i, 2 * s + 1)
                    if active(i, 1):
                        att_transpose(u)
                    if active(i, 3):
                        ffn_out(i, s, u)
                    if active(i, 1):
                        project(i, u, 1)
                for s in range(2):
                    T = i + s
                    u = T - 1
                    if active(i, 2):
                        ffn_in(i, 2 * s)
                    if active(i, 0):
                        t_free = (xt_sb, i + 8) if s == 1 and active(i, -1) else (att_t_sb, T - 1)
                        attend(T, s, t_free)
                    if active(i, s == 0):
                        att_last = not active(i, 0)
                        if att_last:
                            wait(pe, att_ready, u + 1)
                            wait(pe, x1t_sb, i - 4)
                            wait(pe, att_t_sb, u)
                            pe.transpose(ps_t[:, 0:P], att[:, :], ident[:, :]).then_inc(att_t_ps, 1)
                        else:
                            att_transpose(u)
                    if active(i, 2):
                        ffn_in(i, 2 * s + 1)
                    if active(i, s == 0):
                        project(i, u, 1 if s == 0 else 0)
                    if s == 0 and active(i, -1):
                        source = X if is_first(i) else xs
                        if is_first(i):
                            pe.wait_ge(x_ready, NT)
                        else:
                            wait(pe, xs_load, (i + 4) * 4)
                        if active(i, 1):
                            wait(pe, att_t_sb, u + 1)
                        elif active(i, 0):
                            wait(pe, qt_sb, i + 1)
                        for n in range(NT):
                            mm = pe.transpose(ps_t[:, n * P:(n + 1) * P], source[:, n, :], ident[:, :])
                        mm.then_inc(xt_ps, 4)
            steps(pe, step, lambda j: None, lambda j: pe_tail_step(pe, j), lambda half: pe_route(pe, half))
            pe_tail(pe)

        @block.scalar
        def _(act):
            act.wait_ge(c_loaded, 32)
            act.activation(csT[:, :], cT[:, :], ACT.Silu).then_inc(c_silu, 1)
            act.dma_start(bias_f[0:1, 0:E], router_b.rearrange("(a d) -> a d", a=1)).then_inc(bias_loaded, 16)
            rows_each = L * D // 32
            for n, v in enumerate((bq, bk, bv, bo, b2)):
                act.dma_start(bias_f[1 + n * rows_each:1 + (n + 1) * rows_each, :], v.rearrange("l (a d) -> (l a) d", d=32)
                              ).then_inc(bias_loaded, 16)
            act.dma_start(b1c[:, :, :].rearrange("p l c -> p (l c)"), b1.rearrange("l (c p) -> p (l c)", p=P),
                          allow_slow_non_contiguous=True).then_inc(b1_loaded, 16)

            act.wait_ge(c_silu, 1)
            act.activation(table_use[:, :], csT[:, 0:1], ACT.Exp)
            act.wait_ge(consts_ready, 16)

            def qkv_out(i, n):
                wait(act, qkv_ps, i + n + 1)
                wait(act, qk_ready, i + n - 1)
                act.activation(ex[:, n % 2, :], ps_qkv[:, 0:2 * D], ACT.Exp)
                act.activation(rl[:, n % 2, :], ps_qkv[:, 0:2 * D], ACT.Relu).then_inc(er_ready, 1)
                wait(act, kv_ready, i + n - 3)
                wait(act, inter_ps, i + n - 3)
                act.activation(v1[:, n, 0:HD, :].rearrange("p e h -> p h e"),
                               ps_qkv[:, 2 * D:3 * D].rearrange("p (h e) -> p h e", h=H), ACT.Copy).then_inc(v_sb, 1)

            def q_out(T):
                wait(act, qt_ps, T + 1)
                wait(act, inter_ps, T)
                act.activation(qT[:, :], ps_t[:, 0:P], ACT.Copy).then_inc(qt_sb, 1)

            def att_out(u):
                wait(act, att_t_ps, u + 1)
                wait(act, wo_ps, u)
                act.activation(attT[:, :], ps_t[:, 0:P], ACT.Copy).then_inc(att_t_sb, 1)

            def fetch_table(function):
                act.activation(table_use[:, :], csT[:, 0:1], function)

            def gelu(i, j):
                wait(act, h_ps, i - 8 + j + 1)
                if j == 0:
                    wait(act, w2_ps, i - 8)
                    if isinstance(i, int) and i == 2 * NT:
                        act.wait_ge(b1_loaded, 16)
                layer = layer_of(i, 2)
                act.activation(hT[:, j, :], ps_h, ACT.Gelu, bias=b1c[:, ds(layer, 1), j]).then_inc(gelu_done, 1)

            def norm1(w, par):
                wait(act, shift1_ready, w + 1)
                wait(act, xg1_done, w - 1)
                act.activation(xn1[:, par, :], y1[:, par, :], ACT.Identity, bias=shift1[:, par:par + 1],
                               scale=rstd1[:, par:par + 1]).then_inc(norm1_done, 1)

            def norm2(i):
                wait(act, xg2_done, i - 12)
                wait(act, shift2_ready, i - 8)
                for n in range(NT):
                    act.activation(xn2[:, n, :], y2[:, n, :], ACT.Identity, bias=shift2[:, n:n + 1],
                                   scale=rstd2[:, n:n + 1]).then_inc(norm2_done, 1)

            def step(i):
                for s in range(2):
                    T = i - 2 + s
                    if s == 1 and active(i, 2):
                        wait(act, x1t_ps, i - 4)
                        wait(act, h_ps, i - 8)
                        act.activation(x1T[:, :], ps_t[:, :], ACT.Copy).then_inc(x1t_sb, 4)
                    if active(i, 1):
                        q_out(T)
                    if active(i, 0):
                        qkv_out(i, 2 * s)
                        qkv_out(i, 2 * s + 1)
                    if active(i, 1):
                        att_out(T - 1)
                        norm1(i + s - 4, s % 2)
                    if isinstance(i, int):
                        j = head_row(i - NT, 3) if s == 0 else head_row(i, 0)
                        if j:
                            act_head_step(act, j)
                if active(i, 0) and active(i, 2):
                    fetch_table(ACT.Gelu)
                for s in range(2):
                    T = i + s
                    if active(i, 0):
                        q_out(T)
                    if active(i, 2):
                        gelu(i, 2 * s)
                    if s == 1 and active(i, 3):
                        norm2(i)
                    if active(i, s == 0):
                        att_out(T - 1)
                    if active(i, 1) and s == 1:
                        norm1(i + s - 2, s % 2)
                    if active(i, 2):
                        gelu(i, 2 * s + 1)
                    if s == 1 and active(i, 0) and active(i, 2):
                        fetch_table(ACT.Exp)
                    if s == 0 and active(i, -1):
                        wait(act, xt_ps, i + 8)
                        wait(act, qkv_ps, i + 4)
                        act.activation(xT[:, :, :].rearrange("p n t -> p (n t)"), ps_t[:, :], ACT.Copy).then_inc(xt_sb, 4)
                    if active(i, 1) and s == 0:
                        norm1(i + s - 2, s % 2)
                    if s == 0 and head_row(i, 1):
                        act_head_step(act, head_row(i, 1))
            steps(act, step, lambda j: act_head_step(act, j), lambda j: act_tail_step(act, j), lambda half: act_route(act, half))
            act_tail(act)

        @block.vector
        def _(dve):
            done = [0]

            def then(ins):
                done[0] += 1
                ins.then_inc(setup_step, 1)
                dve.wait_ge(setup_step, done[0])

            dve_head_step(dve, 0)

            dve.wait_ge(mod_ps, 1)
            for n in range(2):
                then(dve.tensor_copy(mod8[:, n * NB:(n + 1) * NB], ps[0:B, n, 0:NB]))
            m3 = mod8[:, :].rearrange("b (g m d) -> b g m d", g=2, m=3)
            then(dve.tensor_scalar(m3[:, :, 1, :], m3[:, :, 1, :], 1.0, None, ALU.add))
            then(dve.tensor_scalar(gsign[:, :, :], m3[:, :, 2, :], 0.0, 2.0, ALU.is_ge, ALU.mult))
            then(dve.tensor_scalar(gsign[:, :, :], gsign[:, :, :], -1.0, None, ALU.add))
            then(dve.tensor_tensor(m3[:, :, 2, :], m3[:, :, 2, :], gsign[:, :, :], ALU.mult))
            dve.scalar_tensor_tensor(out=m3[:, :, 2, :], in0=m3[:, :, 2, :], scalar=0.25, in1=gsign[:, :, :],
                                     op0=ALU.max, op1=ALU.mult).then_inc(mod8_ready, 1)

            then(dve.memset(bias_f[0:1, E:2 * E], 0.0))
            dve.wait_ge(bias_loaded, 16 * 6)
            for r in range(3):
                dve.tensor_copy(bias_parts[:, r, :], bias_f[:, :]).then_inc(bias_split, 1)
                dve.wait_ge(bias_split, r + 1)
                if r < 2:
                    then(dve.tensor_tensor(bias_f[:, :], bias_f[:, :], bias_parts[:, r, :], ALU.subtract))
            dve.memset(zrow[:, :], 0.0).then_inc(q["zrow_ready"], 1)

            def feature_map(i, n):
                wait(dve, er_ready, i + n + 1)
                wait(dve, inter_ps, i + n - 3)
                wait(dve, kv_ready, i + n - 3)
                dve.scalar_tensor_tensor(out=qk[:, n, :, :].rearrange("p a d -> p (a d)"), in0=ex[:, n % 2, :], scalar=1.0, in1=rl[:, n % 2, :],
                                         op0=ALU.min, op1=ALU.add).then_inc(qk_ready, 1)

            def weigh(T, n):
                wait(dve, cum_ps, T + 1)
                dve.tensor_tensor(prod[:, :].rearrange("p (b e c) -> p b e c", b=3, e=3),
                                  ps_cum.rearrange("p b (e c) -> p b e c", e=3),
                                  qk[:, n, 0, :].unsqueeze(1).unsqueeze(1).to_broadcast([P, 3, 3, D]),
                                  ALU.mult).then_inc(p_done, 1)

            def outputs(T, n):
                wait(dve, inter_ps, T + 1)
                if n == 0:
                    dve.tensor_tensor(kvm[:, :], ps_s[:, SW:2 * SW], headmask[:, :, :].rearrange("p e h -> p (e h)"), ALU.mult).then_inc(kvm_ready, 1)
                elif n < NT - 1:
                    dve.tensor_tensor(kvt[:, :], ps_s[:, SW:2 * SW], headmask[:, :, :].rearrange("p e h -> p (e h)"), ALU.mult).then_inc(kvt_done, 2)
                wait(dve, p_done, T + 1)
                dve.tensor_reduce(red[:, :], prod[:, :].rearrange("p (c d) -> p c d", d=HD), AXX, ALU.add).then_inc(red_done, 1)
                if 0 < n < NT - 1:
                    wait(dve, kvt_done, T + 1 if n == 1 else T + 2)
                    dve.tensor_tensor(kvm[:, :], kvm[:, :], kvt[:, :], ALU.add).then_inc(kvm_ready, n)
                wait(dve, red_done, T + 1)
                dve.tensor_tensor(tot[:, :, :].rearrange("p e h -> p (e h)"), red[:, :], ps_s[:, 0:SW], ALU.add).then_inc(tot_done, 1)
                wait(dve, tot_done, T + 1)
                dve.reciprocal(rden[:, :], tot[:, HD, :]).then_inc(rden_done, 1)
                wait(dve, rden_done, T + 1)
                wait(dve, att_t_ps, T)
                dve.tensor_tensor(att[:, :].rearrange("p (h e) -> p h e", h=H),
                                  tot[:, 0:HD, :].rearrange("p e h -> p h e"),
                                  rden[:, :].unsqueeze(2).to_broadcast([P, H, HD]), ALU.mult).then_inc(att_ready, 1)

            def ffn_residual(i, s, u):
                wait(dve, norm2_done, i - 12)
                for m in range(2):
                    n = 2 * s + m
                    wait(dve, w2_ps, i - 12 + 2 * s + 2)
                    wait(dve, wo_ps, u + 1)
                    dve.tensor_tensor(y2[:, n, :], ps_y[:, m * D:(m + 1) * D],
                                      X[:, ds(tile_of(i, 3, n), 1), :].rearrange("p a d -> p (a d)"), ALU.add).then_inc(y2_done, 1)

            def ffn_stats(i, s):
                for m in range(2):
                    n = 2 * s + m
                    wait(dve, y2_done, i - 12 + n + 1)
                    dve.bn_stats(st2[:, n, :], y2[:, n, :]).then_inc(st2_done, 1)

            def ffn_moments(i, s):
                for m in range(2):
                    n = 2 * s + m
                    wait_apart(dve, st2_done, i - 12 + n + 1, consts_ready)
                    dve.bn_aggr(mv2[:, n, :], st2[:, n, :]).then_inc(mv2_done, 1)

            def att_residual(i, u, back, n, par):
                wait(dve, wo_ps, u + 1)
                wait(dve, norm1_done, u - 1)
                dve.tensor_tensor(y1[:, par, :], ps_y[:, 2 * D:3 * D],
                                  X[:, ds(tile_of(i, back, n), 1), :].rearrange("p a d -> p (a d)"), ALU.add).then_inc(y1_done, 1)

            def att_stats(u, par):
                wait(dve, y1_done, u + 1)
                dve.bn_stats(st1[:, par, :], y1[:, par, :]).then_inc(st1_done, 1)

            def att_moments(u, par):
                wait_apart(dve, st1_done, u + 1, consts_ready)
                dve.bn_aggr(mv1[:, par, :], st1[:, par, :]).then_inc(mv1_done, 1)

            def step(i):
                for s in range(4):
                    back, n = (1, 2 + s) if s < 2 else (0, s - 2)
                    T = i - 2 + s
                    u_back, u_n = (1, 1 + s) if s < 3 else (0, 0)
                    if s < 2 and active(i, 0):
                        feature_map(i, 2 * s)
                    if active(i, back):
                        weigh(T, n)
                    if active(i, back):
                        outputs(T, n)
                    if s < 2 and active(i, 0):
                        feature_map(i, 2 * s + 1)
                    u = T - 1
                    if s < 2 and active(i, 3):
                        ffn_residual(i, s, u if active(i, 1) else TILES * L - 1)
                    if active(i, u_back):
                        att_residual(i, u, u_back, u_n, (s + 1) % 2)
                    if s < 2 and active(i, 3):
                        ffn_stats(i, s)
                    if active(i, u_back):
                        att_stats(u, (s + 1) % 2)
                    if s < 2 and active(i, 3):
                        ffn_moments(i, s)
                    if active(i, u_back):
                        att_moments(u, (s + 1) % 2)
                    if head_row(i, s):
                        dve_head_step(dve, head_row(i, s))
            steps(dve, step, lambda j: dve_head_step(dve, j) if j else None, lambda j: dve_tail_step(dve, j), lambda half: dve_route(dve, half))
            dve_tail(dve)


_INS = ['L0_attn_x', 'L0_attn_Wq', 'L0_attn_bq', 'L0_attn_Wk', 'L0_attn_bk', 'L0_attn_Wv', 'L0_attn_bv', 'L0_attn_Wo', 'L0_attn_bo', 'L0_attn_W1', 'L0_attn_b1', 'L0_attn_W2', 'L0_attn_b2', 'L0_attn_g1', 'L0_attn_be1', 'L0_attn_g2', 'L0_attn_be2', 'L0_attn_gf', 'L0_attn_bef', 'L0_ffn_router_w', 'L0_ffn_router_b', 'L0_ffn_w_gate', 'L0_ffn_w_up', 'L0_ffn_w_down', 'L0_ffn_sw_gate', 'L0_ffn_sw_up', 'L0_ffn_sw_down', 'L0_c', 'L0_wmod']
_OUTS = [((8, 512, 128), 'float32')]


def kernel(**inputs):
    import numpy as _np
    import concourse.bacc as _bacc
    from concourse import mybir as _mybir
    from concourse.bass_utils import run_bass_kernel_spmd as _run

    nc = _bacc.Bacc("TRN2", target_bir_lowering=False, num_devices=1)
    arrays, args = {}, []
    for name in _INS:
        a = _np.ascontiguousarray(inputs[name])
        arrays[f"in_{name}_dram"] = a
        args.append(nc.dram_tensor(f"in_{name}_dram", a.shape, _mybir.dt.from_np(a.dtype), kind="ExternalInput").ap())
    for i, (shape, dtype) in enumerate(_OUTS):
        dt = _mybir.dt.from_np(_np.dtype(dtype))
        args.append(nc.dram_tensor(f"out_{i}_dram", shape, dt, kind="ExternalOutput").ap())
    adaln_block_kernel(nc, *args)
    r = _run(nc, [arrays], core_ids=[0])
    got = tuple(r.results[0][f"out_{i}_dram"] for i in range(len(_OUTS)))
    return got[0]
```
